# Optimizing a Trainium2 kernel written in Bass

```python
import numpy as np
import jax
import jax.numpy as jnp

def _softmax(x, axis=-1):
    return jax.nn.softmax(x, axis=axis)

def _gelu(x):
    return jax.nn.gelu(x, approximate=True)

def _silu(x):
    return jax.nn.silu(x)

def _sigmoid(x):
    return jax.nn.sigmoid(x)

def _layernorm(x, axis=-1, eps=1e-05):
    m = jnp.mean(x, axis=axis, keepdims=True)
    v = jnp.var(x, axis=axis, keepdims=True)
    return (x - m) / jnp.sqrt(v + eps)

def _scatter_add(tgt, idx, src, axis=0):
    return tgt.at[idx].add(src)

def _segment_sum(src, seg, n):
    return jax.ops.segment_sum(src, seg, n)
kernel_name = 'mk_seq_preln_d1_jaxref_r8_f32816'

def setup_inputs(seed: int=0):
    np.random.seed(seed)
    _w = jnp.asarray

    def _L0_attn_setup():
        import jax, jax.numpy as jnp
        import numpy as np
        import math
        D_MODEL = 128
        N_HEADS = 16
        HEAD_DIM = D_MODEL // N_HEADS
        FEAT = 16
        WINDOW = 64
        EPS_NORM = 1e-06
        EPS_LIN = 1e-06
        CHUNK = 128

        def rmsnorm(x, w):
            return x * jax.lax.rsqrt(jnp.mean(x * x, axis=-1, keepdims=True) + EPS_NORM) * w

        def taylor_feature_map(x):
            d = x.shape[-1]
            iu, ju = jnp.triu_indices(d)
            scale = jnp.where(iu == ju, 0.5, 1.0 / math.sqrt(2.0)).astype(x.dtype)
            quad = x[..., iu] * x[..., ju] * scale
            ones = jnp.ones(x.shape[:-1] + (1,), dtype=x.dtype)
            return jnp.concatenate([ones, x, quad], axis=-1)

        def linear_attention_causal(q_phi, k_phi, v):
            B, T, H, F = q_phi.shape
            D = v.shape[-1]
            Nc = T // CHUNK
            qc = q_phi.reshape(B, Nc, CHUNK, H, F).transpose(1, 0, 2, 3, 4)
            kc = k_phi.reshape(B, Nc, CHUNK, H, F).transpose(1, 0, 2, 3, 4)
            vc = v.reshape(B, Nc, CHUNK, H, D).transpose(1, 0, 2, 3, 4)
            causal = jnp.tril(jnp.ones((CHUNK, CHUNK), dtype=q_phi.dtype))

            def step(carry, inp):
                kv, ksum = carry
                qb, kb, vb = inp
                A = jnp.einsum('bchf,bshf->bhcs', qb, kb) * causal
                y = jnp.einsum('bhcs,bshd->bchd', A, vb) + jnp.einsum('bchf,bhfd->bchd', qb, kv)
                z = jnp.einsum('bhcs->bch', A) + jnp.einsum('bchf,bhf->bch', qb, ksum)
                kv = kv + jnp.einsum('bshf,bshd->bhfd', kb, vb)
                ksum = ksum + kb.sum(axis=1)
                return ((kv, ksum), y / (z[..., None] + EPS_LIN))
            kv0 = jnp.zeros((B, H, F, D), dtype=q_phi.dtype)
            ks0 = jnp.zeros((B, H, F), dtype=q_phi.dtype)
            _, ys = jax.lax.scan(step, (kv0, ks0), (qc, kc, vc))
            return ys.transpose(1, 0, 2, 3, 4).reshape(B, T, H, D)

        def sliding_window_attention(q, k, v):
            B, T, H, D = q.shape
            scale = 1.0 / math.sqrt(D)
            t = jnp.arange(T)
            allowed = (t[None, :] <= t[:, None]) & (t[None, :] >= t[:, None] - WINDOW)
            scores = jnp.einsum('bqhd,bkhd->bhqk', q, k) * scale
            scores = jnp.where(allowed[None, None], scores, -jnp.inf)
            attn = jax.nn.softmax(scores, axis=-1)
            out = jnp.einsum('bhqk,bkhd->bqhd', attn, v)
            return out.reshape(B, T, H * D)
        key = jax.random.key(seed)
        ks = jax.random.split(key, 7)
        B, T = (2, 256)
        s = 0.02
        return {'x': jax.random.normal(ks[0], (B, T, D_MODEL), jnp.float32), 'norm_w': jnp.ones((D_MODEL,), jnp.float32), 'Wq': jax.random.normal(ks[1], (D_MODEL, D_MODEL), jnp.float32) * s, 'Wk': jax.random.normal(ks[2], (D_MODEL, D_MODEL), jnp.float32) * s, 'Wv': jax.random.normal(ks[3], (D_MODEL, D_MODEL), jnp.float32) * s, 'Wqf': jax.random.normal(ks[4], (HEAD_DIM, FEAT), jnp.float32) * s, 'Wkf': jax.random.normal(ks[5], (HEAD_DIM, FEAT), jnp.float32) * s, 'Wout': jax.random.normal(ks[6], (2 * D_MODEL, D_MODEL), jnp.float32) * s}
    _L0_attn_in = _L0_attn_setup()

    def _L0_ffn_setup():
        import jax, jax.numpy as jnp
        import numpy as np
        E, H, F, K = (8, 128, 256, 2)
        B, S = (2, 256)
        key = jax.random.key(seed)
        ks = jax.random.split(key, 8)

        def w(k, shape, fan_in):
            return jax.random.normal(k, shape, jnp.float32) / np.float32(np.sqrt(fan_in))
        return {'x': jax.random.normal(ks[0], (B, S, H), jnp.float32), 'Wgate': w(ks[1], (H, E), H), 'bgate': jnp.zeros((E,), jnp.float32), 'W1': w(ks[2], (E, H, F), H), 'b1': jnp.zeros((E, F), jnp.float32), 'W2': w(ks[3], (E, H, F), H), 'b2': jnp.zeros((E, F), jnp.float32), 'Wg': w(ks[4], (E, F, F), F), 'bg': jnp.zeros((E, F), jnp.float32), 'Wl': w(ks[5], (E, F, F), F), 'bl': jnp.zeros((E, F), jnp.float32), 'W3': w(ks[6], (E, F, H), F), 'b3': jnp.zeros((E, H), jnp.float32)}
    _L0_ffn_in = _L0_ffn_setup()
    _d = {'L0_attn_x': _L0_attn_in['x'], 'L0_attn_norm_w': _L0_attn_in['norm_w'], 'L0_attn_Wq': _L0_attn_in['Wq'], 'L0_attn_Wk': _L0_attn_in['Wk'], 'L0_attn_Wv': _L0_attn_in['Wv'], 'L0_attn_Wqf': _L0_attn_in['Wqf'], 'L0_attn_Wkf': _L0_attn_in['Wkf'], 'L0_attn_Wout': _L0_attn_in['Wout'], 'L0_ffn_Wgate': _L0_ffn_in['Wgate'], 'L0_ffn_bgate': _L0_ffn_in['bgate'], 'L0_ffn_W1': _L0_ffn_in['W1'], 'L0_ffn_b1': _L0_ffn_in['b1'], 'L0_ffn_W2': _L0_ffn_in['W2'], 'L0_ffn_b2': _L0_ffn_in['b2'], 'L0_ffn_Wg': _L0_ffn_in['Wg'], 'L0_ffn_bg': _L0_ffn_in['bg'], 'L0_ffn_Wl': _L0_ffn_in['Wl'], 'L0_ffn_bl': _L0_ffn_in['bl'], 'L0_ffn_W3': _L0_ffn_in['W3'], 'L0_ffn_b3': _L0_ffn_in['b3']}
    _x0 = _d['L0_attn_x']
    _d['L0_attn_x'] = jax.random.normal(jax.random.fold_in(jax.random.key(seed), 1), (2, 1024, 128), dtype=_x0.dtype)
    del _x0
    return _d

def reference(L0_attn_x, L0_attn_norm_w, L0_attn_Wq, L0_attn_Wk, L0_attn_Wv, L0_attn_Wqf, L0_attn_Wkf, L0_attn_Wout, L0_ffn_Wgate, L0_ffn_bgate, L0_ffn_W1, L0_ffn_b1, L0_ffn_W2, L0_ffn_b2, L0_ffn_Wg, L0_ffn_bg, L0_ffn_Wl, L0_ffn_bl, L0_ffn_W3, L0_ffn_b3):

    def _L0_attn_ref(x, norm_w, Wq, Wk, Wv, Wqf, Wkf, Wout):
        import jax, jax.numpy as jnp
        import numpy as np
        import math
        D_MODEL = 128
        N_HEADS = 16
        HEAD_DIM = D_MODEL // N_HEADS
        FEAT = 16
        WINDOW = 64
        EPS_NORM = 1e-06
        EPS_LIN = 1e-06
        CHUNK = 128

        def rmsnorm(x, w):
            return x * jax.lax.rsqrt(jnp.mean(x * x, axis=-1, keepdims=True) + EPS_NORM) * w

        def taylor_feature_map(x):
            d = x.shape[-1]
            iu, ju = jnp.triu_indices(d)
            scale = jnp.where(iu == ju, 0.5, 1.0 / math.sqrt(2.0)).astype(x.dtype)
            quad = x[..., iu] * x[..., ju] * scale
            ones = jnp.ones(x.shape[:-1] + (1,), dtype=x.dtype)
            return jnp.concatenate([ones, x, quad], axis=-1)

        def linear_attention_causal(q_phi, k_phi, v):
            B, T, H, F = q_phi.shape
            D = v.shape[-1]
            Nc = T // CHUNK
            qc = q_phi.reshape(B, Nc, CHUNK, H, F).transpose(1, 0, 2, 3, 4)
            kc = k_phi.reshape(B, Nc, CHUNK, H, F).transpose(1, 0, 2, 3, 4)
            vc = v.reshape(B, Nc, CHUNK, H, D).transpose(1, 0, 2, 3, 4)
            causal = jnp.tril(jnp.ones((CHUNK, CHUNK), dtype=q_phi.dtype))

            def step(carry, inp):
                kv, ksum = carry
                qb, kb, vb = inp
                A = jnp.einsum('bchf,bshf->bhcs', qb, kb) * causal
                y = jnp.einsum('bhcs,bshd->bchd', A, vb) + jnp.einsum('bchf,bhfd->bchd', qb, kv)
                z = jnp.einsum('bhcs->bch', A) + jnp.einsum('bchf,bhf->bch', qb, ksum)
                kv = kv + jnp.einsum('bshf,bshd->bhfd', kb, vb)
                ksum = ksum + kb.sum(axis=1)
                return ((kv, ksum), y / (z[..., None] + EPS_LIN))
            kv0 = jnp.zeros((B, H, F, D), dtype=q_phi.dtype)
            ks0 = jnp.zeros((B, H, F), dtype=q_phi.dtype)
            _, ys = jax.lax.scan(step, (kv0, ks0), (qc, kc, vc))
            return ys.transpose(1, 0, 2, 3, 4).reshape(B, T, H, D)

        def sliding_window_attention(q, k, v):
            B, T, H, D = q.shape
            scale = 1.0 / math.sqrt(D)
            t = jnp.arange(T)
            allowed = (t[None, :] <= t[:, None]) & (t[None, :] >= t[:, None] - WINDOW)
            scores = jnp.einsum('bqhd,bkhd->bhqk', q, k) * scale
            scores = jnp.where(allowed[None, None], scores, -jnp.inf)
            attn = jax.nn.softmax(scores, axis=-1)
            out = jnp.einsum('bhqk,bkhd->bqhd', attn, v)
            return out.reshape(B, T, H * D)
        B, T, _ = x.shape
        h = rmsnorm(x, norm_w)
        q = (h @ Wq).reshape(B, T, N_HEADS, HEAD_DIM)
        k = (h @ Wk).reshape(B, T, N_HEADS, HEAD_DIM)
        v = (h @ Wv).reshape(B, T, N_HEADS, HEAD_DIM)
        q_phi = taylor_feature_map(q @ Wqf)
        k_phi = taylor_feature_map(k @ Wkf)
        lin = linear_attention_causal(q_phi, k_phi, v).reshape(B, T, D_MODEL)
        win = sliding_window_attention(q, k, v)
        out = jnp.concatenate([lin, win], axis=-1) @ Wout
        return x + out

    def _L0_ffn_ref(x, Wgate, bgate, W1, b1, W2, b2, Wg, bg, Wl, bl, W3, b3):
        import jax, jax.numpy as jnp
        import numpy as np
        E, H, F, K = (8, 128, 256, 2)
        B, S = (2, 256)
        gout = x @ Wgate + bgate
        topv, topi = jax.lax.top_k(gout, K)
        topw = jax.nn.softmax(topv, axis=-1)
        combine = jnp.sum(jax.nn.one_hot(topi, E, dtype=x.dtype) * topw[..., None], axis=-2)
        x1 = jnp.einsum('bsh,ehf->bsef', x, W1) + b1
        x2 = jnp.einsum('bsh,ehf->bsef', x, W2) + b2
        z = x1 * x2
        g = jnp.einsum('bsef,efg->bseg', z, Wg) + bg
        o = g * jax.nn.sigmoid(g) * (jnp.einsum('bsef,efg->bseg', z, Wl) + bl)
        y = jnp.einsum('bsef,efh->bseh', o, W3) + b3
        return jnp.einsum('bse,bseh->bsh', combine, y)
    x = L0_attn_x
    x = x + _L0_attn_ref(_layernorm(x, axis=-1), L0_attn_norm_w, L0_attn_Wq, L0_attn_Wk, L0_attn_Wv, L0_attn_Wqf, L0_attn_Wkf, L0_attn_Wout)
    x = x + _L0_ffn_ref(_layernorm(x, axis=-1), L0_ffn_Wgate, L0_ffn_bgate, L0_ffn_W1, L0_ffn_b1, L0_ffn_W2, L0_ffn_b2, L0_ffn_Wg, L0_ffn_bg, L0_ffn_Wl, L0_ffn_bl, L0_ffn_W3, L0_ffn_b3)
    return x

_drawn_inputs = setup_inputs


def setup_inputs(seed=0):
    import zlib

    import numpy as np

    out = dict(_drawn_inputs(seed))
    spreads = {'L0_attn_norm_w': (1.0, 0.6),
     'L0_ffn_bgate': (0.0, 0.1),
     'L0_ffn_b1': (0.0, 0.39),
     'L0_ffn_b2': (0.0, 0.392),
     'L0_ffn_bg': (0.0, 0.354),
     'L0_ffn_bl': (0.0, 0.366),
     'L0_ffn_b3': (0.0, 0.358)}
    factors = {'L0_attn_Wq': 8.0,
     'L0_attn_Wk': 8.0,
     'L0_attn_Wv': 7.105,
     'L0_attn_Wqf': 8.0,
     'L0_attn_Wkf': 8.0,
     'L0_attn_Wout': 6.801}
    for name, (base, spread) in spreads.items():
        noise = np.random.default_rng([zlib.crc32(name.encode()), seed]).standard_normal(out[name].shape)
        drawn = base * np.exp(spread * noise) if base else spread * noise
        out[name] = jnp.asarray(drawn.astype(out[name].dtype))
    for name, factor in factors.items():
        out[name] = (out[name] * factor).astype(out[name].dtype)
    return out
```

```python
from contextlib import ExitStack

import numpy as np
import concourse.bass as bass
from concourse import mybir

ALU = mybir.AluOpType
ACT = mybir.ActivationFunctionType
AX = mybir.AxisListType
F32 = mybir.dt.float32
BF16 = mybir.dt.bfloat16

B, T, D = 2, 1024, 128
H, HD = 16, 8
WINDOW = 64
CH = 128
NC = B * T // CH
GC = 4
NG = NC // GC
GT = GC * CH
UNITS = 4
UD = HD + 1
NF = UD * (UD + 1) // 2
FS = 48
PR = 2 * FS
NP = H // 2
SLOTS = [(0, 0), (0, 1), (1, 0), (1, 1), (0, 2), (2, 0)]
KP = HD * len(SLOTS)
ROW_VALID, ROW_ONE = KP + WINDOW, KP + WINDOW + 1
KR = KP + WINDOW + 2
BIG = -1.0e30
E, F = 8, 256
TOPK = 2
N = B * T
REGION = N + CH
ROW = D + 2 * E
NT = TOPK * N // CH + E
RESULTS = TOPK * N
EPS_LN, EPS_RMS, EPS_LIN = 1e-5, 1e-6, 1e-6


def constants():
    c = {}
    c["ident"] = np.eye(128, dtype=np.float32)
    feats = [(i, i + dl) for dl in range(UD) for i in range(UD - dl)]
    expand = np.zeros((D, NP, PR), np.float32)
    fbias = np.zeros((PR, 1), np.float32)
    for h in range(H):
        for r, (i, j) in enumerate(feats):
            for z in {i, j}:
                if z:
                    expand[h * HD + z - 1, h // 2, (h % 2) * FS + r] = 1.0
            if i == 0:
                fbias[(h % 2) * FS + r] = 1.0
    c["expand"] = expand.reshape(D, NP * PR)
    c["fbias"] = fbias
    blk = np.arange(D) // HD
    c["blockdiag"] = (blk[:, None] == blk[None, :]).astype(np.float32)
    sm = np.zeros((PR, 2, 2, UD), np.float32)
    for par in range(2):
        sm[par * FS:(par + 1) * FS, :, par] = 1.0
    c["statemask"] = sm.reshape(PR, 4 * UD)
    keep = np.ones((128, NC + 1), np.float32)
    keep[:, ::T // CH] = 0.0
    c["keep"] = keep
    q, kap = np.arange(WINDOW), np.arange(CH)
    qrows = np.zeros((KR - KP, H, CH), np.float32)
    qrows[:WINDOW] = (q[:, None] == kap[None, :] % WINDOW)[:, None]
    qrows[WINDOW] = 1.0
    arows = np.zeros((KR - KP, H, CH), np.float32)
    arows[WINDOW + 1] = 1.0
    krows = np.zeros((KR - KP, H, CH), np.float32)
    krows[:WINDOW] = np.where((kap >= q[:, None]) & (kap <= q[:, None] + WINDOW), 0.0, BIG)[:, None]
    krows[WINDOW + 1] = 1.0
    valid = np.zeros((NC, H, CH), np.float32)
    valid[::T // CH, :, :WINDOW] = BIG
    c["iota8"] = np.tile(np.arange(E, dtype=np.float32), (128, 1))
    c["region0"] = np.tile(np.arange(E, dtype=np.float32) * REGION, (128, 1))
    c["tokid"] = (np.arange(CH)[:, None] + CH * np.arange(NC)[None]).astype(np.float32)
    pad = np.zeros((CH, ROW), np.float32)
    pad[:, D + E:] = TOPK * N + np.arange(CH)[:, None]
    c["padrows"] = pad
    c["tiles"] = np.arange(NT, dtype=np.float32)[None]
    bf = mybir.dt.np(BF16)
    c["before"] = np.triu(np.ones((128, 128), np.float32), 1).astype(bf)
    c["ones"] = np.ones((128, 128), np.float32).astype(bf)
    c["qrows"], c["arows"], c["krows"] = (x.reshape(KR - KP, H * CH).astype(bf) for x in (qrows, arows, krows))
    c["valid"] = valid.reshape(NC, H * CH).astype(bf)
    c["identb"] = np.eye(128, dtype=np.float32).astype(bf)
    return c


def build(nc, ins, con, out, dbg=None):
    with ExitStack() as ctx:
        sb = lambda n, s, d=F32: ctx.enter_context(nc.sbuf_tensor(n, s, d))
        sem = lambda n: ctx.enter_context(nc.semaphore(n))
        dram = lambda n, s, d=F32: nc.dram_tensor(n, s, d).ap()

        q_parts = dram("q_parts", (3, HD, NC, H, CH), BF16)
        a_parts = dram("a_parts", (3, HD, NC, H, CH), BF16)
        k_parts = dram("k_parts", (2, 3, HD, NC, H, CH), BF16)

        routed = dram("routed", (E * REGION + CH, ROW))
        results = dram("results", (RESULTS, D))
        ident = sb("ident", [128, 128])
        identb = sb("identb", [128, 128], BF16)
        expand = sb("expand", [D, NP * PR])
        fbias = sb("fbias", [PR, 1])
        blockdiag = sb("blockdiag", [D, D])
        statemask = sb("statemask", [PR, 4 * UD])
        keep = sb("keep", [128, NC + 1])
        norm_w = sb("norm_w", [D, 1])
        wq = sb("wq", [D, D])
        wqT = sb("wqT", [D, D])
        wkv = sb("wkv", [D, 2, D])
        wout = sb("wout", [D, 2, D])
        wfeat = sb("wfeat", [16, 2, D])
        mblk = sb("mblk", [D, D])
        wa = sb("wa", [D, D])
        waT = sb("waT", [D, D])
        wphi = sb("wphi", [D, NP, PR])
        minus_half = sb("minus_half", [128, 2 * GC])
        x_all = sb("x_all", [CH, NC, D])
        stats = sb("stats", [CH, GC, 6])
        mvg = sb("mvg", [CH, GC, 2])
        mv = sb("mv", [CH, NC, 2])
        vareps = sb("vareps", [CH, GC, 2])
        rstd = sb("rstd", [CH, NC])
        rboth = sb("rboth", [CH, GC])
        h_tok = sb("h_tok", [CH, GC, D])
        hT = sb("hT", [D, WINDOW + GT])
        hT_all = sb("hT_all", [D, NC, CH])
        k_tok = sb("k_tok", [CH, NC + 1, D])
        v_all = sb("v_all", [CH, NC + 1, 2, D])
        qa_parts = sb("qa_parts", [D, 2, 3, GT], BF16)
        kp = sb("kp", [D, 3, WINDOW + GT], BF16)
        rest = sb("rest", [D, 3, GT])
        qs_ = sb("qs", [128, 2, H, CH], BF16)
        as_w = sb("as_", [128, 2, H, CH], BF16)
        ks_ = sb("ks", [128, 2, 2, H, CH], BF16)
        qs, as_, ks = qs_[0:KR], as_w[0:KR], ks_[0:KR]
        u_tok = sb("u_tok", [CH, H, UD])
        usum = sb("usum", [CH, H])
        ut = sb("ut", [CH, H, UD])
        phik = sb("phik", [CH, 2, H, FS])
        v1 = sb("v1", [CH, 2, 2, H, 32])
        state = sb("state", [PR, H, 32])
        sadd = sb("sadd", [PR, 4, UD])
        mrow = sb("mrow", [128, 4])
        mneg = sb("mneg", [128, 2, 4], BF16)
        phiq = sb("phiq", [PR, 2, 2, CH])
        amat = sb("amat", [CH, 2, 4, CH])
        pmat = sb("pmat", [CH, 2, 8, WINDOW])
        linT = sb("linT", [128, 2, 4, CH])
        winT = sb("winT", [128, 2, 4, CH])
        zrec = sb("zrec", [CH, H])
        att = sb("att", [CH, 2, H, HD])
        catT = sb("catT", [D, 3, CH])
        xh = sb("xh", [CH, D])
        st2 = sb("st2", [CH, 6])
        mv2 = sb("mv2", [CH, 2])
        ve2 = sb("ve2", [CH, 1])
        rstd2 = sb("rstd2", [CH, 1])
        h2 = sb("h2", [CH, 2, D])
        wgate = sb("wgate", [D, E])
        bgate = sb("bgate", [128, E])
        iota8 = sb("iota8", [128, E])
        tokid = sb("tokid", [CH, NC])
        before = sb("before", [128, 128], BF16)
        ones = sb("ones", [128, 128], BF16)
        count = sb("count", [128, E])
        region0 = sb("region0", [128, E])
        logit = sb("logit", [CH, E])
        top = sb("top", [CH, 8])
        topi = sb("topi", [CH, 8], mybir.dt.uint32)
        topf = sb("topf", [CH, 2])
        onehot = sb("onehot", [CH, 2, E])
        member = sb("member", [CH, E], BF16)
        gap = sb("gap", [CH, 1])
        egap = sb("egap", [CH, 1])
        wsum = sb("wsum", [CH, 1])
        w01 = sb("w01", [CH, 2])
        tmp8 = sb("tmp8", [CH, 2, E])
        place = sb("place", [CH, E])
        placed = sb("placed", [CH, 2, E])
        slotf = sb("slotf", [CH, 2])
        slot = sb("slot", [CH, 2, 2], mybir.dt.uint32)
        routed_row = sb("routed_row", [CH, 2, ROW])
        padrows = sb("padrows", [CH, ROW])
        tiles = sb("tiles", [1, NT])
        table = sb("table", [1, 2, NT], mybir.dt.int32)
        counts_i = sb("counts_i", [1, E], mybir.dt.int32)
        ntile_i = sb("ntile_i", [1, E], mybir.dt.int32)
        ntile = sb("ntile", [1, E])
        ends = sb("ends", [1, E])
        tmpt = sb("tmpt", [1, 4, NT])
        cmp8 = sb("cmp8", [1, 2, NT, E])
        tail_i = sb("tail_i", [1, E], mybir.dt.int32)
        w12 = sb("w12", [D, E, 2 * F])
        wgl = sb("wgl", [128, E, 2, 2 * F])
        w3 = as_w[:].rearrange("p a h t -> p (a h t)").bitcast(F32).rearrange("p (e k d) -> p e k d", e=E, k=2)
        b12 = v_all[:].rearrange("p c w d -> p (c w d)")[:, 0:E * 2 * F].rearrange("p (e f) -> p e f", e=E)
        bgl = ks_[:].rearrange("p a w h t -> p (a w h t)").bitcast(F32).rearrange("p (e f) -> p e f", e=E)
        b3 = qs_[:, 0].rearrange("p h t -> p (h t)").bitcast(F32).rearrange("p (e f) -> p e f", e=E)
        late1 = hT_all[:].rearrange("p c t -> p (c t)")
        x12, glb = (late1[:, o:o + 1024].rearrange("p (a f) -> p a f", a=2) for o in (0, 1024))
        late2 = k_tok[:].rearrange("p c t -> p (c t)")
        z = late2[:, 0:512].rearrange("p (a f) -> p a f", a=2)
        og = late2[:, 512:1024].rearrange("p (a f) -> p a f", a=2)
        oT = late2[:, 1024:1536].rearrange("p (a k t) -> p a k t", a=2, k=2)
        sg = late2[:, 1536:2048].rearrange("p (a f) -> p a f", a=2)
        late3 = rest[:].rearrange("p c t -> p (c t)")
        zxT = late3[:, 0:768].rearrange("p (a k t) -> p a k t", a=2, k=3)
        late4 = wphi[:].rearrange("p a f -> p (a f)")
        yb = late3[:, 768:1024].rearrange("p (a d) -> p a d", a=2)
        yw = late4[:, 0:512].rearrange("p (a d) -> p a d", a=4)
        xin = sb("xin", [CH, 4, ROW])
        mweight = sb("mweight", [CH, 4])
        mrowf = sb("mrowf", [CH, 4])
        mrowid = sb("mrowid", [CH, 4], mybir.dt.uint32)
        res = [v_all[:].rearrange("p c w d -> p (c w d)")[:, 2048 * k:2048 * (k + 1)].rearrange("p (c d) -> p c d", c=NC) for k in range(2)]

        ps = ctx.enter_context(nc.psum_tensor("ps", [128, 8, 512], F32))
        SQ, ST, A, OUT0, OUT1, PHI, KV, TR = range(8)

        w_in, c_in, x_in, s_in = sem("w_in"), sem("c_in"), sem("x_in"), sem("s_in")
        zeroed = sem("zeroed")
        wstep, wstep_c = sem("wstep"), sem("wstep_c")
        mv_ready, ve_ready, pow_ready, rb_ready, h_ready = (sem(n) for n in ("mv_ready", "ve_ready", "pow_ready", "rb_ready", "h_ready"))
        hps_ready, hT_ready, hTall_done = sem("hps_ready"), sem("hT_ready"), sem("hTall_done")
        proj_ready, part0, rest1, part1, part2 = (sem(n) for n in ("proj_ready", "part0", "rest1", "part1", "part2"))
        kv_proj, kv_copied, halo, parts_out = sem("kv_proj"), sem("kv_copied"), sem("halo"), sem("parts_out")
        stack_in = [sem("stack_in0"), sem("stack_in1")]
        sq_ready, max_done, nh_done, mneg_ready = sem("sq_ready"), sem("max_done"), sem("nh_done"), sem("mneg_ready")
        a_ready, square_done, amask_ready = sem("a_ready"), sem("square_done"), sem("amask_ready")
        phi_ready, phisq_done, inter_done = sem("phi_ready"), sem("phisq_done"), sem("inter_done")
        us, ut_done, phik_ready, kv_ready, sadd_done, state_done = (sem(n) for n in ("us", "ut_done", "phik_ready", "kv_ready", "sadd_done", "state_done"))
        st_ready, exp_done, out_ready, evac_done = sem("st_ready"), sem("exp_done"), sem("out_ready"), sem("evac_done")
        t_lin, t_win, t_cat, cat_copied, wout_ready = (sem(n) for n in ("t_lin", "t_win", "t_cat", "cat_copied", "wout_ready"))
        z1, z2, norm_lin, norm_win = sem("z1"), sem("z2"), sem("norm_lin"), sem("norm_win")
        xh0, xh_ready, x1_ready, st2_done, mv2_ready, ve2_ready, rstd2_ready, h2_ready = (
            sem(n) for n in ("xh0", "xh_ready", "x1_ready", "st2_done", "mv2_ready", "ve2_ready", "rstd2_ready", "h2_ready"))
        done = sem("done")
        settled = sem("settled")
        xin_ready = [sem(f"xin_ready{k}") for k in range(4)]
        y_out = [sem(f"y_out{k}") for k in range(4)]
        (r_logit, r_top, r_idx, r_idxf, r_oh, r_member, r_gap, r_egap, r_ws, r_w, r_w2, r_tmp, r_row, r_place, r_placed, r_slotf, r_slot,
         r_count, pos_ready, staged, scattered) = tuple(sem(n) for n in (
             "r_logit", "r_top", "r_idx", "r_idxf", "r_oh", "r_member", "r_gap", "r_egap", "r_ws", "r_w", "r_w2", "r_tmp", "r_row", "r_place",
             "r_placed", "r_slotf", "r_slot", "r_count", "pos_ready", "staged")) + ([sem("scattered0"), sem("scattered1")],)
        tab, table_ready, padded = sem("tab"), sem("table_ready"), sem("padded")
        e_in, b_in = sem("e_in"), sem("b_in")
        (tzx_ready, zx_copied, x12_ready, x12_added, z_ready, meta_copied, meta_ready, gl_ready, g_added, l_added, silu_done, o_ready, to_ready,
         oT_copied, y_ready, y_added, y_weighted) = (sem(n) for n in (
             "tzx_ready", "zx_copied", "x12_ready", "x12_added", "z_ready", "meta_copied", "meta_ready", "gl_ready", "g_added", "l_added",
             "silu_done", "o_ready", "to_ready", "oT_copied", "y_ready", "y_added", "y_weighted"))
        res_in, res_sum, out_sum = sem("res_in"), sem("res_sum"), sem("out_sum")

        TZX, X12, Y, TO, GL = SQ, ST, A, PHI, OUT0

        def settle(engine):
            engine.wait_ge(settled, 1)

        def computed(engine, value):
            if not isinstance(value, int):
                value = engine.snap(engine.to_reg(value))
            settle(engine)
            return value

        def run_steps(engine, step):
            def turns(i, k):
                return lambda d: i + (k + d) // 4

            for j in range(-2, 4):
                step(j, j % 4, turns(j // 4, j % 4))
            with engine.Fori(1, NT // 4 - 1) as i:
                for k in range(4):
                    step(i * 4 + k, k, turns(i, k))
            for j in range(NT - 4, NT + 2):
                step(j, j % 4, turns(j // 4, j % 4))

        x_dram = ins["x"].rearrange("b (c p) d -> p (b c) d", p=CH)
        N_C = 16
        N_W = 10
        N_S = 6

        block = ctx.enter_context(nc.Block())

        @block.sync
        def _(sp):
            sp.dma_start(x_all[:], x_dram).then_inc(x_in, 16)
            for dst, name in ((ident, "ident"), (identb, "identb"), (expand, "expand"), (fbias, "fbias"), (blockdiag, "blockdiag"),
                              (statemask, "statemask"), (keep, "keep"), (iota8, "iota8"), (region0, "region0"), (tokid, "tokid"),
                              (before, "before"), (ones, "ones"), (padrows, "padrows"), (tiles, "tiles"), (count, "region0")):
                sp.dma_start(dst[:], con[name]).then_inc(c_in, 16)
            sp.dma_start(norm_w[:], ins["norm_w"].rearrange("(d a) -> d a", a=1)).then_inc(c_in, 16)
            sp.dma_start(wq[:], ins["Wq"]).then_inc(w_in, 16)
            sp.dma_start(wkv[:, 0, :], ins["Wk"]).then_inc(w_in, 16)
            sp.dma_start(wkv[:, 1, :], ins["Wv"]).then_inc(w_in, 16)
            sp.dma_start(wout[:, 0, :], ins["Wout"][0:D, :]).then_inc(w_in, 16)
            sp.dma_start(wout[:, 1, :], ins["Wout"][D:2 * D, :]).then_inc(w_in, 16)
            sp.dma_start(wqT[:], ins["WqT"]).then_inc(w_in, 16)
            sp.dma_start(wfeat[:, 0, :], ins["WqfT"]).then_inc(w_in, 16)
            sp.dma_start(wfeat[:, 1, :], ins["WkfT"]).then_inc(w_in, 16)
            sp.dma_start(wgate[:], ins["Wgate"]).then_inc(w_in, 16)
            sp.dma_start(bgate[:], ins["bgate"].rearrange("(a e) -> a e", a=1).to_broadcast([128, E])).then_inc(w_in, 16)
            for p in range(2):
                sp.dma_start(qs[KP:KR, p], con["qrows"]).then_inc(s_in, 16)
                sp.dma_start(as_[KP:KR, p], con["arows"]).then_inc(s_in, 16)
                for w in range(2):
                    sp.dma_start(ks[KP:KR, p, w], con["krows"]).then_inc(s_in, 16)
            def group(g):
                sp.wait_ge(part2, 3 * (g + 1))
                for t, dst in ((0, q_parts), (1, a_parts)):
                    for p in range(3):
                        for cc in range(GC):
                            sp.dma_start(dst[p, :, bass.ds(g * GC + cc, 1)].rearrange("d c h t -> h d (c t)"),
                                         qa_parts[:, t, p, cc * CH:(cc + 1) * CH]).then_inc(parts_out, 16)
                for w in range(2):
                    for p in range(3):
                        for cc in range(GC):
                            o = WINDOW * w + cc * CH
                            sp.dma_start(k_parts[w, p, :, bass.ds(g * GC + cc, 1)].rearrange("d c h t -> h d (c t)"),
                                         kp[:, p, o:o + CH]).then_inc(parts_out, 16)
            group(0)
            with sp.Fori(1, NG) as g:
                group(g)

            sp.wait_ge(parts_out, NG * 16 * 12 * GC)
            sp.wait_ge(s_in, 16 * 8)

            def load_stack(c, p, i):
                if i is not None:
                    sp.wait_ge(out_ready, UNITS * (2 * i + p - 1))
                for s, (qp, kpp) in enumerate(SLOTS):
                    rows = slice(HD * s, HD * (s + 1))
                    sp.dma_start(qs[rows, p], q_parts[qp, :, bass.ds(c, 1)].rearrange("d c h t -> d (c h t)")).then_inc(stack_in[p], 16)
                    sp.dma_start(as_[rows, p], a_parts[qp, :, bass.ds(c, 1)].rearrange("d c h t -> d (c h t)")).then_inc(stack_in[p], 16)
                    for w in range(2):
                        sp.dma_start(ks[rows, p, w], k_parts[w, kpp, :, bass.ds(c, 1)].rearrange("d c h t -> d (c h t)")).then_inc(stack_in[p], 16)
                sp.dma_start(ks[ROW_VALID:ROW_VALID + 1, p, 0], con["valid"][bass.ds(c, 1)]).then_inc(stack_in[p], 16)

            load_stack(0, 0, None)
            load_stack(1, 1, None)
            with sp.Fori(1, NC // 2) as i:
                for p in range(2):
                    load_stack(i * 2 + p, p, i)
            sp.dma_start(w12[:, :, 0:F], ins["W1"].rearrange("e d f -> d e f")).then_inc(e_in, 16)
            sp.dma_start(w12[:, :, F:], ins["W2"].rearrange("e d f -> d e f")).then_inc(e_in, 16)
            for k in range(2):
                sp.dma_start(wgl[:, :, k, 0:F], ins["Wg"][:, k * 128:(k + 1) * 128, :].rearrange("e d f -> d e f")).then_inc(e_in, 16)
                sp.dma_start(wgl[:, :, k, F:], ins["Wl"][:, k * 128:(k + 1) * 128, :].rearrange("e d f -> d e f")).then_inc(e_in, 16)
            sp.wait_ge(phik_ready, NC + 1)
            sp.dma_start(b12[:, :, 0:F], ins["b1"].rearrange("(a e) f -> a e f", a=1).to_broadcast([128, E, F])).then_inc(b_in, 16)
            sp.dma_start(b12[:, :, F:], ins["b2"].rearrange("(a e) f -> a e f", a=1).to_broadcast([128, E, F])).then_inc(b_in, 16)
            sp.wait_ge(out_ready, UNITS * NC)
            sp.dma_start(bgl[:, :, 0:F], ins["bg"].rearrange("(a e) f -> a e f", a=1).to_broadcast([128, E, F])).then_inc(b_in, 16)
            sp.dma_start(bgl[:, :, F:], ins["bl"].rearrange("(a e) f -> a e f", a=1).to_broadcast([128, E, F])).then_inc(b_in, 16)
            for k in range(2):
                sp.dma_start(w3[:, :, k, :], ins["W3"][:, k * 128:(k + 1) * 128, :].rearrange("e d f -> d e f")).then_inc(b_in, 16)
            sp.dma_start(b3[:], ins["b3"].rearrange("(a e) f -> a e f", a=1).to_broadcast([128, E, D])).then_inc(b_in, 16)
            sp.dma_start(routed[E * REGION:E * REGION + CH, :], padrows[:]).then_inc(padded, 16)
            sp.wait_ge(table_ready, 1)
            for e in range(E):
                row = sp.value_load(tail_i[0:1, e:e + 1], min_val=0, max_val=E * REGION - CH)
                sp.dma_start(routed[bass.ds(row, CH), :], padrows[:]).then_inc(padded, 16)
            sp.wait_ge(padded, 16 * (E + 1))
            for p in range(2):
                sp.wait_ge(scattered[p], 16 * NC)

            def load_tile(j, k):
                if not isinstance(j, int) or j >= 4:
                    sp.wait_ge(tzx_ready, computed(sp, j - 1))
                    sp.wait_ge(meta_copied, computed(sp, j - 3))
                row = sp.value_load(table[0:1, 1, bass.ds(j, 1)], min_val=0, max_val=E * REGION)
                sp.dma_start(xin[:, k, :], routed[bass.ds(row, CH), :]).then_inc(xin_ready[k], 16)

            for j in range(4):
                load_tile(j, j)
            with sp.Fori(1, NT // 4) as i:
                for k in range(4):
                    load_tile(i * 4 + k, k)
            for k in range(4):
                sp.wait_ge(y_out[k], 16 * (NT // 4))
            for k in range(2):
                sp.dma_start(res[k], results[k * N:(k + 1) * N, :].rearrange("(c p) d -> p c d", p=CH)).then_inc(res_in, 16)
            sp.wait_ge(out_sum, 1)
            sp.dma_start(out.rearrange("b (c p) d -> p (b c) d", p=CH), x_all[:]).then_inc(done, 16)
            sp.wait_ge(done, 16)
        STACKS = 16 * (4 * len(SLOTS) + 1)

        @block.tensor
        def _(pe):
            mm = nc.tensor.matmul
            pe.wait_ge(w_in, 16 * N_W)
            pe.wait_ge(c_in, 16 * N_C)
            mm(ps[:, TR, 0:D], wfeat[:, 0, :], wfeat[:, 1, :], start=True, stop=True).then_inc(wstep, 1)
            pe.wait_ge(wstep_c, 1)
            mm(ps[:, A, 0:D], wqT[:], mblk[:], start=True, stop=True).then_inc(wstep, 1)
            mm(ps[:, ST, 0:D], mblk[:], wqT[:], start=True, stop=True).then_inc(wstep, 1)
            pe.wait_ge(wstep_c, 3)
            half = NP * PR // 2
            mm(ps[:, OUT0, 0:half], waT[:], expand[:, 0:half], start=True, stop=True).then_inc(wstep, 1)
            mm(ps[:, OUT1, 0:half], waT[:], expand[:, half:], start=True, stop=True).then_inc(wstep, 1)
            pe.wait_ge(wstep_c, 5)
            def group(g):
                pe.wait_ge(h_ready, g + 1)
                if not isinstance(g, int) or g:
                    pe.wait_ge(hT_ready, g)
                for cc in range(GC):
                    t = nc.tensor.transpose(ps[:, TR, cc * CH:(cc + 1) * CH], h_tok[:, cc, :], ident[:])
                t.then_inc(hps_ready, 1)
                pe.wait_ge(hT_ready, g + 1)
                for t, w in enumerate((wq[:], wa[:], wkv[:, 0, :])):
                    if not isinstance(g, int) or g:
                        pe.wait_ge(rest1, 3 * g)
                    mm(ps[:, SQ + t, :], w, hT[:, WINDOW:], start=True, stop=True).then_inc(proj_ready, 1)
                for cc in range(GC):
                    if not isinstance(g, int) or g or cc > 1:
                        pe.wait_ge(kv_copied, 2 * GC * g + 2 * (cc - 1))
                    bank = OUT0 + cc % 2
                    mm(ps[:, bank, 0:2 * D], hT[:, WINDOW + cc * CH:WINDOW + (cc + 1) * CH], wkv[:].rearrange("p a d -> p (a d)"),
                       start=True, stop=True)
                    mm(ps[:, bank, 2 * D:3 * D], hT[:, cc * CH:(cc + 1) * CH], wkv[:, 1, :],
                       start=True, stop=True).then_inc(kv_proj, 1)

            group(0)
            with pe.Fori(1, NG) as g:
                group(g)

            pe.wait_ge(hTall_done, NG)
            pe.wait_ge(kv_copied, 2 * GC * NG)
            pe.wait_ge(rest1, 3 * NG)

            def post(c, u, p):
                static = isinstance(c, int)
                has = [not static or 0 <= c - k < NC for k in range(4)]
                if u == 0 and has[1]:
                    pe.wait_ge(evac_done, UNITS * c)
                    if not static or c > 1:
                        pe.wait_ge(x1_ready, c - 1)
                    if not static or c > 2:
                        pe.wait_ge(r_logit, c - 2)
                    for s in range(4):
                        t = nc.tensor.transpose(ps[:, TR, s * CH:(s + 1) * CH], linT[:, 1 - p, s, :], ident[:])
                    t.then_inc(t_lin, 1)
                if u == 1 and has[1]:
                    pe.wait_ge(norm_lin, c)
                    for s in range(4):
                        t = nc.tensor.transpose(ps[:, TR, s * CH:(s + 1) * CH], winT[:, 1 - p, s, :], ident[:])
                    t.then_inc(t_win, 1)
                if u == 2:
                    if has[1]:
                        pe.wait_ge(norm_win, c)
                    else:
                        pe.wait_ge(x1_ready, NC)
                        pe.wait_ge(r_logit, c - 2)
                    if has[3]:
                        pe.wait_ge(r_member, c - 2)
                        mm(ps[:, TR, 384:384 + E], before[:], member[:], start=True, stop=True)
                        mm(ps[:, TR, 392:392 + E], ones[:], member[:], start=True, stop=True).then_inc(pos_ready, 1)
                    if has[1]:
                        for s in range(2):
                            t = nc.tensor.transpose(ps[:, TR, s * CH:(s + 1) * CH], att[:, s].rearrange("p h d -> p (h d)"), ident[:])
                    if has[2]:
                        pe.wait_ge(h2_ready, c - 1)
                        t = nc.tensor.transpose(ps[:, TR, 2 * CH:3 * CH], h2[:, p, :], ident[:])
                    if has[1] or has[2]:
                        t.then_inc(t_cat, 1)
                if u == 3 and (has[1] or has[2]):
                    pe.wait_ge(cat_copied, c)
                    if has[3]:
                        pe.wait_ge(r_count, c - 2)
                    if has[1]:
                        mm(ps[:, TR, 384:384 + D], catT[:, 0, :], wout[:, 0, :], start=True, stop=False)
                        t = mm(ps[:, TR, 384:384 + D], catT[:, 1, :], wout[:, 1, :], start=False, stop=True)
                    if has[2]:
                        t = mm(ps[:, TR, 0:E], catT[:, 2, :], wgate[:], start=True, stop=True)
                    t.then_inc(wout_ready, 1)

            def chunk(c, p, i):
                first = isinstance(c, int) and c == 0
                pe.wait_ge(stack_in[p], STACKS * (i + 1))
                for u in range(UNITS):
                    n = c * UNITS + u
                    j, hf = u // 2, u % 2
                    early = isinstance(n, int)
                    if not early or n:
                        pe.wait_ge(max_done, n)
                    for hh in range(8):
                        h = 8 * hf + hh
                        r = WINDOW * (hh % 2)
                        t = mm(ps[r:r + WINDOW, SQ, (hh // 2) * CH:(hh // 2 + 1) * CH], qs[:, p, h, j * WINDOW:(j + 1) * WINDOW],
                               ks[:, p, j, h, :], start=True, stop=True)
                    t.then_inc(sq_ready, 1)
                    if not early or n:
                        pe.wait_ge(square_done, n)
                    for g in range(4):
                        t = mm(ps[:, A, g * CH:(g + 1) * CH], ks[:, p, 1, 4 * u + g, :], as_[:, p, 4 * u + g, :], start=True, stop=True)
                    t.then_inc(a_ready, 1)
                    if not early or n:
                        pe.wait_ge(phisq_done, n)
                    for k in range(2):
                        t = mm(ps[0:PR, PHI, k * CH:(k + 1) * CH], wphi[:, 2 * u + k, :],
                               hT_all[:, bass.ds(c, 1), :].rearrange("p a t -> p (a t)"), start=True, stop=True)
                    t.then_inc(phi_ready, 1)
                    pe.wait_ge(phik_ready, c + 1)
                    if not early or n:
                        pe.wait_ge(sadd_done, n)
                    for k in range(2):
                        hp = 2 * (2 * u + k)
                        t = mm(ps[0:PR, KV, k * 2 * UD:(k + 1) * 2 * UD], phik[:, p, hp:hp + 2, :].rearrange("p h f -> p (h f)"),
                               v1[:, p, 1, hp:hp + 2, 0:UD], start=True, stop=True)
                    t.then_inc(kv_ready, 1)
                    if not first:
                        post(c, u, p)
                    pe.wait_ge(mneg_ready, n + 1)
                    if not early or n:
                        pe.wait_ge(exp_done, n)
                    for hh in range(8):
                        h = 8 * hf + hh
                        mm(ps[:, ST, hh * WINDOW:(hh + 1) * WINDOW], ks[:, p, j, h, :], qs[:, p, h, j * WINDOW:(j + 1) * WINDOW],
                           start=(hh == 0), stop=False, skip_group_check=True)
                    for pr in range(4):
                        for part in range(2):
                            t = mm(ps[:, ST, pr * CH:(pr + 1) * CH], mneg[:, part, pr:pr + 1].to_broadcast([128, 128]), identb[:],
                                   start=False, stop=(part == 1), skip_group_check=True)
                    t.then_inc(st_ready, 1)
                    bank = OUT0 + u % 2
                    pe.wait_ge(phisq_done, n + 1)
                    if not early or n > 1:
                        pe.wait_ge(evac_done, n - 1)
                    if not early or n > 3:
                        pe.wait_ge(state_done, n - 3)
                    for k in range(2):
                        t = mm(ps[64 * k:64 * k + 64, bank, 0:CH], state[:, 2 * (2 * u + k):2 * (2 * u + k) + 2, :].rearrange("p h f -> p (h f)"),
                               phiq[:, u % 2, k, :], start=True, stop=False, skip_group_check=True)
                    t.then_inc(inter_done, 1)
                    pe.wait_ge(amask_ready, n + 1)
                    for g in range(4):
                        mm(ps[32 * g:32 * g + 32, bank, 0:CH], v1[:, p, 1, 4 * u + g, :], amat[:, u % 2, g, :],
                           start=False, stop=True, skip_group_check=True)
                    pe.wait_ge(exp_done, n + 1)
                    for hh in range(8):
                        g, s = hh % 4, hh // 4
                        t = mm(ps[32 * g:32 * g + 32, bank, CH + s * WINDOW:CH + (s + 1) * WINDOW], v1[:, p, j, 8 * hf + hh, :],
                               pmat[:, u % 2, hh, :], start=True, stop=True, skip_group_check=True)
                    t.then_inc(out_ready, 1)

            for c in range(4):
                chunk(c, c % 2, c // 2)
            with pe.Fori(2, NC // 2) as i:
                for p in range(2):
                    chunk(i * 2 + p, p, i)
            for c in range(NC, NC + 3):
                for u in range(UNITS):
                    post(c, u, c % 2)

            pe.wait_ge(x1_ready, NC)
            pe.wait_ge(r_count, NC)
            pe.wait_ge(table_ready, 1)
            pe.wait_ge(e_in, 16 * 6)
            pe.wait_ge(b_in, 16 * 7)

            def expert(j):
                return pe.value_load(table[0:1, 0, bass.ds(j, 1)], min_val=0, max_val=E - 1)

            def rhs(ap):
                return ap.rearrange("p a f -> p (a f)")

            def step(j, k, turn):
                static = isinstance(j, int)
                on = lambda d: not static or 0 <= j + d < NT
                if (on(0) or on(2)) and not (static and j == -2):
                    pe.wait_ge(zx_copied, j + 2)
                if on(0):
                    pe.wait_ge(z_ready, j + 1)
                    for s in range(2):
                        t = nc.tensor.transpose(ps[:, TZX, s * CH:(s + 1) * CH], z[:, k % 2, s * CH:(s + 1) * CH], ident[:])
                if on(2):
                    pe.wait_ge(xin_ready[(k + 2) % 4], 16 * (turn(2) + 1))
                    t = nc.tensor.transpose(ps[:, TZX, 2 * CH:3 * CH], xin[:, (k + 2) % 4, 0:D], ident[:])
                if on(0) or on(2):
                    t.then_inc(tzx_ready, 1)
                if on(1):
                    pe.wait_ge(zx_copied, computed(pe, j + 2))
                    if not static or j >= 0:
                        pe.wait_ge(x12_added, computed(pe, j + 1))
                    mm(ps[:, X12, :], zxT[:, (k + 1) % 2, 2, :], rhs(w12[:, bass.ds(expert(j + 1), 1), :]), start=True, stop=True).then_inc(x12_ready, 1)
                if on(-2):
                    pe.wait_ge(oT_copied, computed(pe, j - 1))
                    if not static or j > 2:
                        pe.wait_ge(y_added, computed(pe, j - 2))
                    e = expert(j - 2)
                    for s in range(2):
                        t = mm(ps[:, Y, 0:D], oT[:, k % 2, s, :], rhs(w3[:, bass.ds(e, 1), s, :]), start=(s == 0), stop=(s == 1))
                    t.then_inc(y_ready, 1)
                if on(-1):
                    pe.wait_ge(o_ready, j)
                    if not static or j > 1:
                        pe.wait_ge(oT_copied, j - 1)
                    for s in range(2):
                        t = nc.tensor.transpose(ps[:, TO, s * CH:(s + 1) * CH], og[:, (k + 1) % 2, s * CH:(s + 1) * CH], ident[:])
                    t.then_inc(to_ready, 1)
                if on(0):
                    pe.wait_ge(zx_copied, computed(pe, j + 3))
                    if not static or j > 0:
                        pe.wait_ge(l_added, computed(pe, j))
                    e = expert(j)
                    for s in range(2):
                        t = mm(ps[:, GL, :], zxT[:, k % 2, s, :], rhs(wgl[:, bass.ds(e, 1), s, :]), start=(s == 0), stop=(s == 1))
                    t.then_inc(gl_ready, 1)

            run_steps(pe, step)

        @block.scalar
        def _(act):
            a_ = nc.scalar.activation
            act.wait_ge(wstep, 2)
            act.wait_ge(c_in, 16 * N_C)
            nc.scalar.mul(wa[:], ps[:, A, 0:D], 0.5).then_inc(wstep_c, 1)
            act.wait_ge(wstep, 3)
            nc.scalar.mul(waT[:], ps[:, ST, 0:D], 0.5).then_inc(wstep_c, 1)
            act.wait_ge(wstep, 4)
            nc.scalar.copy(wphi[:, 0:NP // 2, :].rearrange("p a f -> p (a f)"), ps[:, OUT0, 0:NP * PR // 2]).then_inc(wstep_c, 1)
            act.wait_ge(wstep, 5)
            nc.scalar.copy(wphi[:, NP // 2:, :].rearrange("p a f -> p (a f)"), ps[:, OUT1, 0:NP * PR // 2]).then_inc(wstep_c, 1)
            def group(g):
                act.wait_ge(hps_ready, g + 1)
                act.wait_ge(halo, 2 * g + 1)
                a_(hT[:, WINDOW:], ps[:, TR, :], ACT.Copy, scale=norm_w[:, 0:1]).then_inc(hT_ready, 1)
                act.wait_ge(hT_ready, g + 1)
                nc.scalar.copy(hT_all[:, bass.ds(g * GC, GC), :].rearrange("p c t -> p (c t)"), hT[:, WINDOW:]).then_inc(hTall_done, 1)
                for t in range(3):
                    act.wait_ge(proj_ready, 3 * g + t + 1)
                    if t == 0:
                        if not isinstance(g, int) or g:
                            act.wait_ge(parts_out, g * (16 * 12 * GC))
                    if t == 2:
                        act.wait_ge(halo, 2 * g + 2)
                    dst = kp[:, 0, WINDOW:] if t == 2 else qa_parts[:, t, 0, :]
                    a_(dst, ps[:, SQ + t, :], ACT.Copy, scale=float(HD) ** -0.5 if t == 0 else 1.0).then_inc(part0, 1)
                for t in range(3):
                    act.wait_ge(rest1, 3 * g + t + 1)
                    dst = kp[:, 1, WINDOW:] if t == 2 else qa_parts[:, t, 1, :]
                    nc.scalar.copy(dst, rest[:, t, :]).then_inc(part1, 1)
                for cc in range(GC):
                    act.wait_ge(kv_proj, g * GC + cc + 1)
                    bank = OUT0 + cc % 2
                    nc.scalar.copy(k_tok[:, bass.ds(g * GC + cc, 1), :].rearrange("p a d -> p (a d)"), ps[:, bank, 0:D]).then_inc(kv_copied, 1)
                    nc.scalar.copy(v_all[:, bass.ds(g * GC + cc, 1), :, :].rearrange("p a w d -> p (a w d)"),
                                   ps[:, bank, D:3 * D]).then_inc(kv_copied, 1)

            group(0)
            with act.Fori(1, NG) as g:
                group(g)

            def post(c, u):
                static = isinstance(c, int)
                has = [not static or 0 <= c - k < NC for k in range(4)]
                if u == 0 and has[3]:
                    act.wait_ge(r_gap, c - 2)
                    a_(egap[:], gap[:], ACT.Exp).then_inc(r_egap, 1)
                if u == 2 and (has[1] or has[2]):
                    lo, hi = (0 if has[1] else 2), (3 if has[2] else 2)
                    act.wait_ge(t_cat, c)
                    nc.scalar.copy(catT[:, lo:hi].rearrange("p k t -> p (k t)"), ps[:, TR, lo * CH:hi * CH]).then_inc(cat_copied, 1)

            def chunk(c, p):
                for u in range(UNITS):
                    n = c * UNITS + u
                    early = isinstance(n, int)
                    j, hf = u // 2, u % 2
                    bank = OUT0 + u % 2
                    act.wait_ge(a_ready, n + 1)
                    if not early or n > 1:
                        act.wait_ge(out_ready, n - 1)
                    a_(amat[:, u % 2].rearrange("p g t -> p (g t)"), ps[:, A, :], ACT.Square).then_inc(square_done, 1)
                    act.wait_ge(phi_ready, n + 1)
                    a_(phiq[:, u % 2].rearrange("p k t -> p (k t)"), ps[0:PR, PHI, 0:2 * CH], ACT.Square, bias=fbias[:, 0:1]).then_inc(phisq_done, 1)
                    if not (early and c == 0):
                        post(c, u)
                    act.wait_ge(st_ready, n + 1)
                    a_(pmat[:, u % 2].rearrange("p g t -> p (g t)"), ps[:, ST, :], ACT.Exp).then_inc(exp_done, 1)
                    act.wait_ge(out_ready, n + 1)
                    if u == 0 and (not early or n > 4):
                        act.wait_ge(t_win, c - 1)
                    nc.scalar.copy(linT[:, p, u, :], ps[:, bank, 0:CH])
                    nc.scalar.copy(winT[:, p, 2 * hf:2 * hf + 2, j * WINDOW:(j + 1) * WINDOW],
                                   ps[:, bank, CH:2 * CH].rearrange("p (s t) -> p s t", s=2)).then_inc(evac_done, 1)

            for c in range(4):
                chunk(c, c % 2)
            with act.Fori(2, NC // 2) as i:
                for p in range(2):
                    chunk(i * 2 + p, p)
            for c in range(NC, NC + 3):
                for u in range(UNITS):
                    post(c, u)

            def step(j, k, turn):
                static = isinstance(j, int)
                on = lambda d: not static or 0 <= j + d < NT
                if on(0) or on(2):
                    lo, hi = (0 if on(0) else 2), (3 if on(2) else 2)
                    act.wait_ge(tzx_ready, j + 3)
                    if not static or j > -1:
                        act.wait_ge(x12_ready, j + 1)
                    if not static or j > 1:
                        act.wait_ge(gl_ready, j - 1)
                    if on(0):
                        nc.scalar.copy(zxT[:, k % 2, 0:2, :], ps[:, TZX, 0:2 * CH].rearrange("p (k t) -> p k t", k=2))
                    if on(2):
                        t = nc.scalar.copy(zxT[:, k % 2, 2, :], ps[:, TZX, 2 * CH:3 * CH])
                        t.then_inc(zx_copied, 1)
                    else:
                        nc.scalar.copy(zxT[:, k % 2, 2, 0:1], ident[:, 0:1]).then_inc(zx_copied, 1)
                if on(-1):
                    act.wait_ge(g_added, j)
                    if not static or j > 2:
                        act.wait_ge(o_ready, j - 2)
                    a_(sg[:, (k + 1) % 2, :], glb[:, (k + 1) % 2, 0:F], ACT.Silu).then_inc(silu_done, 1)
                    act.wait_ge(to_ready, j)
                    if not static or j > 2:
                        act.wait_ge(y_ready, j - 2)
                    nc.scalar.copy(oT[:, (k + 1) % 2].rearrange("p a t -> p (a t)"), ps[:, TO, 0:F]).then_inc(oT_copied, 1)
                if on(-2):
                    act.wait_ge(y_added, j - 1)
                    act.wait_ge(meta_copied, j - 1)
                    if not static or j >= 6:
                        act.wait_ge(y_out[(k + 2) % 4], 16 * turn(-2))
                    a_(yw[:, (k + 2) % 4, :], yb[:, k % 2, :], ACT.Copy, scale=mweight[:, (k + 2) % 4:(k + 2) % 4 + 1]).then_inc(y_weighted, 1)

            run_steps(act, step)

        @block.vector
        def _(dve):
            v = nc.vector
            v.memset(hT[:, 0:WINDOW], 0.0).then_inc(settled, 1)
            v.memset(hT[:, GT:GT + WINDOW], 0.0).then_inc(zeroed, 1)
            v.memset(kp[:, :, GT:GT + WINDOW], 0.0).then_inc(zeroed, 1)
            v.memset(phik[:], 0.0).then_inc(zeroed, 1)
            v.memset(v1[:], 0.0).then_inc(zeroed, 1)
            v.memset(state[:], 0.0).then_inc(zeroed, 1)
            v.memset(u_tok[:, :, 0:1], 1.0).then_inc(zeroed, 1)
            v.memset(minus_half[:], -0.5).then_inc(zeroed, 1)
            v.memset(k_tok[:, NC, :], 0.0).then_inc(zeroed, 1)
            v.memset(v_all[:, NC, :, :], 0.0).then_inc(zeroed, 1)
            dve.wait_ge(zeroed, 9)
            v.memset(v1[:, :, :, :, HD:HD + 1], 1.0).then_inc(zeroed, 1)
            dve.wait_ge(zeroed, 10)
            dve.wait_ge(wstep, 1)
            dve.wait_ge(c_in, 16 * N_C)
            v.tensor_tensor(mblk[:], ps[:, TR, 0:D], blockdiag[:], ALU.mult).then_inc(wstep_c, 1)
            def group(g):
                dve.wait_ge(x_in, 16)
                for cc in range(GC):
                    v.bn_stats(stats[:, cc, :], x_all[:, bass.ds(g * GC + cc, 1), :].rearrange("p a d -> p (a d)")).then_inc(mv_ready, 1)
                dve.wait_ge(mv_ready, computed(dve, g * (2 * GC) + GC))
                for cc in range(GC):
                    v.bn_aggr(mvg[:, cc, :], stats[:, cc, :]).then_inc(mv_ready, 1)
                dve.wait_ge(mv_ready, (g + 1) * (2 * GC))
                v.tensor_copy(mv[:, bass.ds(g * GC, GC), :].rearrange("p c a -> p (c a)"), mvg[:].rearrange("p c a -> p (c a)"))
                var = mvg[:, :, 1]
                v.tensor_scalar(vareps[:, :, 0], var, EPS_LN, None, ALU.add).then_inc(ve_ready, 1)
                dve.wait_ge(pow_ready, g * 2 + 1)
                rs = rstd[:, bass.ds(g * GC, GC)]
                v.tensor_tensor(rboth[:], rs, rs, ALU.mult).then_inc(rb_ready, 1)
                dve.wait_ge(rb_ready, g * 3 + 1)
                v.tensor_tensor(rboth[:], rboth[:], var, ALU.mult).then_inc(rb_ready, 1)
                dve.wait_ge(rb_ready, g * 3 + 2)
                v.tensor_scalar(vareps[:, :, 1], rboth[:], EPS_RMS, None, ALU.add).then_inc(ve_ready, 1)
                dve.wait_ge(pow_ready, g * 2 + 2)
                v.tensor_tensor(rboth[:], vareps[:, :, 1], rs, ALU.mult).then_inc(rb_ready, 1)
                dve.wait_ge(rb_ready, g * 3 + 3)
                if not isinstance(g, int) or g:
                    dve.wait_ge(hps_ready, g)
                for cc in range(GC):
                    t = v.tensor_scalar(h_tok[:, cc, :], x_all[:, bass.ds(g * GC + cc, 1), :].rearrange("p a d -> p (a d)"),
                                        mvg[:, cc, 0:1], rboth[:, cc:cc + 1],
                                        ALU.subtract, ALU.mult)
                t.then_inc(h_ready, 1)
                kg = keep[:, bass.ds(g * GC, 1)]
                if not isinstance(g, int) or g:
                    dve.wait_ge(kv_proj, g * GC)
                if not isinstance(g, int) or g:
                    dve.wait_ge(proj_ready, g * 3)
                if not isinstance(g, int) or g:
                    dve.wait_ge(hTall_done, g)
                v.tensor_scalar(hT[:, 0:WINDOW], hT[:, GT:GT + WINDOW], kg, None, ALU.mult).then_inc(halo, 1)
                if not isinstance(g, int) or g:
                    dve.wait_ge(parts_out, g * (16 * 12 * GC))
                v.tensor_scalar(kp[:, :, 0:WINDOW], kp[:, :, GT:GT + WINDOW], kg, None, ALU.mult).then_inc(halo, 1)
                for t in range(3):
                    dve.wait_ge(part0, 3 * g + t + 1)
                    if t == 0:
                        if not isinstance(g, int) or g:
                            dve.wait_ge(part2, 3 * g)
                    p0 = kp[:, 0, WINDOW:] if t == 2 else qa_parts[:, t, 0, :]
                    v.scalar_tensor_tensor(out=rest[:, t, :], in0=ps[:, SQ + t, :], scalar=float(HD) ** -0.5 if t == 0 else 1.0, in1=p0,
                                           op0=ALU.mult, op1=ALU.subtract).then_inc(rest1, 1)
                for t in range(3):
                    dve.wait_ge(part1, 3 * g + t + 1)
                    p1 = kp[:, 1, WINDOW:] if t == 2 else qa_parts[:, t, 1, :]
                    p2 = kp[:, 2, WINDOW:] if t == 2 else qa_parts[:, t, 2, :]
                    v.tensor_tensor(p2, rest[:, t, :], p1, ALU.subtract).then_inc(part2, 1)

            group(0)
            with dve.Fori(1, NG) as g:
                group(g)

            def key_features(c, p):
                static = isinstance(c, int)
                if not static or c > 1:
                    dve.wait_ge(out_ready, UNITS * (c - 1))
                    dve.wait_ge(phik_ready, c)
                if static:
                    dve.wait_ge(kv_copied, 2 * GC * NG)
                v.tensor_copy(v1[:, p, 1, :, 0:HD], v_all[:, bass.ds(c, 1), 0, :].rearrange("p a (h d) -> p (a h) d", h=H))
                v.tensor_copy(v1[:, p, 0, :, 0:HD], v_all[:, bass.ds(c, 1), 1, :].rearrange("p a (h d) -> p (a h) d", h=H))
                v.tensor_copy(u_tok[:, :, 1:UD], k_tok[:, bass.ds(c, 1), :].rearrange("p a (h d) -> p (a h) d", h=H)).then_inc(us, 1)
                dve.wait_ge(us, c * 2 + 1)
                v.tensor_reduce(usum[:], u_tok[:], AX.X, ALU.add).then_inc(us, 1)
                dve.wait_ge(us, c * 2 + 2)
                v.scalar_tensor_tensor(out=ut[:], in0=u_tok[:], scalar=2.0, in1=usum[:].to_broadcast([CH, H, UD]),
                                       op0=ALU.mult, op1=ALU.subtract).then_inc(ut_done, 1)
                at = UD
                for dl in range(1, UD):
                    w = UD - dl
                    v.tensor_tensor(phik[:, p, :, at:at + w], u_tok[:, :, 0:w], u_tok[:, :, dl:UD], ALU.mult)
                    at += w
                dve.wait_ge(ut_done, c + 1)
                v.tensor_tensor(phik[:, p, :, 0:UD], ut[:], u_tok[:], ALU.mult).then_inc(phik_ready, 1)

            def post(c, u, p, i):
                static = isinstance(c, int)
                has = [not static or 0 <= c - k < NC for k in range(4)]
                tr = ps[:, TR, :].rearrange("p (h f) -> p h f", f=32)
                z3 = zrec[:].rearrange("p (h a) -> p h a", a=1)
                if u == 0 and has[1]:
                    xc = x_all[:, bass.ds(c - 1, 1), :].rearrange("p a d -> p (a d)")
                    v.tensor_scalar(xh[:], xc, mv[:, bass.ds(c - 1, 1), 0:1].rearrange("p a d -> p (a d)"), rstd[:, bass.ds(c - 1, 1)],
                                    ALU.subtract, ALU.mult).then_inc(xh0, 1)
                    dve.wait_ge(xh0, c)
                    v.tensor_tensor(xh[:], xh[:], xc, ALU.add).then_inc(xh_ready, 1)
                    dve.wait_ge(t_lin, c)
                    v.tensor_scalar(z3, tr[:, :, HD:UD], EPS_LIN, None, ALU.add).then_inc(z1, 1)
                    dve.wait_ge(z1, c)
                    v.reciprocal(zrec[:], zrec[:]).then_inc(z2, 1)
                    dve.wait_ge(z2, c * 2 - 1)
                    if not static or c > 1:
                        dve.wait_ge(t_cat, c - 1)
                    v.tensor_tensor(att[:, 0], tr[:, :, 0:HD], zrec[:].to_broadcast([CH, H, HD]), ALU.mult).then_inc(norm_lin, 1)
                if u == 1 and has[1]:
                    dve.wait_ge(t_win, c)
                    dve.wait_ge(norm_lin, c)
                    v.reciprocal(z3, tr[:, :, HD:UD]).then_inc(z2, 1)
                    dve.wait_ge(z2, c * 2)
                    v.tensor_tensor(att[:, 1], tr[:, :, 0:HD], zrec[:].to_broadcast([CH, H, HD]), ALU.mult).then_inc(norm_win, 1)
                if u == 1 and has[3]:
                    n = c - 2
                    row = routed_row[:, 1 - p, :]
                    dve.wait_ge(r_egap, n)
                    v.tensor_scalar(wsum[:], egap[:], 1.0, None, ALU.add).then_inc(r_ws, 1)
                    dve.wait_ge(r_ws, n)
                    v.reciprocal(w01[:, 0:1], wsum[:]).then_inc(r_w, 1)
                    dve.wait_ge(r_w, n)
                    v.tensor_tensor(w01[:, 1:2], w01[:, 0:1], egap[:], ALU.mult).then_inc(r_w2, 1)
                    dve.wait_ge(r_w2, n)
                    if not static or c > 4:
                        dve.wait_ge(scattered[1 - p], 32 * (i - 2 + p))
                    v.tensor_scalar(tmp8[:, 0], onehot[:, 0], w01[:, 0:1], None, ALU.mult).then_inc(r_tmp, 1)
                    v.tensor_scalar(tmp8[:, 1], onehot[:, 1], float(N), None, ALU.mult).then_inc(r_tmp, 1)
                    dve.wait_ge(r_tmp, 2 * n)
                    v.scalar_tensor_tensor(out=row[:, D:D + E], in0=onehot[:, 1], scalar=w01[:, 1:2], in1=tmp8[:, 0], op0=ALU.mult, op1=ALU.add)
                    v.scalar_tensor_tensor(out=row[:, D + E:], in0=member[:], scalar=tokid[:, bass.ds(c - 3, 1)], in1=tmp8[:, 1],
                                           op0=ALU.mult, op1=ALU.add).then_inc(r_row, 1)
                if u == 2 and has[3]:
                    n = c - 2
                    dve.wait_ge(pos_ready, n)
                    if has[1] or has[2]:
                        dve.wait_ge(cat_copied, c)
                    v.tensor_tensor(place[:], ps[:, TR, 384:384 + E], count[:], ALU.add).then_inc(r_place, 1)
                    dve.wait_ge(r_place, n)
                    v.tensor_tensor(count[:], ps[:, TR, 392:392 + E], count[:], ALU.add).then_inc(r_count, 1)
                    v.tensor_tensor(placed[:], onehot[:], place[:].rearrange("p (a e) -> p a e", a=1).to_broadcast([CH, 2, E]),
                                    ALU.mult).then_inc(r_placed, 1)
                    dve.wait_ge(r_placed, n)
                    v.tensor_reduce(slotf[:], placed[:], AX.X, ALU.add).then_inc(r_slotf, 1)
                    dve.wait_ge(r_slotf, n)
                    v.tensor_copy(slot[:, 1 - p, :], slotf[:]).then_inc(r_slot, 1)
                if u == 3 and has[1]:
                    dve.wait_ge(wout_ready, c)
                    dve.wait_ge(xh_ready, c)
                    xc = x_all[:, bass.ds(c - 1, 1), :].rearrange("p a d -> p (a d)")
                    v.tensor_tensor(xc, ps[:, TR, 384:384 + D], xh[:], ALU.add).then_inc(x1_ready, 1)
                    dve.wait_ge(x1_ready, computed(dve, c))
                    v.bn_stats(st2[:], xc).then_inc(st2_done, 1)
                    dve.wait_ge(st2_done, computed(dve, c))
                    if not static or c > 1:
                        dve.wait_ge(h2_ready, computed(dve, c - 1))
                    v.bn_aggr(mv2[:], st2[:]).then_inc(mv2_ready, 1)
                    dve.wait_ge(mv2_ready, c)
                    v.tensor_scalar(ve2[:], mv2[:, 1:2], EPS_LN, None, ALU.add).then_inc(ve2_ready, 1)
                if u == 3 and has[1]:
                    dve.wait_ge(rstd2_ready, c)
                    if has[3]:
                        dve.wait_ge(staged, c - 2)
                    v.tensor_scalar(h2[:, 1 - p, :], x_all[:, bass.ds(c - 1, 1), :].rearrange("p a d -> p (a d)"), mv2[:, 0:1], rstd2[:, 0:1],
                                    ALU.subtract, ALU.mult).then_inc(h2_ready, 1)
                if u == 3 and has[2]:
                    n = c - 1
                    dve.wait_ge(wout_ready, c)
                    v.tensor_tensor(logit[:], ps[:, TR, 0:E], bgate[:], ALU.add).then_inc(r_logit, 1)
                    dve.wait_ge(r_logit, computed(dve, n))
                    v.max(top[:], logit[:]).then_inc(r_top, 1)
                    dve.wait_ge(r_top, computed(dve, n))
                    v.max_index(topi[:], top[:], logit[:]).then_inc(r_idx, 1)
                    if not static or c > 2:
                        dve.wait_ge(r_egap, n - 1)
                    v.tensor_tensor(gap[:], top[:, 1:2], top[:, 0:1], ALU.subtract).then_inc(r_gap, 1)
                    dve.wait_ge(r_idx, n)
                    v.tensor_copy(topf[:], topi[:, 0:2]).then_inc(r_idxf, 1)
                    dve.wait_ge(r_idxf, n)
                    if not static or c > 2:
                        dve.wait_ge(r_placed, n - 1)
                        dve.wait_ge(r_row, n - 1)
                    for s in range(2):
                        v.tensor_scalar(onehot[:, s], iota8[:], topf[:, s:s + 1], None, ALU.is_equal).then_inc(r_oh, 1)
                    dve.wait_ge(r_oh, 2 * n)
                    if not static or c > 2:
                        dve.wait_ge(pos_ready, n - 1)
                    v.tensor_tensor(member[:], onehot[:, 0], onehot[:, 1], ALU.add).then_inc(r_member, 1)

            def chunk(c, p, i):
                first = isinstance(c, int) and c == 0
                for u in range(UNITS):
                    n = c * UNITS + u
                    dve.wait_ge(sq_ready, n + 1)
                    v.tensor_reduce(mrow[:], ps[:, SQ, :].rearrange("p (a k) -> p a k", k=CH), AX.X, ALU.max).then_inc(max_done, 1)
                    dve.wait_ge(max_done, n + 1)
                    v.tensor_scalar(mneg[:, 0], mrow[:], -1.0, None, ALU.mult).then_inc(nh_done, 1)
                    dve.wait_ge(nh_done, n + 1)
                    v.scalar_tensor_tensor(out=mneg[:, 1], in0=mrow[:], scalar=-1.0, in1=mneg[:, 0],
                                           op0=ALU.mult, op1=ALU.subtract).then_inc(mneg_ready, 1)
                    if not first:
                        post(c, u, p, i)
                    kc = keep[0:PR, bass.ds(c + 1, 1)]
                    dve.wait_ge(kv_ready, n + 1)
                    dve.wait_ge(mneg_ready, n + 1)
                    v.scalar_tensor_tensor(out=sadd[:], in0=ps[0:PR, KV, 0:4 * UD].rearrange("p (h f) -> p h f", f=UD), scalar=kc,
                                           in1=statemask[:].rearrange("p (h f) -> p h f", f=UD), op0=ALU.mult, op1=ALU.mult).then_inc(sadd_done, 1)
                    dve.wait_ge(sadd_done, n + 1)
                    dve.wait_ge(inter_done, n + 1)
                    s = state[:, 4 * u:4 * u + 4, 0:UD]
                    v.scalar_tensor_tensor(out=s, in0=s, scalar=kc, in1=sadd[:], op0=ALU.mult, op1=ALU.add).then_inc(state_done, 1)
                    if u == 1:
                        key_features(c + 1, 1 - p)

            key_features(0, 0)
            for c in range(4):
                chunk(c, c % 2, c // 2)
            with dve.Fori(2, NC // 2) as i:
                for p in range(2):
                    chunk(i * 2 + p, p, i)
            for c in range(NC, NC + 3):
                for u in range(UNITS):
                    post(c, u, c % 2, c // 2)

            links = [0]

            def link(t):
                links[0] += 1
                t.then_inc(tab, 1)
                dve.wait_ge(tab, links[0])

            dve.wait_ge(r_count, NC)
            link(v.tensor_copy(tail_i[:], count[0:1, :]))
            link(v.tensor_tensor(ntile[:], count[0:1, :], region0[0:1, :], ALU.subtract))
            link(v.tensor_scalar(ntile[:], ntile[:], float(CH - 1), None, ALU.add))
            link(v.tensor_copy(counts_i[:], ntile[:]))
            link(v.tensor_scalar(ntile_i[:], counts_i[:], 7, None, ALU.arith_shift_right))
            link(v.tensor_copy(ntile[:], ntile_i[:]))
            link(v.tensor_tensor_scan(ends[:], ntile[:], ntile[:], 0.0, ALU.add, ALU.bypass))
            link(v.tensor_tensor(tmpt[:, 0], ends[:, E - 1:E].to_broadcast([1, NT]), tiles[:], ALU.min))
            t3 = lambda k: tmpt[:, k].rearrange("p (t a) -> p t a", a=1)
            e3 = lambda x: x.rearrange("p (a e) -> p a e", a=1).to_broadcast([1, NT, E])
            link(v.tensor_tensor(cmp8[:, 0], t3(0).to_broadcast([1, NT, E]), e3(ends[:]), ALU.is_ge))
            link(v.tensor_reduce(tmpt[:, 1], cmp8[:, 0], AX.X, ALU.add))
            link(v.tensor_tensor(cmp8[:, 1], cmp8[:, 0], e3(ntile[:]), ALU.mult))
            link(v.tensor_reduce(tmpt[:, 2], cmp8[:, 1], AX.X, ALU.add))
            link(v.tensor_tensor(tmpt[:, 0], tmpt[:, 0], tmpt[:, 2], ALU.subtract))
            link(v.tensor_scalar(tmpt[:, 0], tmpt[:, 0], float(CH), None, ALU.mult))
            link(v.scalar_tensor_tensor(out=tmpt[:, 3], in0=tmpt[:, 1], scalar=float(REGION), in1=tmpt[:, 0], op0=ALU.mult, op1=ALU.add))
            link(v.tensor_scalar(table[:, 0, :], tmpt[:, 1], float(E - 1), None, ALU.min))
            v.tensor_copy(table[:, 1, :], tmpt[:, 3]).then_inc(table_ready, 1)
            dve.wait_ge(table_ready, 1)
            dve.wait_ge(b_in, 16 * 7)

            def expert(j):
                return dve.value_load(table[0:1, 0, bass.ds(j, 1)], min_val=0, max_val=E - 1)

            def flat(ap):
                return ap.rearrange("p a f -> p (a f)")

            def step(j, k, turn):
                static = isinstance(j, int)
                on = lambda d: not static or 0 <= j + d < NT
                if on(-1):
                    dve.wait_ge(gl_ready, computed(dve, j))
                    e = expert(j - 1)
                    q = (k + 1) % 2
                    if not static or j > 2:
                        dve.wait_ge(silu_done, j - 2)
                        dve.wait_ge(o_ready, j - 2)
                    v.tensor_tensor(glb[:, q, 0:F], ps[:, GL, 0:F], flat(bgl[:, bass.ds(e, 1), 0:F]), ALU.add).then_inc(g_added, 1)
                    v.tensor_tensor(glb[:, q, F:], ps[:, GL, F:], flat(bgl[:, bass.ds(e, 1), F:]), ALU.add).then_inc(l_added, 1)
                    dve.wait_ge(silu_done, j)
                    dve.wait_ge(l_added, j)
                    if not static or j > 2:
                        dve.wait_ge(to_ready, j - 2)
                    v.tensor_tensor(og[:, q, :], sg[:, q, :], glb[:, q, F:], ALU.mult).then_inc(o_ready, 1)
                if on(1):
                    dve.wait_ge(x12_ready, computed(dve, j + 2))
                    q = (k + 1) % 2
                    e = expert(j + 1)
                    if not static or j > 0:
                        dve.wait_ge(z_ready, j)
                    v.tensor_tensor(x12[:, q, :], ps[:, X12, :], flat(b12[:, bass.ds(e, 1), :]), ALU.add).then_inc(x12_added, 1)
                    dve.wait_ge(x12_added, j + 2)
                    if not static or j > 0:
                        dve.wait_ge(tzx_ready, j + 2)
                    v.tensor_tensor(z[:, q, :], x12[:, q, 0:F], x12[:, q, F:], ALU.mult).then_inc(z_ready, 1)
                    m = (k + 1) % 4
                    if not static or j >= 3:
                        dve.wait_ge(y_weighted, j - 2)
                        dve.wait_ge(y_out[m], 16 * turn(1))
                    v.tensor_copy(mweight[:, m:m + 1], xin[:, m, bass.ds(e + D, 1)])
                    v.tensor_copy(mrowid[:, m:m + 1], xin[:, m, bass.ds(e + (D + E), 1)]).then_inc(meta_copied, 1)
                if on(-2):
                    dve.wait_ge(y_ready, computed(dve, j - 1))
                    if not static or j > 3:
                        dve.wait_ge(y_weighted, computed(dve, j - 3))
                    v.tensor_tensor(yb[:, k % 2, :], ps[:, Y, 0:D], flat(b3[:, bass.ds(expert(j - 2), 1), :]), ALU.add).then_inc(y_added, 1)

            run_steps(dve, step)
            dve.wait_ge(res_in, 32)
            v.tensor_tensor(res[0], res[0], res[1], ALU.add).then_inc(res_sum, 1)
            dve.wait_ge(res_sum, 1)
            v.tensor_tensor(x_all[:], x_all[:], res[0], ALU.add).then_inc(out_sum, 1)

        @block.gpsimd
        def _(pool):
            q = nc.gpsimd
            pool.wait_ge(zeroed, 7)
            mh = minus_half[:, 0:GC]
            def group(g):
                pool.wait_ge(ve_ready, computed(pool, g * 2 + 1))
                q.tensor_tensor(rstd[:, bass.ds(g * GC, GC)], vareps[:, :, 0], mh, ALU.pow).then_inc(pow_ready, 1)
                pool.wait_ge(ve_ready, computed(pool, g * 2 + 2))
                q.tensor_tensor(vareps[:, :, 1], vareps[:, :, 1], mh, ALU.pow).then_inc(pow_ready, 1)

            group(0)
            with pool.Fori(1, NG) as g:
                group(g)

            def post(c, u, p, i):
                static = isinstance(c, int)
                has = [not static or 0 <= c - k < NC for k in range(4)]
                if u == 1 and has[3]:
                    if not static or c > 4:
                        pool.wait_ge(scattered[1 - p], computed(pool, 32 * (i - 2 + p)))
                    pool.wait_ge(h2_ready, computed(pool, c - 2))
                    q.tensor_copy(routed_row[:, 1 - p, 0:D], h2[:, 1 - p, :]).then_inc(staged, 1)
                if u == 3 and has[1]:
                    pool.wait_ge(ve2_ready, computed(pool, c))
                    q.tensor_tensor(rstd2[:], ve2[:], minus_half[:, 0:1], ALU.pow).then_inc(rstd2_ready, 1)
                if u == 3 and has[3]:
                    pool.wait_ge(r_slot, computed(pool, c - 2))
                    pool.wait_ge(r_row, computed(pool, c - 2))
                    pool.wait_ge(staged, computed(pool, c - 2))
                    for k in range(2):
                        q.indirect_dma_start(routed, bass.IndirectOffsetOnAxis(slot[:, 1 - p, k:k + 1], 0), routed_row[:, 1 - p, :], None).then_inc(scattered[1 - p], 16)

            def chunk(c, p, i):
                first = isinstance(c, int) and c == 0
                for u in range(UNITS):
                    n = c * UNITS + u
                    pool.wait_ge(square_done, computed(pool, n + 1))
                    q.affine_select(out=amat[:, u % 2], in_=amat[:, u % 2], compare_op=ALU.is_ge, fill=0.0, base=0,
                                    pattern=[[0, 4], [1, CH]], channel_multiplier=-1).then_inc(amask_ready, 1)
                    if not first:
                        post(c, u, p, i)

            for c in range(4):
                chunk(c, c % 2, c // 2)
            with pool.Fori(2, NC // 2) as i:
                for p in range(2):
                    chunk(i * 2 + p, p, i)
            for c in range(NC, NC + 3):
                for u in range(UNITS):
                    post(c, u, c % 2, c // 2)

            def step(j, k, turn):
                if not isinstance(j, int) or 0 <= j - 2 < NT:
                    m = (k + 2) % 4
                    pool.wait_ge(y_weighted, computed(pool, j - 1))
                    q.indirect_dma_start(results, bass.IndirectOffsetOnAxis(mrowid[:, m:m + 1], 0), yw[:, m, :], None,
                                         bounds_check=RESULTS - 1, oob_is_err=False).then_inc(y_out[m], 16)

            run_steps(pool, step)


_NAMES = {"x": "L0_attn_x", "norm_w": "L0_attn_norm_w", "Wq": "L0_attn_Wq", "Wk": "L0_attn_Wk", "Wv": "L0_attn_Wv", "Wout": "L0_attn_Wout",
          **{n: "L0_ffn_" + n for n in ("Wgate", "bgate", "W1", "b1", "W2", "b2", "Wg", "bg", "Wl", "bl", "W3", "b3")}}


def kernel(**inputs):
    import concourse.bacc as _bacc
    from concourse.bass_utils import run_bass_kernel_spmd as _run

    arrays = {k: np.ascontiguousarray(inputs[v]) for k, v in _NAMES.items()}
    arrays["WqT"] = np.ascontiguousarray(np.transpose(inputs["L0_attn_Wq"]))
    arrays["WqfT"] = np.ascontiguousarray(np.tile(np.transpose(inputs["L0_attn_Wqf"]), (1, H)))
    arrays["WkfT"] = np.ascontiguousarray(np.tile(np.transpose(inputs["L0_attn_Wkf"]), (1, H)))
    con = constants()
    nc = _bacc.Bacc("TRN2", target_bir_lowering=False, num_devices=1)
    feed, ins, cin = {}, {}, {}
    for group, aps, pre in ((arrays, ins, "in_"), (con, cin, "const_")):
        for k, a in group.items():
            feed[pre + k] = a
            aps[k] = nc.dram_tensor(pre + k, a.shape, mybir.dt.from_np(a.dtype), kind="ExternalInput").ap()
    out = nc.dram_tensor("out", (B, T, D), F32, kind="ExternalOutput").ap()
    build(nc, ins, cin, out)
    r = _run(nc, [feed], core_ids=[0])
    return r.results[0]["out"]
```

```python
from contextlib import ExitStack

import numpy as np
import concourse.bass as bass
from concourse import mybir

ALU = mybir.AluOpType
ACT = mybir.ActivationFunctionType
AX = mybir.AxisListType
F32 = mybir.dt.float32
BF16 = mybir.dt.bfloat16

B, T, D = 2, 1024, 128
H, HD = 16, 8
WINDOW = 64
CH = 128
NC = B * T // CH
GC = 4
NG = NC // GC
GT = GC * CH
UNITS = 4
UD = HD + 1
NF = UD * (UD + 1) // 2
FS = 48
PR = 2 * FS
NP = H // 2
SLOTS = [(0, 2), (1, 1), (2, 0), (0, 1), (1, 0), (0, 0)]
RUNS = [(0, 0, 0, 3), (3, 0, 1, 2), (5, 0, 2, 1)]
KP = HD * len(SLOTS)
ROW_VALID, ROW_ONE = KP + WINDOW, KP + WINDOW + 1
KR = KP + WINDOW + 2
BIG = -1.0e30
E, F = 8, 256
TOPK = 2
N = B * T
REGION = N + CH
ROW = D + 2 * E
NT = TOPK * N // CH + E
RESULTS = TOPK * N
EPS_LN, EPS_RMS, EPS_LIN = 1e-5, 1e-6, 1e-6


def constants():
    c = {}
    c["ident"] = np.eye(128, dtype=np.float32)
    feats = [(i, i + dl) for dl in range(UD) for i in range(UD - dl)]
    sums = np.zeros((KR, 2, PR), np.float32)
    for par in range(2):
        for r, (i, j) in enumerate(feats):
            for z in {i, j}:
                for s in range(3):
                    if z:
                        sums[s * HD + z - 1, par, par * FS + r] = 1.0
            if i == 0:
                sums[ROW_ONE, par, par * FS + r] = 1.0
    blk = np.arange(D) // HD
    c["blockdiag"] = (blk[:, None] == blk[None, :]).astype(np.float32)
    sm = np.zeros((PR, 2, 2, UD), np.float32)
    for par in range(2):
        sm[par * FS:(par + 1) * FS, :, par] = 1.0
    c["statemask"] = sm.reshape(PR, 4 * UD)
    keep = np.ones((128, NC + 1), np.float32)
    keep[:, ::T // CH] = 0.0
    c["keep"] = keep
    q, kap = np.arange(WINDOW), np.arange(CH)
    qrows = np.zeros((KR - KP, H, CH), np.float32)
    qrows[:WINDOW] = (q[:, None] == kap[None, :] % WINDOW)[:, None]
    qrows[WINDOW] = 1.0
    arows = np.zeros((KR - KP, H, CH), np.float32)
    arows[WINDOW + 1] = 1.0
    krows = np.zeros((KR - KP, H, CH), np.float32)
    krows[:WINDOW] = np.where((kap >= q[:, None]) & (kap <= q[:, None] + WINDOW), 0.0, BIG)[:, None]
    krows[WINDOW + 1] = 1.0
    valid = np.zeros((NC, H, CH), np.float32)
    valid[::T // CH, :, :WINDOW] = BIG
    c["iota8"] = np.tile(np.arange(E, dtype=np.float32), (128, 1))
    c["region0"] = np.tile(np.arange(E, dtype=np.float32) * REGION, (128, 1))
    c["tokid"] = (np.arange(CH)[:, None] + CH * np.arange(NC)[None]).astype(np.float32)
    pad = np.zeros((CH, ROW), np.float32)
    pad[:, D + E:] = TOPK * N + np.arange(CH)[:, None]
    c["padrows"] = pad
    c["tiles"] = np.arange(NT, dtype=np.float32)[None]
    bf = mybir.dt.np(BF16)
    c["before"] = np.triu(np.ones((128, 128), np.float32), 1).astype(bf)
    c["ones"] = np.ones((128, 128), np.float32).astype(bf)
    c["sums"] = sums.reshape(KR, 2 * PR).astype(bf)
    c["qrows"], c["arows"], c["krows"] = (x.reshape(KR - KP, H * CH).astype(bf) for x in (qrows, arows, krows))
    c["valid"] = valid.reshape(NC, H * CH).astype(bf)
    c["identb"] = np.eye(128, dtype=np.float32).astype(bf)
    return c


def build(nc, ins, con, out, dbg=None):
    with ExitStack() as ctx:
        sb = lambda n, s, d=F32: ctx.enter_context(nc.sbuf_tensor(n, s, d))
        sem = lambda n: ctx.enter_context(nc.semaphore(n))
        dram = lambda n, s, d=F32: nc.dram_tensor(n, s, d).ap()

        qa_parts = dram("qa_parts", (3, HD, 2, H, N), BF16)
        k_parts = dram("k_parts", (3, HD, H, WINDOW + N), BF16)

        routed = dram("routed", (E * REGION + CH, ROW))
        results = dram("results", (RESULTS, D))
        ident = sb("ident", [128, 128])
        identb = sb("identb", [128, 128], BF16)
        sums = sb("sums", [KR, 2, PR], BF16)
        blockdiag = sb("blockdiag", [D, D])
        statemask = sb("statemask", [PR, 4 * UD])
        keep = sb("keep", [128, NC + 1])
        norm_w = sb("norm_w", [D, 1])
        wq = sb("wq", [D, D])
        wqT = sb("wqT", [D, D])
        wkv = sb("wkv", [D, 2, D])
        wout = sb("wout", [D, 2, D])
        wfeat = sb("wfeat", [16, 2, D])
        mblk = sb("mblk", [D, D])
        wa = sb("wa", [D, D])
        minus_half = sb("minus_half", [128, NC])
        x_all = sb("x_all", [CH, NC, D])
        stats = sb("stats", [CH, NC, 6])
        mv = sb("mv", [CH, NC, 2])
        vareps = sb("vareps", [CH, 2, NC])
        rstd = sb("rstd", [CH, NC])
        rboth = sb("rboth", [CH, NC])
        h_tok = sb("h_tok", [CH, GC, D])
        hT = sb("hT", [D, WINDOW + N])
        kv_tok = sb("kv_tok", [CH, NC + 1, 3, D])
        rest = sb("rest", [D, 3, GT])
        w12_ = sb("w12", [D, E * 2 * F])
        wgl_ = sb("wgl", [128, E * 2 * 2 * F])
        qa = wgl_[:, 0:3 * N].bitcast(BF16).rearrange("p (a s t) -> p a s t", a=2, s=3)
        kp = w12_[:, 0:3 * (WINDOW + N) // 2].bitcast(BF16).rearrange("p (s t) -> p s t", s=3)
        qas_ = sb("qas", [128, 2, 2, H, CH], BF16)
        ks_ = sb("ks", [128, 2, 2, H, CH], BF16)
        qas, qs, as_, ks = qas_[0:KR], qas_[0:KR, :, 0], qas_[0:KR, :, 1], ks_[0:KR]
        u_tok = sb("u_tok", [CH, H, UD])
        usum = sb("usum", [CH, H])
        ut = sb("ut", [CH, H, UD])
        phik = sb("phik", [CH, 2, H, FS])
        v1 = sb("v1", [CH, 2, 2, H, 32])
        state = sb("state", [PR, H, 32])
        sadd = sb("sadd", [PR, 4, UD])
        mrow = sb("mrow", [128, 4])
        mneg = sb("mneg", [128, 2, 4], BF16)
        phiq = sb("phiq", [PR, 2, 2, CH])
        amat = sb("amat", [CH, 2, 4, CH])
        pmat = sb("pmat", [CH, 2, 8, WINDOW])
        linT = sb("linT", [128, 2, 4, CH])
        winT = sb("winT", [128, 2, 4, CH])
        zrec = sb("zrec", [CH, H])
        att = sb("att", [CH, 2, H, HD])
        catT = sb("catT", [D, 3, CH])
        xh = sb("xh", [CH, D])
        st2 = sb("st2", [CH, 6])
        mv2 = sb("mv2", [CH, 2])
        ve2 = sb("ve2", [CH, 1])
        rstd2 = sb("rstd2", [CH, 1])
        h2 = sb("h2", [CH, 2, D])
        wgate = sb("wgate", [D, E])
        bgate = sb("bgate", [128, E])
        iota8 = sb("iota8", [128, E])
        tokid = sb("tokid", [CH, NC])
        before = sb("before", [128, 128], BF16)
        ones = sb("ones", [128, 128], BF16)
        count = sb("count", [128, E])
        region0 = sb("region0", [128, E])
        logit = sb("logit", [CH, E])
        top = sb("top", [CH, 8])
        topi = sb("topi", [CH, 8], mybir.dt.uint32)
        topf = sb("topf", [CH, 2])
        onehot = sb("onehot", [CH, 2, E])
        member = sb("member", [CH, E], BF16)
        gap = sb("gap", [CH, 1])
        egap = sb("egap", [CH, 1])
        wsum = sb("wsum", [CH, 1])
        w01 = sb("w01", [CH, 2])
        tmp8 = sb("tmp8", [CH, 2, E])
        place = sb("place", [CH, E])
        placed = sb("placed", [CH, 2, E])
        slotf = sb("slotf", [CH, 2])
        slot = sb("slot", [CH, 2, 2], mybir.dt.uint32)
        routed_row = sb("routed_row", [CH, 2, ROW])
        padrows = sb("padrows", [CH, ROW])
        tiles = sb("tiles", [1, NT])
        table = sb("table", [1, 2, NT], mybir.dt.int32)
        counts_i = sb("counts_i", [1, E], mybir.dt.int32)
        ntile_i = sb("ntile_i", [1, E], mybir.dt.int32)
        ntile = sb("ntile", [1, E])
        ends = sb("ends", [1, E])
        tmpt = sb("tmpt", [1, 4, NT])
        cmp8 = sb("cmp8", [1, 2, NT, E])
        tail_i = sb("tail_i", [1, E], mybir.dt.int32)
        w12 = w12_[:].rearrange("p (e f) -> p e f", e=E)
        wgl = wgl_[:].rearrange("p (e k f) -> p e k f", e=E, k=2)
        b12 = sb("b12", [128, E, 2 * F])
        b3 = sb("b3", [128, E, D])
        late0 = kv_tok[:].rearrange("p c w d -> p (c w d)")
        bgl = late0[:, 0:E * 2 * F].rearrange("p (e f) -> p e f", e=E)
        w3 = late0[:, E * 2 * F:E * 2 * F + E * 2 * D].rearrange("p (e k d) -> p e k d", e=E, k=2)
        x12, glb = (hT[:, o:o + 1024].rearrange("p (a f) -> p a f", a=2) for o in (0, 1024))
        late2 = qas_[:].rearrange("p a w h t -> p (a w h t)").bitcast(F32)
        z = late2[:, 0:512].rearrange("p (a f) -> p a f", a=2)
        og = late2[:, 512:1024].rearrange("p (a f) -> p a f", a=2)
        oT = late2[:, 1024:1536].rearrange("p (a k t) -> p a k t", a=2, k=2)
        sg = late2[:, 1536:2048].rearrange("p (a f) -> p a f", a=2)
        yw = late2[:, 2048:2560].rearrange("p (a d) -> p a d", a=4)
        late3 = rest[:].rearrange("p c t -> p (c t)")
        zxT = late3[:, 0:768].rearrange("p (a k t) -> p a k t", a=2, k=3)
        yb = late3[:, 768:1024].rearrange("p (a d) -> p a d", a=2)
        xin = sb("xin", [CH, 4, ROW])
        mweight = sb("mweight", [CH, 4])
        mrowf = sb("mrowf", [CH, 4])
        mrowid = sb("mrowid", [CH, 4], mybir.dt.uint32)
        res = [ks_[:].rearrange("p a w h t -> p (a w h t)").bitcast(F32)[:, 2048 * k:2048 * (k + 1)].rearrange("p (c d) -> p c d", c=NC) for k in range(2)]

        ps = ctx.enter_context(nc.psum_tensor("ps", [128, 8, 512], F32))
        SQ, ST, A, OUT0, OUT1, PHI, KV, TR = range(8)

        w_in, c_in, s_in = sem("w_in"), sem("c_in"), sem("s_in")
        x_in = [sem(f"x_in{g}") for g in range(NG)]
        zeroed = sem("zeroed")
        wstep, wstep_c = sem("wstep"), sem("wstep_c")
        mv_ready, ve_ready, pow_ready, rb_ready, h_ready = (sem(n) for n in ("mv_ready", "ve_ready", "pow_ready", "rb_ready", "h_ready"))
        hps_ready, hT_ready = sem("hps_ready"), sem("hT_ready")
        proj_ready, part0, rest1, part1, part2 = (sem(n) for n in ("proj_ready", "part0", "rest1", "part1", "part2"))
        kv_proj, kv_copied = sem("kv_proj"), sem("kv_copied")
        parts_out = [sem(f"parts_out{g}") for g in range(NG)]
        stack_in = [sem("stack_in0"), sem("stack_in1")]
        sq_ready, max_done, nh_done, mneg_ready = sem("sq_ready"), sem("max_done"), sem("nh_done"), sem("mneg_ready")
        a_ready, square_done, amask_ready = sem("a_ready"), sem("square_done"), sem("amask_ready")
        phi_ready, phisq_done, inter_done = sem("phi_ready"), sem("phisq_done"), sem("inter_done")
        us, ut_done, phik_ready, kv_ready, sadd_done, state_done = (sem(n) for n in ("us", "ut_done", "phik_ready", "kv_ready", "sadd_done", "state_done"))
        st_ready, exp_done, out_ready, evac_done = sem("st_ready"), sem("exp_done"), sem("out_ready"), sem("evac_done")
        t_lin, t_win, t_cat, cat_copied, wout_ready = (sem(n) for n in ("t_lin", "t_win", "t_cat", "cat_copied", "wout_ready"))
        z1, z2, norm_lin, norm_win = sem("z1"), sem("z2"), sem("norm_lin"), sem("norm_win")
        xh0, xh_ready, x1_ready, st2_done, mv2_ready, ve2_ready, rstd2_ready, h2_ready = (
            sem(n) for n in ("xh0", "xh_ready", "x1_ready", "st2_done", "mv2_ready", "ve2_ready", "rstd2_ready", "h2_ready"))
        done = sem("done")
        settled = sem("settled")
        xin_ready = [sem(f"xin_ready{k}") for k in range(4)]
        y_out = [sem(f"y_out{k}") for k in range(4)]
        (r_logit, r_top, r_idx, r_idxf, r_oh, r_member, r_gap, r_egap, r_ws, r_w, r_w2, r_tmp, r_row, r_place, r_placed, r_slotf, r_slot,
         r_count, pos_ready, staged, scattered) = tuple(sem(n) for n in (
             "r_logit", "r_top", "r_idx", "r_idxf", "r_oh", "r_member", "r_gap", "r_egap", "r_ws", "r_w", "r_w2", "r_tmp", "r_row", "r_place",
             "r_placed", "r_slotf", "r_slot", "r_count", "pos_ready", "staged")) + ([sem("scattered0"), sem("scattered1")],)
        tab, table_ready, padded = sem("tab"), sem("table_ready"), sem("padded")
        e_in, b_in = sem("e_in"), sem("b_in")
        (tzx_ready, zx_copied, x12_ready, x12_added, z_ready, meta_copied, meta_ready, gl_ready, g_added, l_added, silu_done, o_ready, to_ready,
         oT_copied, y_ready, y_added, y_weighted) = (sem(n) for n in (
             "tzx_ready", "zx_copied", "x12_ready", "x12_added", "z_ready", "meta_copied", "meta_ready", "gl_ready", "g_added", "l_added",
             "silu_done", "o_ready", "to_ready", "oT_copied", "y_ready", "y_added", "y_weighted"))
        res_in = [sem(f"res_in{g}") for g in range(NG)]
        res_sum, out_sum = sem("res_sum"), sem("out_sum")

        TZX, X12, Y, TO, GL = SQ, ST, A, PHI, OUT0

        def settle(engine):
            engine.wait_ge(settled, 1)

        def computed(engine, value):
            if not isinstance(value, int):
                value = engine.snap(engine.to_reg(value))
            settle(engine)
            return value

        def run_steps(engine, step):
            def turns(i, k):
                return lambda d: i + (k + d) // 4

            for j in range(-2, 4):
                step(j, j % 4, turns(j // 4, j % 4))
            with engine.Fori(1, NT // 4 - 1) as i:
                for k in range(4):
                    step(i * 4 + k, k, turns(i, k))
            for j in range(NT - 4, NT + 2):
                step(j, j % 4, turns(j // 4, j % 4))

        x_dram = ins["x"].rearrange("b (c p) d -> p (b c) d", p=CH)
        N_W, N_C = 9, 16
        WRITES = 9
        STACKS = 16 * 3 * len(RUNS)
        split = lambda n: ins[n].rearrange("(a e) f -> a e f", a=1).to_broadcast([128, E, ins[n].shape[1]])

        def part_of(g, t, part):
            if t == 1:
                return kp[:, part, bass.ds(g * GT + WINDOW, GT)]
            return qa[:, t // 2, part, bass.ds(g * GT, GT)]

        block = ctx.enter_context(nc.Block())

        @block.sync
        def _(sp):
            for g in range(NG):
                sp.dma_start(x_all[:, g * GC:(g + 1) * GC], x_dram[:, g * GC:(g + 1) * GC]).then_inc(x_in[g], 16)
            for dst, name in ((identb, "identb"), (sums, "sums"), (statemask, "statemask"), (keep, "keep"), (iota8, "iota8"),
                              (region0, "region0"), (tokid, "tokid"), (before, "before"), (ones, "ones"), (padrows, "padrows"),
                              (tiles, "tiles"), (count, "region0")):
                sp.dma_start(dst[:].rearrange("r a f -> r (a f)") if name == "sums" else dst[:], con[name]).then_inc(c_in, 16)
            sp.dma_start(wout[:, 0, :], ins["Wout"][0:D, :]).then_inc(c_in, 16)
            sp.dma_start(wout[:, 1, :], ins["Wout"][D:2 * D, :]).then_inc(c_in, 16)
            sp.dma_start(wgate[:], ins["Wgate"]).then_inc(c_in, 16)
            sp.dma_start(bgate[:], ins["bgate"].rearrange("(a e) -> a e", a=1).to_broadcast([128, E])).then_inc(c_in, 16)
            for p in range(2):
                sp.dma_start(qs[KP:KR, p], con["qrows"]).then_inc(s_in, 16)
                sp.dma_start(as_[KP:KR, p], con["arows"]).then_inc(s_in, 16)
                for w in range(2):
                    sp.dma_start(ks[KP:KR, p, w], con["krows"]).then_inc(s_in, 16)

            def write_parts(g):
                sp.wait_ge(part2, 3 * (g + 1))
                for p in range(3):
                    for t in range(2):
                        sp.dma_start(qa_parts[p, :, t, :, g * GT:(g + 1) * GT].rearrange("d h t -> h d t"),
                                     qa[:, t, p, g * GT:(g + 1) * GT]).then_inc(parts_out[g], 16)
                    lo = WINDOW + g * GT if g else 0
                    sp.dma_start(k_parts[2 - p, :, :, lo:WINDOW + (g + 1) * GT].rearrange("d h t -> h d t"),
                                 kp[:, p, lo:WINDOW + (g + 1) * GT]).then_inc(parts_out[g], 16)

            def load_stack(c, p, i):
                if not isinstance(c, int) or c >= 2:
                    sp.wait_ge(out_ready, UNITS * (2 * i + p - 1))
                for s, qp, kpp, n in RUNS:
                    rows = slice(HD * s, HD * (s + n))
                    sp.dma_start(qas[rows, p].rearrange("r a h t -> r (a h) t"),
                                 qa_parts[qp:qp + n, :, :, :, bass.ds(c * CH, CH)].rearrange("s d a h t -> (s d) (a h) t")).then_inc(stack_in[p], 16)
                    for w in range(2):
                        sp.dma_start(ks[rows, p, w],
                                     k_parts[kpp:kpp + n, :, :, bass.ds(c * CH + w * WINDOW, CH)].rearrange("s d h t -> (s d) h t")).then_inc(stack_in[p], 16)
                if p == 0:
                    sp.dma_start(ks[ROW_VALID:ROW_VALID + 1, p, 0], con["valid"][bass.ds(c, 1)]).then_inc(stack_in[p], 16)

            write_parts(0)
            sp.wait_ge(parts_out[0], 16 * WRITES)
            sp.wait_ge(s_in, 16 * 8)
            load_stack(0, 0, 0)
            load_stack(1, 1, 0)
            for g in range(1, NG):
                write_parts(g)
            for g in range(1, NG):
                sp.wait_ge(parts_out[g], 16 * WRITES)
            for c in range(2, 4):
                load_stack(c, c % 2, c // 2)
            sp.dma_start(b12[:, :, 0:F], split("b1")).then_inc(b_in, 16)
            sp.dma_start(b12[:, :, F:], split("b2")).then_inc(b_in, 16)
            sp.dma_start(b3[:], split("b3")).then_inc(b_in, 16)
            with sp.Fori(2, NC // 2) as i:
                for p in range(2):
                    load_stack(i * 2 + p, p, i)
            sp.wait_ge(phik_ready, NC + 1)
            sp.dma_start(bgl[:, :, 0:F], split("bg")).then_inc(b_in, 16)
            sp.dma_start(bgl[:, :, F:], split("bl")).then_inc(b_in, 16)
            for k in range(2):
                sp.dma_start(w3[:, :, k, :], ins["W3"][:, k * 128:(k + 1) * 128, :].rearrange("e d f -> d e f")).then_inc(b_in, 16)
            sp.dma_start(routed[E * REGION:E * REGION + CH, :], padrows[:]).then_inc(padded, 16)
            sp.wait_ge(table_ready, 1)
            for e in range(E):
                row = sp.value_load(tail_i[0:1, e:e + 1], min_val=0, max_val=E * REGION - CH)
                sp.dma_start(routed[bass.ds(row, CH), :], padrows[:]).then_inc(padded, 16)
            sp.wait_ge(padded, 16 * (E + 1))
            for p in range(2):
                sp.wait_ge(scattered[p], 16 * NC)

            def load_tile(j, k):
                if not isinstance(j, int) or j >= 4:
                    sp.wait_ge(tzx_ready, computed(sp, j - 1))
                    sp.wait_ge(meta_copied, computed(sp, j - 3))
                row = sp.value_load(table[0:1, 1, bass.ds(j, 1)], min_val=0, max_val=E * REGION)
                sp.dma_start(xin[:, k, :], routed[bass.ds(row, CH), :]).then_inc(xin_ready[k], 16)

            for j in range(4):
                load_tile(j, j)
            with sp.Fori(1, NT // 4) as i:
                for k in range(4):
                    load_tile(i * 4 + k, k)
            for k in range(4):
                sp.wait_ge(y_out[k], 16 * (NT // 4))
            for g in range(NG):
                for k in range(2):
                    lo = k * N + g * GT
                    sp.dma_start(res[k][:, g * GC:(g + 1) * GC], results[lo:lo + GT, :].rearrange("(c p) d -> p c d", p=CH)).then_inc(res_in[g], 16)
            for g in range(NG):
                sp.wait_ge(out_sum, g + 1)
                sp.dma_start(out.rearrange("b (c p) d -> p (b c) d", p=CH)[:, g * GC:(g + 1) * GC], x_all[:, g * GC:(g + 1) * GC]).then_inc(done, 16)
            sp.wait_ge(done, 16 * NG)

        @block.tensor
        def _(pe):
            mm = nc.tensor.matmul
            pe.wait_ge(w_in, 16 * N_W)
            mm(ps[:, TR, 0:D], wfeat[:, 0, :], wfeat[:, 1, :], start=True, stop=True).then_inc(wstep, 1)
            pe.wait_ge(wstep_c, 1)
            mm(ps[:, A, 0:D], wqT[:], mblk[:], start=True, stop=True).then_inc(wstep, 1)

            def transposes(g):
                pe.wait_ge(h_ready, g + 1)
                if not isinstance(g, int) or g:
                    pe.wait_ge(hT_ready, g)
                for cc in range(GC):
                    t = nc.tensor.transpose(ps[:, TR, cc * CH:(cc + 1) * CH], h_tok[:, cc, :], ident[:])
                t.then_inc(hps_ready, 1)

            def group(g, last):
                pe.wait_ge(hT_ready, g + 1)
                pe.wait_ge(wstep_c, 2)
                for t, w in enumerate((wq[:], wkv[:, 0, :], wa[:])):
                    if not isinstance(g, int) or g:
                        pe.wait_ge(rest1, 3 * (g - 1) + t + 1)
                    mm(ps[:, SQ + t, :], w, hT[:, bass.ds(g * GT + WINDOW, GT)], start=True, stop=True).then_inc(proj_ready, 1)
                if not last:
                    transposes(g + 1)
                for cc in range(GC):
                    bank, lo = OUT0 + cc % 2, g * GT + cc * CH
                    if not isinstance(g, int) or g or cc > 1:
                        pe.wait_ge(kv_copied, GC * g + cc - 1)
                    mm(ps[:, bank, 0:2 * D], hT[:, lo + WINDOW:lo + WINDOW + CH], wkv[:].rearrange("p a d -> p (a d)"),
                       start=True, stop=True)
                    mm(ps[:, bank, 2 * D:3 * D], hT[:, lo:lo + CH], wkv[:, 1, :],
                       start=True, stop=True).then_inc(kv_proj, 1)

            transposes(0)
            for g in range(NG):
                group(g, g == NG - 1)
            pe.wait_ge(kv_copied, NC)
            pe.wait_ge(rest1, 3 * NG)
            pe.wait_ge(c_in, 16 * N_C)

            def post(c, u, p):
                static = isinstance(c, int)
                has = [not static or 0 <= c - k < NC for k in range(4)]
                if u == 0 and has[1]:
                    pe.wait_ge(evac_done, UNITS * c)
                    if not static or c > 1:
                        pe.wait_ge(x1_ready, c - 1)
                    if not static or c > 2:
                        pe.wait_ge(r_logit, c - 2)
                    for s in range(4):
                        t = nc.tensor.transpose(ps[:, TR, s * CH:(s + 1) * CH], linT[:, 1 - p, s, :], ident[:])
                    t.then_inc(t_lin, 1)
                if u == 1 and has[1]:
                    pe.wait_ge(norm_lin, c)
                    for s in range(4):
                        t = nc.tensor.transpose(ps[:, TR, s * CH:(s + 1) * CH], winT[:, 1 - p, s, :], ident[:])
                    t.then_inc(t_win, 1)
                if u == 2:
                    if has[1]:
                        pe.wait_ge(norm_win, c)
                    else:
                        pe.wait_ge(x1_ready, NC)
                        pe.wait_ge(r_logit, c - 2)
                    if has[3]:
                        pe.wait_ge(r_member, c - 2)
                        mm(ps[:, TR, 384:384 + E], before[:], member[:], start=True, stop=True)
                        mm(ps[:, TR, 392:392 + E], ones[:], member[:], start=True, stop=True).then_inc(pos_ready, 1)
                    if has[1]:
                        for s in range(2):
                            t = nc.tensor.transpose(ps[:, TR, s * CH:(s + 1) * CH], att[:, s].rearrange("p h d -> p (h d)"), ident[:])
                    if has[2]:
                        pe.wait_ge(h2_ready, c - 1)
                        t = nc.tensor.transpose(ps[:, TR, 2 * CH:3 * CH], h2[:, p, :], ident[:])
                    if has[1] or has[2]:
                        t.then_inc(t_cat, 1)
                if u == 3 and (has[1] or has[2]):
                    pe.wait_ge(cat_copied, c)
                    if has[3]:
                        pe.wait_ge(r_count, c - 2)
                    if has[1]:
                        mm(ps[:, TR, 384:384 + D], catT[:, 0, :], wout[:, 0, :], start=True, stop=False)
                        t = mm(ps[:, TR, 384:384 + D], catT[:, 1, :], wout[:, 1, :], start=False, stop=True)
                    if has[2]:
                        t = mm(ps[:, TR, 0:E], catT[:, 2, :], wgate[:], start=True, stop=True)
                    t.then_inc(wout_ready, 1)

            def chunk(c, p, i):
                first = isinstance(c, int) and c == 0
                pe.wait_ge(stack_in[p], (STACKS + 16 * (1 - p)) * (i + 1))
                for u in range(UNITS):
                    n = c * UNITS + u
                    j, hf = u // 2, u % 2
                    early = isinstance(n, int)
                    if not early or n:
                        pe.wait_ge(max_done, n)
                    for hh in range(8):
                        h = 8 * hf + hh
                        r = WINDOW * (hh % 2)
                        t = mm(ps[r:r + WINDOW, SQ, (hh // 2) * CH:(hh // 2 + 1) * CH], qs[:, p, h, j * WINDOW:(j + 1) * WINDOW],
                               ks[:, p, j, h, :], start=True, stop=True)
                    t.then_inc(sq_ready, 1)
                    if not early or n:
                        pe.wait_ge(square_done, n)
                    for g in range(4):
                        t = mm(ps[:, A, g * CH:(g + 1) * CH], ks[:, p, 1, 4 * u + g, :], as_[:, p, 4 * u + g, :], start=True, stop=True)
                    t.then_inc(a_ready, 1)
                    if not early or n:
                        pe.wait_ge(phisq_done, n)
                    for k in range(2):
                        for par in range(2):
                            t = mm(ps[0:PR, PHI, k * CH:(k + 1) * CH], sums[:, par, :], as_[:, p, 4 * u + 2 * k + par, :],
                                   start=par == 0, stop=par == 1)
                    t.then_inc(phi_ready, 1)
                    pe.wait_ge(phik_ready, c + 1)
                    if not early or n:
                        pe.wait_ge(sadd_done, n)
                    for k in range(2):
                        hp = 2 * (2 * u + k)
                        t = mm(ps[0:PR, KV, k * 2 * UD:(k + 1) * 2 * UD], phik[:, p, hp:hp + 2, :].rearrange("p h f -> p (h f)"),
                               v1[:, p, 1, hp:hp + 2, 0:UD], start=True, stop=True)
                    t.then_inc(kv_ready, 1)
                    if not first:
                        post(c, u, p)
                    pe.wait_ge(mneg_ready, n + 1)
                    if not early or n:
                        pe.wait_ge(exp_done, n)
                    for hh in range(8):
                        h = 8 * hf + hh
                        mm(ps[:, ST, hh * WINDOW:(hh + 1) * WINDOW], ks[:, p, j, h, :], qs[:, p, h, j * WINDOW:(j + 1) * WINDOW],
                           start=(hh == 0), stop=False, skip_group_check=True)
                    for pr in range(4):
                        for part in range(2):
                            t = mm(ps[:, ST, pr * CH:(pr + 1) * CH], mneg[:, part, pr:pr + 1].to_broadcast([128, 128]), identb[:],
                                   start=False, stop=(part == 1), skip_group_check=True)
                    t.then_inc(st_ready, 1)
                    bank = OUT0 + u % 2
                    pe.wait_ge(phisq_done, n + 1)
                    if not early or n > 1:
                        pe.wait_ge(evac_done, n - 1)
                    if not early or n > 3:
                        pe.wait_ge(state_done, n - 3)
                    for k in range(2):
                        t = mm(ps[64 * k:64 * k + 64, bank, 0:CH], state[:, 2 * (2 * u + k):2 * (2 * u + k) + 2, :].rearrange("p h f -> p (h f)"),
                               phiq[:, u % 2, k, :], start=True, stop=False, skip_group_check=True)
                    t.then_inc(inter_done, 1)
                    pe.wait_ge(amask_ready, n + 1)
                    for g in range(4):
                        mm(ps[32 * g:32 * g + 32, bank, 0:CH], v1[:, p, 1, 4 * u + g, :], amat[:, u % 2, g, :],
                           start=False, stop=True, skip_group_check=True)
                    pe.wait_ge(exp_done, n + 1)
                    for hh in range(8):
                        g, s = hh % 4, hh // 4
                        t = mm(ps[32 * g:32 * g + 32, bank, CH + s * WINDOW:CH + (s + 1) * WINDOW], v1[:, p, j, 8 * hf + hh, :],
                               pmat[:, u % 2, hh, :], start=True, stop=True, skip_group_check=True)
                    t.then_inc(out_ready, 1)

            for c in range(4):
                chunk(c, c % 2, c // 2)
            with pe.Fori(2, NC // 2) as i:
                for p in range(2):
                    chunk(i * 2 + p, p, i)
            for c in range(NC, NC + 3):
                for u in range(UNITS):
                    post(c, u, c % 2)

            pe.wait_ge(x1_ready, NC)
            pe.wait_ge(r_count, NC)
            pe.wait_ge(table_ready, 1)
            pe.wait_ge(e_in, 16 * 6)
            pe.wait_ge(b_in, 16 * 7)

            def expert(j):
                return pe.value_load(table[0:1, 0, bass.ds(j, 1)], min_val=0, max_val=E - 1)

            def rhs(ap):
                return ap.rearrange("p a f -> p (a f)")

            def step(j, k, turn):
                static = isinstance(j, int)
                on = lambda d: not static or 0 <= j + d < NT
                if (on(0) or on(2)) and not (static and j == -2):
                    pe.wait_ge(zx_copied, j + 2)
                if on(0):
                    pe.wait_ge(z_ready, j + 1)
                    for s in range(2):
                        t = nc.tensor.transpose(ps[:, TZX, s * CH:(s + 1) * CH], z[:, k % 2, s * CH:(s + 1) * CH], ident[:])
                if on(2):
                    pe.wait_ge(xin_ready[(k + 2) % 4], 16 * (turn(2) + 1))
                    t = nc.tensor.transpose(ps[:, TZX, 2 * CH:3 * CH], xin[:, (k + 2) % 4, 0:D], ident[:])
                if on(0) or on(2):
                    t.then_inc(tzx_ready, 1)
                if on(1):
                    pe.wait_ge(zx_copied, computed(pe, j + 2))
                    if not static or j >= 0:
                        pe.wait_ge(x12_added, computed(pe, j + 1))
                    mm(ps[:, X12, :], zxT[:, (k + 1) % 2, 2, :], rhs(w12[:, bass.ds(expert(j + 1), 1), :]), start=True, stop=True).then_inc(x12_ready, 1)
                if on(-2):
                    pe.wait_ge(oT_copied, computed(pe, j - 1))
                    if not static or j > 2:
                        pe.wait_ge(y_added, computed(pe, j - 2))
                    e = expert(j - 2)
                    for s in range(2):
                        t = mm(ps[:, Y, 0:D], oT[:, k % 2, s, :], rhs(w3[:, bass.ds(e, 1), s, :]), start=(s == 0), stop=(s == 1))
                    t.then_inc(y_ready, 1)
                if on(-1):
                    pe.wait_ge(o_ready, j)
                    if not static or j > 1:
                        pe.wait_ge(oT_copied, j - 1)
                    for s in range(2):
                        t = nc.tensor.transpose(ps[:, TO, s * CH:(s + 1) * CH], og[:, (k + 1) % 2, s * CH:(s + 1) * CH], ident[:])
                    t.then_inc(to_ready, 1)
                if on(0):
                    pe.wait_ge(zx_copied, computed(pe, j + 3))
                    if not static or j > 0:
                        pe.wait_ge(l_added, computed(pe, j))
                    e = expert(j)
                    for s in range(2):
                        t = mm(ps[:, GL, :], zxT[:, k % 2, s, :], rhs(wgl[:, bass.ds(e, 1), s, :]), start=(s == 0), stop=(s == 1))
                    t.then_inc(gl_ready, 1)

            run_steps(pe, step)

        @block.scalar
        def _(act):
            a_ = nc.scalar.activation
            for dst, src in ((wfeat[:, 0, :], ins["WqfT"]), (wfeat[:, 1, :], ins["WkfT"]), (blockdiag[:], con["blockdiag"]), (wqT[:], ins["WqT"]),
                             (ident[:], con["ident"]), (norm_w[:], ins["norm_w"].rearrange("(d a) -> d a", a=1)), (wq[:], ins["Wq"]),
                             (wkv[:, 0, :], ins["Wk"]), (wkv[:, 1, :], ins["Wv"])):
                act.dma_start(dst, src).then_inc(w_in, 16)
            act.wait_ge(w_in, 16 * N_W)
            act.wait_ge(wstep, 2)
            nc.scalar.mul(wa[:], ps[:, A, 0:D], 0.5).then_inc(wstep_c, 1)

            def group(g):
                act.wait_ge(hps_ready, g + 1)
                a_(hT[:, bass.ds(g * GT + WINDOW, GT)], ps[:, TR, :], ACT.Copy, scale=norm_w[:, 0:1]).then_inc(hT_ready, 1)
                for t in range(3):
                    act.wait_ge(proj_ready, 3 * g + t + 1)
                    a_(part_of(g, t, 0), ps[:, SQ + t, :], ACT.Copy, scale=float(HD) ** -0.5 if t == 0 else 1.0).then_inc(part0, 1)
                for t in range(3):
                    act.wait_ge(rest1, 3 * g + t + 1)
                    nc.scalar.copy(part_of(g, t, 1), rest[:, t, :]).then_inc(part1, 1)
                for cc in range(GC):
                    act.wait_ge(kv_proj, g * GC + cc + 1)
                    nc.scalar.copy(kv_tok[:, bass.ds(g * GC + cc, 1)].rearrange("p a w d -> p (a w d)"),
                                   ps[:, OUT0 + cc % 2, 0:3 * D]).then_inc(kv_copied, 1)

            group(0)
            with act.Fori(1, NG) as g:
                group(g)

            def post(c, u):
                static = isinstance(c, int)
                has = [not static or 0 <= c - k < NC for k in range(4)]
                if u == 0 and has[3]:
                    act.wait_ge(r_gap, c - 2)
                    a_(egap[:], gap[:], ACT.Exp).then_inc(r_egap, 1)
                if u == 2 and (has[1] or has[2]):
                    lo, hi = (0 if has[1] else 2), (3 if has[2] else 2)
                    act.wait_ge(t_cat, c)
                    nc.scalar.copy(catT[:, lo:hi].rearrange("p k t -> p (k t)"), ps[:, TR, lo * CH:hi * CH]).then_inc(cat_copied, 1)

            def chunk(c, p):
                for u in range(UNITS):
                    n = c * UNITS + u
                    early = isinstance(n, int)
                    j, hf = u // 2, u % 2
                    bank = OUT0 + u % 2
                    act.wait_ge(a_ready, n + 1)
                    if not early or n > 1:
                        act.wait_ge(out_ready, n - 1)
                    a_(amat[:, u % 2].rearrange("p g t -> p (g t)"), ps[:, A, :], ACT.Square).then_inc(square_done, 1)
                    act.wait_ge(phi_ready, n + 1)
                    a_(phiq[:, u % 2].rearrange("p k t -> p (k t)"), ps[0:PR, PHI, 0:2 * CH], ACT.Square).then_inc(phisq_done, 1)
                    if not (early and c == 0):
                        post(c, u)
                    act.wait_ge(st_ready, n + 1)
                    a_(pmat[:, u % 2].rearrange("p g t -> p (g t)"), ps[:, ST, :], ACT.Exp).then_inc(exp_done, 1)
                    act.wait_ge(out_ready, n + 1)
                    if u == 0 and (not early or n > 4):
                        act.wait_ge(t_win, c - 1)
                    nc.scalar.copy(linT[:, p, u, :], ps[:, bank, 0:CH])
                    nc.scalar.copy(winT[:, p, 2 * hf:2 * hf + 2, j * WINDOW:(j + 1) * WINDOW],
                                   ps[:, bank, CH:2 * CH].rearrange("p (s t) -> p s t", s=2)).then_inc(evac_done, 1)

            for c in range(4):
                chunk(c, c % 2)
            for g in range(NG):
                act.wait_ge(parts_out[g], 16 * WRITES)
            for dst, name in ((w12[:, :, 0:F], "W1"), (w12[:, :, F:], "W2")):
                act.dma_start(dst, ins[name].rearrange("e d f -> d e f")).then_inc(e_in, 16)
            for k in range(2):
                for lo, name in ((0, "Wg"), (F, "Wl")):
                    act.dma_start(wgl[:, :, k, lo:lo + F], ins[name][:, k * 128:(k + 1) * 128, :].rearrange("e d f -> d e f")).then_inc(e_in, 16)
            with act.Fori(2, NC // 2) as i:
                for p in range(2):
                    chunk(i * 2 + p, p)
            for c in range(NC, NC + 3):
                for u in range(UNITS):
                    post(c, u)

            def step(j, k, turn):
                static = isinstance(j, int)
                on = lambda d: not static or 0 <= j + d < NT
                if on(0) or on(2):
                    lo, hi = (0 if on(0) else 2), (3 if on(2) else 2)
                    act.wait_ge(tzx_ready, j + 3)
                    if not static or j > -1:
                        act.wait_ge(x12_ready, j + 1)
                    if not static or j > 1:
                        act.wait_ge(gl_ready, j - 1)
                    if on(0):
                        nc.scalar.copy(zxT[:, k % 2, 0:2, :], ps[:, TZX, 0:2 * CH].rearrange("p (k t) -> p k t", k=2))
                    if on(2):
                        t = nc.scalar.copy(zxT[:, k % 2, 2, :], ps[:, TZX, 2 * CH:3 * CH])
                        t.then_inc(zx_copied, 1)
                    else:
                        nc.scalar.copy(zxT[:, k % 2, 2, 0:1], ident[:, 0:1]).then_inc(zx_copied, 1)
                if on(-1):
                    act.wait_ge(g_added, j)
                    if not static or j > 2:
                        act.wait_ge(o_ready, j - 2)
                    a_(sg[:, (k + 1) % 2, :], glb[:, (k + 1) % 2, 0:F], ACT.Silu).then_inc(silu_done, 1)
                    act.wait_ge(to_ready, j)
                    if not static or j > 2:
                        act.wait_ge(y_ready, j - 2)
                    nc.scalar.copy(oT[:, (k + 1) % 2].rearrange("p a t -> p (a t)"), ps[:, TO, 0:F]).then_inc(oT_copied, 1)
                if on(-2):
                    act.wait_ge(y_added, j - 1)
                    act.wait_ge(meta_copied, j - 1)
                    if not static or j >= 6:
                        act.wait_ge(y_out[(k + 2) % 4], 16 * turn(-2))
                    a_(yw[:, (k + 2) % 4, :], yb[:, k % 2, :], ACT.Copy, scale=mweight[:, (k + 2) % 4:(k + 2) % 4 + 1]).then_inc(y_weighted, 1)

            run_steps(act, step)

        @block.vector
        def _(dve):
            v = nc.vector
            v.memset(hT[:, 0:WINDOW], 0.0).then_inc(settled, 1)
            v.memset(minus_half[:], -0.5).then_inc(zeroed, 1)
            for c in range(NC):
                if c % GC == 0:
                    dve.wait_ge(x_in[c // GC], 16)
                v.bn_stats(stats[:, c, :], x_all[:, c, :]).then_inc(mv_ready, 1)
            for c in range(NC):
                if c % GC == 0:
                    dve.wait_ge(mv_ready, NC)
                v.bn_aggr(mv[:, c, :], stats[:, c, :]).then_inc(mv_ready, 1)
            dve.wait_ge(mv_ready, 2 * NC)
            var = mv[:, :, 1]
            v.tensor_scalar(vareps[:, 0, :], var, EPS_LN, None, ALU.add).then_inc(ve_ready, 1)
            v.memset(kp[:, :, 0:WINDOW], 0.0).then_inc(zeroed, 1)
            v.memset(v1[:], 0.0).then_inc(zeroed, 1)
            dve.wait_ge(pow_ready, 1)
            v.tensor_tensor(rboth[:], rstd[:], rstd[:], ALU.mult).then_inc(rb_ready, 1)
            dve.wait_ge(rb_ready, 1)
            v.tensor_tensor(rboth[:], rboth[:], var, ALU.mult).then_inc(rb_ready, 1)
            dve.wait_ge(rb_ready, 2)
            v.tensor_scalar(vareps[:, 1, :], rboth[:], EPS_RMS, None, ALU.add).then_inc(ve_ready, 1)
            dve.wait_ge(w_in, 16 * N_W)
            dve.wait_ge(wstep, 1)
            v.tensor_tensor(mblk[:], ps[:, TR, 0:D], blockdiag[:], ALU.mult).then_inc(wstep_c, 1)
            dve.wait_ge(pow_ready, 2)
            v.tensor_tensor(rboth[:], vareps[:, 1, :], rstd[:], ALU.mult).then_inc(rb_ready, 1)
            dve.wait_ge(rb_ready, 3)

            def rows(g):
                if not isinstance(g, int) or g:
                    dve.wait_ge(hps_ready, g)
                for cc in range(GC):
                    at = bass.ds(g * GC + cc, 1)
                    t = v.tensor_scalar(h_tok[:, cc, :], x_all[:, at, :].rearrange("p a d -> p (a d)"),
                                        mv[:, at, 0:1].rearrange("p a d -> p (a d)"), rboth[:, at], ALU.subtract, ALU.mult)
                t.then_inc(h_ready, 1)

            def group(g, last):
                if not last:
                    rows(g + 1)
                for t in range(3):
                    dve.wait_ge(part0, 3 * g + t + 1)
                    if t == 0 and (not isinstance(g, int) or g):
                        dve.wait_ge(part2, 3 * g)
                    v.scalar_tensor_tensor(out=rest[:, t, :], in0=ps[:, SQ + t, :], scalar=float(HD) ** -0.5 if t == 0 else 1.0,
                                           in1=part_of(g, t, 0), op0=ALU.mult, op1=ALU.subtract).then_inc(rest1, 1)
                for t in range(3):
                    dve.wait_ge(part1, 3 * g + t + 1)
                    v.tensor_tensor(part_of(g, t, 2), rest[:, t, :], part_of(g, t, 1), ALU.subtract).then_inc(part2, 1)

            rows(0)
            group(0, False)
            with dve.Fori(1, NG - 1) as g:
                group(g, False)
            group(NG - 1, True)
            v.memset(phik[:], 0.0).then_inc(zeroed, 1)
            v.memset(state[:], 0.0).then_inc(zeroed, 1)
            v.memset(u_tok[:, :, 0:1], 1.0).then_inc(zeroed, 1)
            v.memset(kv_tok[:, NC], 0.0).then_inc(zeroed, 1)
            dve.wait_ge(zeroed, 7)
            v.memset(v1[:, :, :, :, HD:HD + 1], 1.0).then_inc(zeroed, 1)
            dve.wait_ge(zeroed, 8)
            dve.wait_ge(c_in, 16 * N_C)

            def key_features(c, p):
                static = isinstance(c, int)
                if not static or c > 1:
                    dve.wait_ge(out_ready, UNITS * (c - 1))
                    dve.wait_ge(phik_ready, c)
                if static:
                    dve.wait_ge(kv_copied, NC)
                v.tensor_copy(v1[:, p, 1, :, 0:HD], kv_tok[:, bass.ds(c, 1), 1, :].rearrange("p a (h d) -> p (a h) d", h=H))
                v.tensor_copy(v1[:, p, 0, :, 0:HD], kv_tok[:, bass.ds(c, 1), 2, :].rearrange("p a (h d) -> p (a h) d", h=H))
                v.tensor_copy(u_tok[:, :, 1:UD], kv_tok[:, bass.ds(c, 1), 0, :].rearrange("p a (h d) -> p (a h) d", h=H)).then_inc(us, 1)
                dve.wait_ge(us, c * 2 + 1)
                v.tensor_reduce(usum[:], u_tok[:], AX.X, ALU.add).then_inc(us, 1)
                dve.wait_ge(us, c * 2 + 2)
                v.scalar_tensor_tensor(out=ut[:], in0=u_tok[:], scalar=2.0, in1=usum[:].to_broadcast([CH, H, UD]),
                                       op0=ALU.mult, op1=ALU.subtract).then_inc(ut_done, 1)
                at = UD
                for dl in range(1, UD):
                    w = UD - dl
                    v.tensor_tensor(phik[:, p, :, at:at + w], u_tok[:, :, 0:w], u_tok[:, :, dl:UD], ALU.mult)
                    at += w
                dve.wait_ge(ut_done, c + 1)
                v.tensor_tensor(phik[:, p, :, 0:UD], ut[:], u_tok[:], ALU.mult).then_inc(phik_ready, 1)

            def post(c, u, p, i):
                static = isinstance(c, int)
                has = [not static or 0 <= c - k < NC for k in range(4)]
                tr = ps[:, TR, :].rearrange("p (h f) -> p h f", f=32)
                z3 = zrec[:].rearrange("p (h a) -> p h a", a=1)
                if u == 0 and has[1]:
                    xc = x_all[:, bass.ds(c - 1, 1), :].rearrange("p a d -> p (a d)")
                    v.tensor_scalar(xh[:], xc, mv[:, bass.ds(c - 1, 1), 0:1].rearrange("p a d -> p (a d)"), rstd[:, bass.ds(c - 1, 1)],
                                    ALU.subtract, ALU.mult).then_inc(xh0, 1)
                    dve.wait_ge(xh0, c)
                    v.tensor_tensor(xh[:], xh[:], xc, ALU.add).then_inc(xh_ready, 1)
                    dve.wait_ge(t_lin, c)
                    v.tensor_scalar(z3, tr[:, :, HD:UD], EPS_LIN, None, ALU.add).then_inc(z1, 1)
                    dve.wait_ge(z1, c)
                    v.reciprocal(zrec[:], zrec[:]).then_inc(z2, 1)
                    dve.wait_ge(z2, c * 2 - 1)
                    if not static or c > 1:
                        dve.wait_ge(t_cat, c - 1)
                    v.tensor_tensor(att[:, 0], tr[:, :, 0:HD], zrec[:].to_broadcast([CH, H, HD]), ALU.mult).then_inc(norm_lin, 1)
                if u == 1 and has[1]:
                    dve.wait_ge(t_win, c)
                    dve.wait_ge(norm_lin, c)
                    v.reciprocal(z3, tr[:, :, HD:UD]).then_inc(z2, 1)
                    dve.wait_ge(z2, c * 2)
                    v.tensor_tensor(att[:, 1], tr[:, :, 0:HD], zrec[:].to_broadcast([CH, H, HD]), ALU.mult).then_inc(norm_win, 1)
                if u == 1 and has[3]:
                    n = c - 2
                    row = routed_row[:, 1 - p, :]
                    dve.wait_ge(r_egap, n)
                    v.tensor_scalar(wsum[:], egap[:], 1.0, None, ALU.add).then_inc(r_ws, 1)
                    dve.wait_ge(r_ws, n)
                    v.reciprocal(w01[:, 0:1], wsum[:]).then_inc(r_w, 1)
                    dve.wait_ge(r_w, n)
                    v.tensor_tensor(w01[:, 1:2], w01[:, 0:1], egap[:], ALU.mult).then_inc(r_w2, 1)
                    dve.wait_ge(r_w2, n)
                    if not static or c > 4:
                        dve.wait_ge(scattered[1 - p], 32 * (i - 2 + p))
                    v.tensor_scalar(tmp8[:, 0], onehot[:, 0], w01[:, 0:1], None, ALU.mult).then_inc(r_tmp, 1)
                    v.tensor_scalar(tmp8[:, 1], onehot[:, 1], float(N), None, ALU.mult).then_inc(r_tmp, 1)
                    dve.wait_ge(r_tmp, 2 * n)
                    v.scalar_tensor_tensor(out=row[:, D:D + E], in0=onehot[:, 1], scalar=w01[:, 1:2], in1=tmp8[:, 0], op0=ALU.mult, op1=ALU.add)
                    v.scalar_tensor_tensor(out=row[:, D + E:], in0=member[:], scalar=tokid[:, bass.ds(c - 3, 1)], in1=tmp8[:, 1],
                                           op0=ALU.mult, op1=ALU.add).then_inc(r_row, 1)
                if u == 2 and has[3]:
                    n = c - 2
                    dve.wait_ge(pos_ready, n)
                    if has[1] or has[2]:
                        dve.wait_ge(cat_copied, c)
                    v.tensor_tensor(place[:], ps[:, TR, 384:384 + E], count[:], ALU.add).then_inc(r_place, 1)
                    dve.wait_ge(r_place, n)
                    v.tensor_tensor(count[:], ps[:, TR, 392:392 + E], count[:], ALU.add).then_inc(r_count, 1)
                    v.tensor_tensor(placed[:], onehot[:], place[:].rearrange("p (a e) -> p a e", a=1).to_broadcast([CH, 2, E]),
                                    ALU.mult).then_inc(r_placed, 1)
                    dve.wait_ge(r_placed, n)
                    v.tensor_reduce(slotf[:], placed[:], AX.X, ALU.add).then_inc(r_slotf, 1)
                    dve.wait_ge(r_slotf, n)
                    v.tensor_copy(slot[:, 1 - p, :], slotf[:]).then_inc(r_slot, 1)
                if u == 3 and has[1]:
                    dve.wait_ge(wout_ready, c)
                    dve.wait_ge(xh_ready, c)
                    xc = x_all[:, bass.ds(c - 1, 1), :].rearrange("p a d -> p (a d)")
                    v.tensor_tensor(xc, ps[:, TR, 384:384 + D], xh[:], ALU.add).then_inc(x1_ready, 1)
                    dve.wait_ge(x1_ready, computed(dve, c))
                    v.bn_stats(st2[:], xc).then_inc(st2_done, 1)
                    dve.wait_ge(st2_done, computed(dve, c))
                    if not static or c > 1:
                        dve.wait_ge(h2_ready, computed(dve, c - 1))
                    v.bn_aggr(mv2[:], st2[:]).then_inc(mv2_ready, 1)
                    dve.wait_ge(mv2_ready, c)
                    v.tensor_scalar(ve2[:], mv2[:, 1:2], EPS_LN, None, ALU.add).then_inc(ve2_ready, 1)
                if u == 3 and has[1]:
                    dve.wait_ge(rstd2_ready, c)
                    if has[3]:
                        dve.wait_ge(staged, c - 2)
                    v.tensor_scalar(h2[:, 1 - p, :], x_all[:, bass.ds(c - 1, 1), :].rearrange("p a d -> p (a d)"), mv2[:, 0:1], rstd2[:, 0:1],
                                    ALU.subtract, ALU.mult).then_inc(h2_ready, 1)
                if u == 3 and has[2]:
                    n = c - 1
                    dve.wait_ge(wout_ready, c)
                    v.tensor_tensor(logit[:], ps[:, TR, 0:E], bgate[:], ALU.add).then_inc(r_logit, 1)
                    dve.wait_ge(r_logit, computed(dve, n))
                    v.max(top[:], logit[:]).then_inc(r_top, 1)
                    dve.wait_ge(r_top, computed(dve, n))
                    v.max_index(topi[:], top[:], logit[:]).then_inc(r_idx, 1)
                    if not static or c > 2:
                        dve.wait_ge(r_egap, n - 1)
                    v.tensor_tensor(gap[:], top[:, 1:2], top[:, 0:1], ALU.subtract).then_inc(r_gap, 1)
                    dve.wait_ge(r_idx, n)
                    v.tensor_copy(topf[:], topi[:, 0:2]).then_inc(r_idxf, 1)
                    dve.wait_ge(r_idxf, n)
                    if not static or c > 2:
                        dve.wait_ge(r_placed, n - 1)
                        dve.wait_ge(r_row, n - 1)
                    for s in range(2):
                        v.tensor_scalar(onehot[:, s], iota8[:], topf[:, s:s + 1], None, ALU.is_equal).then_inc(r_oh, 1)
                    dve.wait_ge(r_oh, 2 * n)
                    if not static or c > 2:
                        dve.wait_ge(pos_ready, n - 1)
                    v.tensor_tensor(member[:], onehot[:, 0], onehot[:, 1], ALU.add).then_inc(r_member, 1)

            def chunk(c, p, i):
                first = isinstance(c, int) and c == 0
                for u in range(UNITS):
                    n = c * UNITS + u
                    dve.wait_ge(sq_ready, n + 1)
                    v.tensor_reduce(mrow[:], ps[:, SQ, :].rearrange("p (a k) -> p a k", k=CH), AX.X, ALU.max).then_inc(max_done, 1)
                    dve.wait_ge(max_done, n + 1)
                    v.tensor_scalar(mneg[:, 0], mrow[:], -1.0, None, ALU.mult).then_inc(nh_done, 1)
                    dve.wait_ge(nh_done, n + 1)
                    v.scalar_tensor_tensor(out=mneg[:, 1], in0=mrow[:], scalar=-1.0, in1=mneg[:, 0],
                                           op0=ALU.mult, op1=ALU.subtract).then_inc(mneg_ready, 1)
                    if not first:
                        post(c, u, p, i)
                    kc = keep[0:PR, bass.ds(c + 1, 1)]
                    dve.wait_ge(kv_ready, n + 1)
                    dve.wait_ge(mneg_ready, n + 1)
                    v.scalar_tensor_tensor(out=sadd[:], in0=ps[0:PR, KV, 0:4 * UD].rearrange("p (h f) -> p h f", f=UD), scalar=kc,
                                           in1=statemask[:].rearrange("p (h f) -> p h f", f=UD), op0=ALU.mult, op1=ALU.mult).then_inc(sadd_done, 1)
                    dve.wait_ge(sadd_done, n + 1)
                    dve.wait_ge(inter_done, n + 1)
                    s = state[:, 4 * u:4 * u + 4, 0:UD]
                    v.scalar_tensor_tensor(out=s, in0=s, scalar=kc, in1=sadd[:], op0=ALU.mult, op1=ALU.add).then_inc(state_done, 1)
                    if u == 1:
                        key_features(c + 1, 1 - p)

            key_features(0, 0)
            for c in range(4):
                chunk(c, c % 2, c // 2)
            with dve.Fori(2, NC // 2) as i:
                for p in range(2):
                    chunk(i * 2 + p, p, i)
            for c in range(NC, NC + 3):
                for u in range(UNITS):
                    post(c, u, c % 2, c // 2)

            links = [0]

            def link(t):
                links[0] += 1
                t.then_inc(tab, 1)
                dve.wait_ge(tab, links[0])

            dve.wait_ge(r_count, NC)
            link(v.tensor_copy(tail_i[:], count[0:1, :]))
            link(v.tensor_tensor(ntile[:], count[0:1, :], region0[0:1, :], ALU.subtract))
            link(v.tensor_scalar(ntile[:], ntile[:], float(CH - 1), None, ALU.add))
            link(v.tensor_copy(counts_i[:], ntile[:]))
            link(v.tensor_scalar(ntile_i[:], counts_i[:], 7, None, ALU.arith_shift_right))
            link(v.tensor_copy(ntile[:], ntile_i[:]))
            link(v.tensor_tensor_scan(ends[:], ntile[:], ntile[:], 0.0, ALU.add, ALU.bypass))
            link(v.tensor_tensor(tmpt[:, 0], ends[:, E - 1:E].to_broadcast([1, NT]), tiles[:], ALU.min))
            t3 = lambda k: tmpt[:, k].rearrange("p (t a) -> p t a", a=1)
            e3 = lambda x: x.rearrange("p (a e) -> p a e", a=1).to_broadcast([1, NT, E])
            link(v.tensor_tensor(cmp8[:, 0], t3(0).to_broadcast([1, NT, E]), e3(ends[:]), ALU.is_ge))
            link(v.tensor_reduce(tmpt[:, 1], cmp8[:, 0], AX.X, ALU.add))
            link(v.tensor_tensor(cmp8[:, 1], cmp8[:, 0], e3(ntile[:]), ALU.mult))
            link(v.tensor_reduce(tmpt[:, 2], cmp8[:, 1], AX.X, ALU.add))
            link(v.tensor_tensor(tmpt[:, 0], tmpt[:, 0], tmpt[:, 2], ALU.subtract))
            link(v.tensor_scalar(tmpt[:, 0], tmpt[:, 0], float(CH), None, ALU.mult))
            link(v.scalar_tensor_tensor(out=tmpt[:, 3], in0=tmpt[:, 1], scalar=float(REGION), in1=tmpt[:, 0], op0=ALU.mult, op1=ALU.add))
            link(v.tensor_scalar(table[:, 0, :], tmpt[:, 1], float(E - 1), None, ALU.min))
            v.tensor_copy(table[:, 1, :], tmpt[:, 3]).then_inc(table_ready, 1)
            dve.wait_ge(table_ready, 1)
            dve.wait_ge(b_in, 16 * 7)

            def expert(j):
                return dve.value_load(table[0:1, 0, bass.ds(j, 1)], min_val=0, max_val=E - 1)

            def flat(ap):
                return ap.rearrange("p a f -> p (a f)")

            def step(j, k, turn):
                static = isinstance(j, int)
                on = lambda d: not static or 0 <= j + d < NT
                if on(-1):
                    dve.wait_ge(gl_ready, computed(dve, j))
                    e = expert(j - 1)
                    q = (k + 1) % 2
                    if not static or j > 2:
                        dve.wait_ge(silu_done, j - 2)
                        dve.wait_ge(o_ready, j - 2)
                    v.tensor_tensor(glb[:, q, 0:F], ps[:, GL, 0:F], flat(bgl[:, bass.ds(e, 1), 0:F]), ALU.add).then_inc(g_added, 1)
                    v.tensor_tensor(glb[:, q, F:], ps[:, GL, F:], flat(bgl[:, bass.ds(e, 1), F:]), ALU.add).then_inc(l_added, 1)
                    dve.wait_ge(silu_done, j)
                    dve.wait_ge(l_added, j)
                    if not static or j > 2:
                        dve.wait_ge(to_ready, j - 2)
                    v.tensor_tensor(og[:, q, :], sg[:, q, :], glb[:, q, F:], ALU.mult).then_inc(o_ready, 1)
                if on(1):
                    dve.wait_ge(x12_ready, computed(dve, j + 2))
                    q = (k + 1) % 2
                    e = expert(j + 1)
                    if not static or j > 0:
                        dve.wait_ge(z_ready, j)
                    v.tensor_tensor(x12[:, q, :], ps[:, X12, :], flat(b12[:, bass.ds(e, 1), :]), ALU.add).then_inc(x12_added, 1)
                    dve.wait_ge(x12_added, j + 2)
                    if not static or j > 0:
                        dve.wait_ge(tzx_ready, j + 2)
                    v.tensor_tensor(z[:, q, :], x12[:, q, 0:F], x12[:, q, F:], ALU.mult).then_inc(z_ready, 1)
                    m = (k + 1) % 4
                    if not static or j >= 3:
                        dve.wait_ge(y_weighted, j - 2)
                        dve.wait_ge(y_out[m], 16 * turn(1))
                    v.tensor_copy(mweight[:, m:m + 1], xin[:, m, bass.ds(e + D, 1)])
                    v.tensor_copy(mrowid[:, m:m + 1], xin[:, m, bass.ds(e + (D + E), 1)]).then_inc(meta_copied, 1)
                if on(-2):
                    dve.wait_ge(y_ready, computed(dve, j - 1))
                    if not static or j > 3:
                        dve.wait_ge(y_weighted, computed(dve, j - 3))
                    v.tensor_tensor(yb[:, k % 2, :], ps[:, Y, 0:D], flat(b3[:, bass.ds(expert(j - 2), 1), :]), ALU.add).then_inc(y_added, 1)

            run_steps(dve, step)
            for g in range(NG):
                at = slice(g * GC, (g + 1) * GC)
                dve.wait_ge(res_in[g], 32)
                v.tensor_tensor(res[0][:, at], res[0][:, at], res[1][:, at], ALU.add).then_inc(res_sum, 1)
                dve.wait_ge(res_sum, g + 1)
                v.tensor_tensor(x_all[:, at], x_all[:, at], res[0][:, at], ALU.add).then_inc(out_sum, 1)

        @block.gpsimd
        def _(pool):
            q = nc.gpsimd
            pool.wait_ge(zeroed, 1)
            for k in range(2):
                pool.wait_ge(ve_ready, k + 1)
                q.tensor_tensor(rstd[:] if k == 0 else vareps[:, 1, :], vareps[:, k, :], minus_half[:], ALU.pow).then_inc(pow_ready, 1)

            def post(c, u, p, i):
                static = isinstance(c, int)
                has = [not static or 0 <= c - k < NC for k in range(4)]
                if u == 1 and has[3]:
                    if not static or c > 4:
                        pool.wait_ge(scattered[1 - p], computed(pool, 32 * (i - 2 + p)))
                    pool.wait_ge(h2_ready, computed(pool, c - 2))
                    q.tensor_copy(routed_row[:, 1 - p, 0:D], h2[:, 1 - p, :]).then_inc(staged, 1)
                if u == 3 and has[1]:
                    pool.wait_ge(ve2_ready, computed(pool, c))
                    q.tensor_tensor(rstd2[:], ve2[:], minus_half[:, 0:1], ALU.pow).then_inc(rstd2_ready, 1)
                if u == 3 and has[3]:
                    pool.wait_ge(r_slot, computed(pool, c - 2))
                    pool.wait_ge(r_row, computed(pool, c - 2))
                    pool.wait_ge(staged, computed(pool, c - 2))
                    for k in range(2):
                        q.indirect_dma_start(routed, bass.IndirectOffsetOnAxis(slot[:, 1 - p, k:k + 1], 0), routed_row[:, 1 - p, :], None).then_inc(scattered[1 - p], 16)

            def chunk(c, p, i):
                first = isinstance(c, int) and c == 0
                for u in range(UNITS):
                    n = c * UNITS + u
                    pool.wait_ge(square_done, computed(pool, n + 1))
                    q.affine_select(out=amat[:, u % 2], in_=amat[:, u % 2], compare_op=ALU.is_ge, fill=0.0, base=0,
                                    pattern=[[0, 4], [1, CH]], channel_multiplier=-1).then_inc(amask_ready, 1)
                    if not first:
                        post(c, u, p, i)

            for c in range(4):
                chunk(c, c % 2, c // 2)
            with pool.Fori(2, NC // 2) as i:
                for p in range(2):
                    chunk(i * 2 + p, p, i)
            for c in range(NC, NC + 3):
                for u in range(UNITS):
                    post(c, u, c % 2, c // 2)

            def step(j, k, turn):
                if not isinstance(j, int) or 0 <= j - 2 < NT:
                    m = (k + 2) % 4
                    pool.wait_ge(y_weighted, computed(pool, j - 1))
                    q.indirect_dma_start(results, bass.IndirectOffsetOnAxis(mrowid[:, m:m + 1], 0), yw[:, m, :], None,
                                         bounds_check=RESULTS - 1, oob_is_err=False).then_inc(y_out[m], 16)

            run_steps(pool, step)


_NAMES = {"x": "L0_attn_x", "norm_w": "L0_attn_norm_w", "Wq": "L0_attn_Wq", "Wk": "L0_attn_Wk", "Wv": "L0_attn_Wv", "Wout": "L0_attn_Wout",
          **{n: "L0_ffn_" + n for n in ("Wgate", "bgate", "W1", "b1", "W2", "b2", "Wg", "bg", "Wl", "bl", "W3", "b3")}}


def kernel(**inputs):
    import concourse.bacc as _bacc
    from concourse.bass_utils import run_bass_kernel_spmd as _run

    arrays = {k: np.ascontiguousarray(inputs[v]) for k, v in _NAMES.items()}
    arrays["WqT"] = np.ascontiguousarray(np.transpose(inputs["L0_attn_Wq"]))
    arrays["WqfT"] = np.ascontiguousarray(np.tile(np.transpose(inputs["L0_attn_Wqf"]), (1, H)))
    arrays["WkfT"] = np.ascontiguousarray(np.tile(np.transpose(inputs["L0_attn_Wkf"]), (1, H)))
    con = constants()
    nc = _bacc.Bacc("TRN2", target_bir_lowering=False, num_devices=1)
    feed, ins, cin = {}, {}, {}
    for group, aps, pre in ((arrays, ins, "in_"), (con, cin, "const_")):
        for k, a in group.items():
            feed[pre + k] = a
            aps[k] = nc.dram_tensor(pre + k, a.shape, mybir.dt.from_np(a.dtype), kind="ExternalInput").ap()
    out = nc.dram_tensor("out", (B, T, D), F32, kind="ExternalOutput").ap()
    build(nc, ins, cin, out)
    r = _run(nc, [feed], core_ids=[0])
    return r.results[0]["out"]
```

```python
from contextlib import ExitStack

import numpy as np
import concourse.bass as bass
from concourse import mybir

ALU = mybir.AluOpType
ACT = mybir.ActivationFunctionType
AX = mybir.AxisListType
F32 = mybir.dt.float32
BF16 = mybir.dt.bfloat16

B, T, D = 2, 1024, 128
H, HD = 16, 8
WINDOW = 64
CH = 128
NC = B * T // CH
GC = 4
NG = NC // GC
GT = GC * CH
UNITS = 4
UD = HD + 1
NF = UD * (UD + 1) // 2
FS = 48
PR = 2 * FS
NP = H // 2
SLOTS = [(0, 2), (1, 1), (2, 0), (0, 1), (1, 0), (0, 0)]
RUNS = [(0, 0, 0, 3), (3, 0, 1, 2), (5, 0, 2, 1)]
KP = HD * len(SLOTS)
ROW_VALID, ROW_ONE = KP + WINDOW, KP + WINDOW + 1
KR = KP + WINDOW + 2
BIG = -1.0e30
E, F = 8, 256
TOPK = 2
N = B * T
REGION = N + CH
ROW = D + 2 * E
NT = TOPK * N // CH + E
RESULTS = TOPK * N
EPS_LN, EPS_RMS, EPS_LIN = 1e-5, 1e-6, 1e-6


def constants():
    c = {}
    c["ident"] = np.eye(128, dtype=np.float32)
    feats = [(i, i + dl) for dl in range(UD) for i in range(UD - dl)]
    sums = np.zeros((KR, 2, PR), np.float32)
    for par in range(2):
        for r, (i, j) in enumerate(feats):
            for z in {i, j}:
                for s in range(3):
                    if z:
                        sums[s * HD + z - 1, par, par * FS + r] = 1.0
            if i == 0:
                sums[ROW_ONE, par, par * FS + r] = 1.0
    blk = np.arange(D) // HD
    c["blockdiag"] = (blk[:, None] == blk[None, :]).astype(np.float32)
    sm = np.zeros((PR, 2, 2, UD), np.float32)
    for par in range(2):
        sm[par * FS:(par + 1) * FS, :, par] = 1.0
    c["statemask"] = sm.reshape(PR, 4 * UD)
    keep = np.ones((128, NC + 1), np.float32)
    keep[:, ::T // CH] = 0.0
    c["keep"] = keep
    q, kap = np.arange(WINDOW), np.arange(CH)
    qrows = np.zeros((KR - KP, H, CH), np.float32)
    qrows[:WINDOW] = (q[:, None] == kap[None, :] % WINDOW)[:, None]
    qrows[WINDOW] = 1.0
    arows = np.zeros((KR - KP, H, CH), np.float32)
    arows[WINDOW + 1] = 1.0
    krows = np.zeros((KR - KP, H, CH), np.float32)
    krows[:WINDOW] = np.where((kap >= q[:, None]) & (kap <= q[:, None] + WINDOW), 0.0, BIG)[:, None]
    krows[WINDOW + 1] = 1.0
    valid = np.zeros((NC, H, CH), np.float32)
    valid[::T // CH, :, :WINDOW] = BIG
    c["iota8"] = np.tile(np.arange(E, dtype=np.float32), (128, 1))
    c["region0"] = np.tile(np.arange(E, dtype=np.float32) * REGION, (128, 1))
    c["tokid"] = (np.arange(CH)[:, None] + CH * np.arange(NC)[None]).astype(np.float32)
    pad = np.zeros((CH, ROW), np.float32)
    pad[:, D + E:] = TOPK * N + np.arange(CH)[:, None]
    c["padrows"] = pad
    c["tiles"] = np.arange(NT, dtype=np.float32)[None]
    bf = mybir.dt.np(BF16)
    c["before"] = np.triu(np.ones((128, 128), np.float32), 1).astype(bf)
    c["ones"] = np.ones((128, 128), np.float32).astype(bf)
    c["sums"] = sums.reshape(KR, 2 * PR).astype(bf)
    c["qrows"], c["arows"], c["krows"] = (x.reshape(KR - KP, H * CH).astype(bf) for x in (qrows, arows, krows))
    c["valid"] = valid.reshape(NC, H * CH).astype(bf)
    c["identb"] = np.eye(128, dtype=np.float32).astype(bf)
    return c


def build(nc, ins, con, out):
    with ExitStack() as ctx:
        sb = lambda n, s, d=F32: ctx.enter_context(nc.sbuf_tensor(n, s, d))
        sem = lambda n: ctx.enter_context(nc.semaphore(n))
        dram = lambda n, s, d=F32: nc.dram_tensor(n, s, d).ap()

        qa_parts = dram("qa_parts", (3, HD, 2, H, N), BF16)
        k_parts = dram("k_parts", (3, HD, H, WINDOW + N), BF16)

        routed = dram("routed", (E * REGION + CH, ROW))
        results = dram("results", (RESULTS, D))
        ident = sb("ident", [128, 128])
        identb = sb("identb", [128, 128], BF16)
        sums = sb("sums", [KR, 2, PR], BF16)
        blockdiag = sb("blockdiag", [D, D])
        statemask = sb("statemask", [PR, 4 * UD])
        keep = sb("keep", [128, NC + 1])
        norm_w = sb("norm_w", [D, 1])
        wq = sb("wq", [D, D])
        wqT = sb("wqT", [D, D])
        wkv = sb("wkv", [D, 2, D])
        wout = sb("wout", [D, 2, D])
        wfeat = sb("wfeat", [16, 2, D])
        mblk = sb("mblk", [D, D])
        wa = sb("wa", [D, D])
        minus_half = sb("minus_half", [128, NC])
        x_all = sb("x_all", [CH, NC, D])
        stats = sb("stats", [CH, NC, 6])
        mv = sb("mv", [CH, NC, 2])
        vareps = sb("vareps", [CH, 2, NC])
        rstd = sb("rstd", [CH, NC])
        rboth = sb("rboth", [CH, NC])
        xscale = sb("xscale", [CH, NC])
        xbias = sb("xbias", [CH, NC])
        h_tok = sb("h_tok", [CH, GC, D])
        hT = sb("hT", [D, WINDOW + N])
        kv_tok = sb("kv_tok", [CH, NC, 3, D])
        rest = sb("rest", [D, 3, GT])
        w12_ = sb("w12", [D, E * 2 * F])
        wgl_ = sb("wgl", [128, E * 2 * 2 * F])
        qa = wgl_[:, 0:3 * N].bitcast(BF16).rearrange("p (a s t) -> p a s t", a=2, s=3)
        kp = w12_[:, 0:3 * (WINDOW + N) // 2].bitcast(BF16).rearrange("p (s t) -> p s t", s=3)
        qas_ = sb("qas", [128, 2, 2, H, CH], BF16)
        ks_ = sb("ks", [128, 2, 2, H, CH], BF16)
        qas, qs, as_, ks = qas_[0:KR], qas_[0:KR, :, 0], qas_[0:KR, :, 1], ks_[0:KR]
        u_tok = sb("u_tok", [CH, H, UD])
        usum = sb("usum", [CH, H])
        ut = sb("ut", [CH, H, UD])
        phik = sb("phik", [CH, 2, H, FS])
        v1 = sb("v1", [CH, 2, 2, H, 32])
        state = sb("state", [PR, H, 32])
        sadd = sb("sadd", [PR, 4, UD])
        mrow = sb("mrow", [128, 4])
        mneg = sb("mneg", [128, 2, 2, 4], BF16)
        phiq = sb("phiq", [PR, 2, 2, CH])
        amat = sb("amat", [CH, 2, 4, CH])
        pmat = sb("pmat", [CH, 2, 8, WINDOW])
        linT = sb("linT", [128, 2, 4, CH])
        winT = sb("winT", [128, 2, 4, CH])
        zrec = sb("zrec", [CH, H])
        att = sb("att", [CH, 2, H, HD])
        catT = sb("catT", [D, 3, CH])
        xh = sb("xh", [CH, D])
        st2 = sb("st2", [CH, 6])
        mv2 = sb("mv2", [CH, 2])
        ve2 = sb("ve2", [CH, 1])
        rstd2 = sb("rstd2", [CH, 1])
        h2 = sb("h2", [CH, 2, D])
        wgate = sb("wgate", [D, E])
        bgate = sb("bgate", [128, E])
        iota8 = sb("iota8", [128, E])
        tokid = sb("tokid", [CH, NC])
        before = sb("before", [128, 128], BF16)
        ones = sb("ones", [128, 128], BF16)
        count = sb("count", [128, E])
        region0 = sb("region0", [128, E])
        logit = sb("logit", [CH, E])
        top = sb("top", [CH, 8])
        topi = sb("topi", [CH, 8], mybir.dt.uint32)
        topf = sb("topf", [CH, 2])
        onehot = sb("onehot", [CH, 2, E])
        member = sb("member", [CH, E], BF16)
        gap = sb("gap", [CH, 1])
        egap = sb("egap", [CH, 1])
        wsum = sb("wsum", [CH, 1])
        w01 = sb("w01", [CH, 2])
        tmp8 = sb("tmp8", [CH, 2, E])
        place = sb("place", [CH, E])
        placed = sb("placed", [CH, 2, E])
        slotf = sb("slotf", [CH, 2])
        slot = sb("slot", [CH, 2, 2], mybir.dt.uint32)
        routed_row = sb("routed_row", [CH, 2, ROW])
        padrows = sb("padrows", [CH, ROW])
        tiles = sb("tiles", [1, NT])
        table = sb("table", [1, 2, NT], mybir.dt.int32)
        counts_i = sb("counts_i", [1, E], mybir.dt.int32)
        ntile_i = sb("ntile_i", [1, E], mybir.dt.int32)
        ntile = sb("ntile", [1, E])
        ends = sb("ends", [1, E])
        tmpt = sb("tmpt", [1, 4, NT])
        cmp8 = sb("cmp8", [1, 2, NT, E])
        tail_i = sb("tail_i", [1, E], mybir.dt.int32)
        w12 = w12_[:].rearrange("p (e f) -> p e f", e=E)
        wgl = wgl_[:].rearrange("p (e k f) -> p e k f", e=E, k=2)
        b12 = sb("b12", [128, E, 2 * F])
        b3 = sb("b3", [128, E, D])
        late0 = kv_tok[:].rearrange("p c w d -> p (c w d)")
        bgl = late0[:, 0:E * 2 * F].rearrange("p (e f) -> p e f", e=E)
        w3 = late0[:, E * 2 * F:E * 2 * F + E * 2 * D].rearrange("p (e k d) -> p e k d", e=E, k=2)
        x12, glb = (hT[:, o:o + 1024].rearrange("p (a f) -> p a f", a=2) for o in (0, 1024))
        late2 = qas_[:].rearrange("p a w h t -> p (a w h t)").bitcast(F32)
        z = late2[:, 0:512].rearrange("p (a f) -> p a f", a=2)
        og = late2[:, 512:1024].rearrange("p (a f) -> p a f", a=2)
        oT = late2[:, 1024:1536].rearrange("p (a k t) -> p a k t", a=2, k=2)
        sg = late2[:, 1536:2048].rearrange("p (a f) -> p a f", a=2)
        yw = late2[:, 2048:2560].rearrange("p (a d) -> p a d", a=4)
        late3 = rest[:].rearrange("p c t -> p (c t)")
        zxT = late3[:, 0:768].rearrange("p (a k t) -> p a k t", a=2, k=3)
        yb = late3[:, 768:1024].rearrange("p (a d) -> p a d", a=2)
        xin = sb("xin", [CH, 4, ROW])
        mweight = sb("mweight", [CH, 4])
        mrowid = sb("mrowid", [CH, 4], mybir.dt.uint32)
        res = [ks_[:].rearrange("p a w h t -> p (a w h t)").bitcast(F32)[:, 2048 * k:2048 * (k + 1)].rearrange("p (c d) -> p c d", c=NC) for k in range(2)]

        ps = ctx.enter_context(nc.psum_tensor("ps", [128, 8, 512], F32))
        SQ, ST, A, OUT0, OUT1, PHI, KV, TR = range(8)

        w_in, c_in, s_in = sem("w_in"), sem("c_in"), sem("s_in")
        x_in = [sem(f"x_in{g}") for g in range(NG)]
        zeroed = sem("zeroed")
        wstep, wstep_c = sem("wstep"), sem("wstep_c")
        mv_ready, ve_ready, pow_ready, rb_ready, h_ready = (sem(n) for n in ("mv_ready", "ve_ready", "pow_ready", "rb_ready", "h_ready"))
        hps_ready, hT_ready = sem("hps_ready"), sem("hT_ready")
        proj_ready, part0, rest1, part1, part2 = (sem(n) for n in ("proj_ready", "part0", "rest1", "part1", "part2"))
        kv_proj, kv_copied = sem("kv_proj"), sem("kv_copied")
        parts_out = [sem(f"parts_out{g}") for g in range(NG)]
        stack_in = [sem("stack_in0"), sem("stack_in1")]
        sq_ready, max_done, nh_done, mneg_ready = sem("sq_ready"), sem("max_done"), sem("nh_done"), sem("mneg_ready")
        a_ready, square_done, amask_ready = sem("a_ready"), sem("square_done"), sem("amask_ready")
        phi_ready, phisq_done, inter_done = sem("phi_ready"), sem("phisq_done"), sem("inter_done")
        us, ut_done, phik_ready, cross_ready, kv_ready, sadd_done, state_done = (sem(n) for n in ("us", "ut_done", "phik_ready", "cross_ready", "kv_ready", "sadd_done", "state_done"))
        st_ready, exp_done, out_ready, evac_done = sem("st_ready"), sem("exp_done"), sem("out_ready"), sem("evac_done")
        t_lin, t_win, t_cat, cat_copied, wout_ready = (sem(n) for n in ("t_lin", "t_win", "t_cat", "cat_copied", "wout_ready"))
        z1, z2, norm_lin, norm_win = sem("z1"), sem("z2"), sem("norm_lin"), sem("norm_win")
        xaffine, xh_ready, x1_ready, st2_done, mv2_ready, ve2_ready, rstd2_ready, h2_ready = (
            sem(n) for n in ("xaffine", "xh_ready", "x1_ready", "st2_done", "mv2_ready", "ve2_ready", "rstd2_ready", "h2_ready"))
        done = sem("done")
        settled = sem("settled")
        xin_ready = [sem(f"xin_ready{k}") for k in range(4)]
        y_out = [sem(f"y_out{k}") for k in range(4)]
        (r_logit, r_top, r_idx, r_idxf, r_oh, r_member, r_gap, r_egap, r_ws, r_w, r_w2, r_tmp, r_row, r_place, r_placed, r_slotf, r_slot,
         r_count, pos_ready, staged, scattered) = tuple(sem(n) for n in (
             "r_logit", "r_top", "r_idx", "r_idxf", "r_oh", "r_member", "r_gap", "r_egap", "r_ws", "r_w", "r_w2", "r_tmp", "r_row", "r_place",
             "r_placed", "r_slotf", "r_slot", "r_count", "pos_ready", "staged")) + ([sem("scattered0"), sem("scattered1")],)
        tab, tail_ready, table_ready, padded = sem("tab"), sem("tail_ready"), sem("table_ready"), sem("padded")
        e_in, b_in = sem("e_in"), sem("b_in")
        (tzx_ready, zx_copied, x12_ready, x12_added, z_ready, meta_copied, gl_ready, gl_added, silu_done, o_ready, to_ready,
         oT_copied, y_ready, y_added, y_weighted) = (sem(n) for n in (
             "tzx_ready", "zx_copied", "x12_ready", "x12_added", "z_ready", "meta_copied", "gl_ready", "gl_added",
             "silu_done", "o_ready", "to_ready", "oT_copied", "y_ready", "y_added", "y_weighted"))
        res_in = [sem(f"res_in{g}") for g in range(NG)]
        res_sum, out_sum = sem("res_sum"), sem("out_sum")

        TZX, X12, Y, TO, GL = SQ, ST, A, PHI, OUT0

        def settle(engine):
            engine.wait_ge(settled, 1)

        def computed(engine, value):
            if not isinstance(value, int):
                value = engine.snap(engine.to_reg(value))
            settle(engine)
            return value

        def run_steps(engine, step, places=()):
            def turns(i, k):
                return lambda d: i + (k + d) // 4

            def run(j, k, i, known, at):
                for d in places:
                    if at + d not in known and (not isinstance(j, int) or 0 <= j + d < NT):
                        known[at + d] = engine.value_load(table[0:1, 0, bass.ds(j + d, 1)], min_val=0, max_val=E - 1)
                step(j, k, turns(i, k), lambda d: known[at + d])

            known = {}
            for j in range(-2, 4):
                run(j, j % 4, j // 4, known, j)
            with engine.Fori(0, (NT - 8) // 8) as i:
                body = {}
                for k in range(4, 12):
                    run(i * 8 + k, k % 4, i * 2 + k // 4, body, k)
            known = {}
            for j in range(NT - 4, NT + 2):
                run(j, j % 4, j // 4, known, j)

        x_dram = ins["x"].rearrange("b (c p) d -> p (b c) d", p=CH)
        N_W, N_C = 9, 16
        WRITES = 9
        STACKS = 16 * 3 * len(RUNS)
        split = lambda n: ins[n].rearrange("(a e) f -> a e f", a=1).to_broadcast([128, E, ins[n].shape[1]])

        def part_of(g, t, part):
            if t == 1:
                return kp[:, part, bass.ds(g * GT + WINDOW, GT)]
            return qa[:, t // 2, part, bass.ds(g * GT, GT)]

        def pad_regions(engine, experts):
            engine.wait_ge(tail_ready, 1)
            for e in experts:
                row = engine.value_load(tail_i[0:1, e:e + 1], min_val=0, max_val=E * REGION - CH)
                engine.dma_start(routed[bass.ds(row, CH), :], padrows[:]).then_inc(padded, 16)

        block = ctx.enter_context(nc.Block())

        @block.sync
        def _(sp):
            for g in range(NG):
                sp.dma_start(x_all[:, g * GC:(g + 1) * GC], x_dram[:, g * GC:(g + 1) * GC]).then_inc(x_in[g], 16)
            sp.wait_ge(w_in, 16 * N_W)
            for dst, name in ((identb, "identb"), (sums, "sums"), (statemask, "statemask"), (keep, "keep"), (iota8, "iota8"),
                              (region0, "region0"), (tokid, "tokid"), (before, "before"), (ones, "ones"), (padrows, "padrows"),
                              (tiles, "tiles"), (count, "region0")):
                sp.dma_start(dst[:].rearrange("r a f -> r (a f)") if name == "sums" else dst[:], con[name]).then_inc(c_in, 16)
            sp.dma_start(wout[:, 0, :], ins["Wout"][0:D, :]).then_inc(c_in, 16)
            sp.dma_start(wout[:, 1, :], ins["Wout"][D:2 * D, :]).then_inc(c_in, 16)
            sp.dma_start(wgate[:], ins["Wgate"]).then_inc(c_in, 16)
            sp.dma_start(bgate[:], ins["bgate"].rearrange("(a e) -> a e", a=1).to_broadcast([128, E])).then_inc(c_in, 16)
            for p in range(2):
                sp.dma_start(qs[KP:KR, p], con["qrows"]).then_inc(s_in, 16)
                sp.dma_start(as_[KP:KR, p], con["arows"]).then_inc(s_in, 16)
                for w in range(2):
                    sp.dma_start(ks[KP:KR, p, w], con["krows"]).then_inc(s_in, 16)

            sp.dma_start(b12[:, :, 0:F], split("b1")).then_inc(b_in, 16)
            sp.dma_start(b12[:, :, F:], split("b2")).then_inc(b_in, 16)
            sp.dma_start(b3[:], split("b3")).then_inc(b_in, 16)

            def write_parts(g):
                sp.wait_ge(part2, 3 * (g + 1))
                for p in range(3):
                    for t in range(2):
                        sp.dma_start(qa_parts[p, :, t, :, g * GT:(g + 1) * GT].rearrange("d h t -> h d t"),
                                     qa[:, t, p, g * GT:(g + 1) * GT]).then_inc(parts_out[g], 16)
                    lo = WINDOW + g * GT if g else 0
                    sp.dma_start(k_parts[2 - p, :, :, lo:WINDOW + (g + 1) * GT].rearrange("d h t -> h d t"),
                                 kp[:, p, lo:WINDOW + (g + 1) * GT]).then_inc(parts_out[g], 16)

            def load_stack(c, p, i):
                if not isinstance(c, int) or c >= 2:
                    sp.wait_ge(out_ready, UNITS * (2 * i + p - 1))
                for s, qp, kpp, n in RUNS:
                    rows = slice(HD * s, HD * (s + n))
                    sp.dma_start(qas[rows, p].rearrange("r a h t -> r (a h) t"),
                                 qa_parts[qp:qp + n, :, :, :, bass.ds(c * CH, CH)].rearrange("s d a h t -> (s d) (a h) t")).then_inc(stack_in[p], 16)
                    for w in range(2):
                        sp.dma_start(ks[rows, p, w],
                                     k_parts[kpp:kpp + n, :, :, bass.ds(c * CH + w * WINDOW, CH)].rearrange("s d h t -> (s d) h t")).then_inc(stack_in[p], 16)
                if p == 0:
                    sp.dma_start(ks[ROW_VALID:ROW_VALID + 1, p, 0], con["valid"][bass.ds(c, 1)]).then_inc(stack_in[p], 16)

            write_parts(0)
            sp.wait_ge(parts_out[0], 16 * WRITES)
            sp.wait_ge(s_in, 16 * 8)
            load_stack(0, 0, 0)
            load_stack(1, 1, 0)
            for g in range(1, NG):
                write_parts(g)
            for g in range(1, NG):
                sp.wait_ge(parts_out[g], 16 * WRITES)
            for c in range(2, 4):
                load_stack(c, c % 2, c // 2)
            with sp.Fori(2, NC // 2) as i:
                for p in range(2):
                    load_stack(i * 2 + p, p, i)
            sp.wait_ge(phik_ready, NC)
            sp.dma_start(bgl[:, :, 0:F], split("bg")).then_inc(b_in, 16)
            sp.dma_start(bgl[:, :, F:], split("bl")).then_inc(b_in, 16)
            for k in range(2):
                sp.dma_start(w3[:, :, k, :], ins["W3"][:, k * 128:(k + 1) * 128, :].rearrange("e d f -> d e f")).then_inc(b_in, 16)
            sp.dma_start(routed[E * REGION:E * REGION + CH, :], padrows[:]).then_inc(padded, 16)
            pad_regions(sp, range(0, E // 2))
            sp.wait_ge(table_ready, 1)
            sp.wait_ge(padded, 16 * (E + 1))
            for p in range(2):
                sp.wait_ge(scattered[p], 16 * NC)

            def load_tile(j, k):
                if not isinstance(j, int) or j >= 4:
                    sp.wait_ge(tzx_ready, computed(sp, j - 1))
                    sp.wait_ge(meta_copied, computed(sp, j - 3))
                row = sp.value_load(table[0:1, 1, bass.ds(j, 1)], min_val=0, max_val=E * REGION)
                sp.dma_start(xin[:, k, :], routed[bass.ds(row, CH), :]).then_inc(xin_ready[k], 16)

            for j in range(4):
                load_tile(j, j)
            with sp.Fori(1, NT // 4) as i:
                for k in range(4):
                    load_tile(i * 4 + k, k)
            for k in range(4):
                sp.wait_ge(y_out[k], 16 * (NT // 4))
            for g in range(NG):
                for k in range(2):
                    lo = k * N + g * GT
                    sp.dma_start(res[k][:, g * GC:(g + 1) * GC], results[lo:lo + GT, :].rearrange("(c p) d -> p c d", p=CH)).then_inc(res_in[g], 16)
            for g in range(NG):
                sp.wait_ge(out_sum, g + 1)
                sp.dma_start(out.rearrange("b (c p) d -> p (b c) d", p=CH)[:, g * GC:(g + 1) * GC], x_all[:, g * GC:(g + 1) * GC]).then_inc(done, 16)
            sp.wait_ge(done, 16 * NG)

        @block.tensor
        def _(pe):
            mm = nc.tensor.matmul
            pe.wait_ge(w_in, 16 * N_W)
            mm(ps[:, TR, 0:D], wfeat[:, 0, :], wfeat[:, 1, :], start=True, stop=True).then_inc(wstep, 1)
            pe.wait_ge(wstep_c, 1)
            mm(ps[:, A, 0:D], wqT[:], mblk[:], start=True, stop=True).then_inc(wstep, 1)

            def transposes(g):
                pe.wait_ge(h_ready, g + 1)
                if not isinstance(g, int) or g:
                    pe.wait_ge(hT_ready, g)
                for cc in range(GC):
                    t = nc.tensor.transpose(ps[:, TR, cc * CH:(cc + 1) * CH], h_tok[:, cc, :], ident[:])
                t.then_inc(hps_ready, 1)

            def group(g, last):
                pe.wait_ge(hT_ready, g + 1)
                pe.wait_ge(wstep_c, 2)
                for t, w in enumerate((wq[:], wkv[:, 0, :], wa[:])):
                    if not isinstance(g, int) or g:
                        pe.wait_ge(rest1, 3 * (g - 1) + t + 1)
                    mm(ps[:, SQ + t, :], w, hT[:, bass.ds(g * GT + WINDOW, GT)], start=True, stop=True).then_inc(proj_ready, 1)
                if not last:
                    transposes(g + 1)
                for cc in range(GC):
                    bank, lo = OUT0 + cc % 2, g * GT + cc * CH
                    if not isinstance(g, int) or g or cc > 1:
                        pe.wait_ge(kv_copied, GC * g + cc - 1)
                    mm(ps[:, bank, 0:2 * D], hT[:, lo + WINDOW:lo + WINDOW + CH], wkv[:].rearrange("p a d -> p (a d)"),
                       start=True, stop=True)
                    mm(ps[:, bank, 2 * D:3 * D], hT[:, lo:lo + CH], wkv[:, 1, :],
                       start=True, stop=True).then_inc(kv_proj, 1)

            transposes(0)
            for g in range(NG):
                group(g, g == NG - 1)
            pe.wait_ge(kv_copied, NC)
            pe.wait_ge(rest1, 3 * NG)
            pe.wait_ge(c_in, 16 * N_C)

            def post(c, u, p):
                static = isinstance(c, int)
                has = [not static or 0 <= c - k < NC for k in range(4)]
                if u == 0 and has[1]:
                    pe.wait_ge(evac_done, UNITS * c)
                    if not static or c > 1:
                        pe.wait_ge(x1_ready, c - 1)
                    if not static or c > 2:
                        pe.wait_ge(r_logit, c - 2)
                    for s in range(4):
                        t = nc.tensor.transpose(ps[:, TR, s * CH:(s + 1) * CH], linT[:, 1 - p, s, :], ident[:])
                    t.then_inc(t_lin, 1)
                if u == 1 and has[1]:
                    pe.wait_ge(norm_lin, c)
                    for s in range(4):
                        t = nc.tensor.transpose(ps[:, TR, s * CH:(s + 1) * CH], winT[:, 1 - p, s, :], ident[:])
                    t.then_inc(t_win, 1)
                if u == 2:
                    if has[1]:
                        pe.wait_ge(norm_win, c)
                    else:
                        pe.wait_ge(x1_ready, NC)
                        pe.wait_ge(r_logit, c - 2)
                    if has[3]:
                        pe.wait_ge(r_member, c - 2)
                        mm(ps[:, TR, 384:384 + E], before[:], member[:], start=True, stop=True)
                        mm(ps[:, TR, 392:392 + E], ones[:], member[:], start=True, stop=True).then_inc(pos_ready, 1)
                    if has[1]:
                        for s in range(2):
                            t = nc.tensor.transpose(ps[:, TR, s * CH:(s + 1) * CH], att[:, s].rearrange("p h d -> p (h d)"), ident[:])
                    if has[2]:
                        pe.wait_ge(h2_ready, c - 1)
                        t = nc.tensor.transpose(ps[:, TR, 2 * CH:3 * CH], h2[:, p, :], ident[:])
                    if has[1] or has[2]:
                        t.then_inc(t_cat, 1)
                if u == 3 and (has[1] or has[2]):
                    pe.wait_ge(cat_copied, c)
                    if has[3]:
                        pe.wait_ge(r_count, c - 2)
                    if has[1]:
                        mm(ps[:, TR, 384:384 + D], catT[:, 0, :], wout[:, 0, :], start=True, stop=False)
                        t = mm(ps[:, TR, 384:384 + D], catT[:, 1, :], wout[:, 1, :], start=False, stop=True)
                    if has[2]:
                        t = mm(ps[:, TR, 0:E], catT[:, 2, :], wgate[:], start=True, stop=True)
                    t.then_inc(wout_ready, 1)

            def window_scores(n, u, p, i):
                if u == 0:
                    pe.wait_ge(stack_in[p], (STACKS + 16 * (1 - p)) * (i + 1))
                if not isinstance(n, int) or n:
                    pe.wait_ge(max_done, n)
                j, hf = u // 2, u % 2
                for hh in range(8):
                    h = 8 * hf + hh
                    r = WINDOW * (hh % 2)
                    t = mm(ps[r:r + WINDOW, SQ, (hh // 2) * CH:(hh // 2 + 1) * CH], qs[:, p, h, j * WINDOW:(j + 1) * WINDOW],
                           ks[:, p, j, h, :], start=True, stop=True)
                t.then_inc(sq_ready, 1)

            def linear_scores(n, u, p):
                if not isinstance(n, int) or n:
                    pe.wait_ge(square_done, n)
                for g in range(4):
                    t = mm(ps[:, A, g * CH:(g + 1) * CH], ks[:, p, 1, 4 * u + g, :], as_[:, p, 4 * u + g, :], start=True, stop=True)
                t.then_inc(a_ready, 1)
                if not isinstance(n, int) or n:
                    pe.wait_ge(phisq_done, n)
                for k in range(2):
                    for par in range(2):
                        t = mm(ps[0:PR, PHI, k * CH:(k + 1) * CH], sums[:, par, :], as_[:, p, 4 * u + 2 * k + par, :],
                               start=par == 0, stop=par == 1)
                t.then_inc(phi_ready, 1)

            def chunk(c, p, i):
                first = isinstance(c, int) and c == 0
                for u in range(UNITS):
                    n = c * UNITS + u
                    j, hf = u // 2, u % 2
                    early = isinstance(n, int)
                    pe.wait_ge(phik_ready, c + 1)
                    pe.wait_ge(cross_ready, c + 1)
                    if not early or n:
                        pe.wait_ge(sadd_done, n)
                    for k in range(2):
                        hp = 2 * (2 * u + k)
                        t = mm(ps[0:PR, KV, k * 2 * UD:(k + 1) * 2 * UD], phik[:, p, hp:hp + 2, :].rearrange("p h f -> p (h f)"),
                               v1[:, p, 1, hp:hp + 2, 0:UD], start=True, stop=True)
                    t.then_inc(kv_ready, 1)
                    if u < 3:
                        window_scores(n + 1, u + 1, p, i)
                    elif not early or c < NC - 1:
                        window_scores(n + 1, 0, 1 - p, i + p)
                    if not first:
                        post(c, u, p)
                    pe.wait_ge(mneg_ready, n + 1)
                    if not early or n:
                        pe.wait_ge(exp_done, n)
                    for hh in range(8):
                        h = 8 * hf + hh
                        mm(ps[:, ST, hh * WINDOW:(hh + 1) * WINDOW], ks[:, p, j, h, :], qs[:, p, h, j * WINDOW:(j + 1) * WINDOW],
                           start=(hh == 0), stop=False, skip_group_check=True)
                    for pr in range(4):
                        for part in range(2):
                            t = mm(ps[:, ST, pr * CH:(pr + 1) * CH], mneg[:, u % 2, part, pr:pr + 1].to_broadcast([128, 128]), identb[:],
                                   start=False, stop=(part == 1), skip_group_check=True)
                    t.then_inc(st_ready, 1)
                    bank = OUT0 + u % 2
                    pe.wait_ge(phisq_done, n + 1)
                    if not early or n > 1:
                        pe.wait_ge(evac_done, n - 1)
                    if not early or n > 3:
                        pe.wait_ge(state_done, n - 3)
                    for k in range(2):
                        t = mm(ps[64 * k:64 * k + 64, bank, 0:CH], state[:, 2 * (2 * u + k):2 * (2 * u + k) + 2, :].rearrange("p h f -> p (h f)"),
                               phiq[:, u % 2, k, :], start=True, stop=False, skip_group_check=True)
                    t.then_inc(inter_done, 1)
                    pe.wait_ge(amask_ready, n + 1)
                    for g in range(4):
                        mm(ps[32 * g:32 * g + 32, bank, 0:CH], v1[:, p, 1, 4 * u + g, :], amat[:, u % 2, g, :],
                           start=False, stop=True, skip_group_check=True)
                    if u < 3:
                        linear_scores(n + 1, u + 1, p)
                    elif not early or c < NC - 1:
                        linear_scores(n + 1, 0, 1 - p)
                    pe.wait_ge(exp_done, n + 1)
                    for hh in range(8):
                        g, s = hh % 4, hh // 4
                        t = mm(ps[32 * g:32 * g + 32, bank, CH + s * WINDOW:CH + (s + 1) * WINDOW], v1[:, p, j, 8 * hf + hh, :],
                               pmat[:, u % 2, hh, :], start=True, stop=True, skip_group_check=True)
                    t.then_inc(out_ready, 1)

            window_scores(0, 0, 0, 0)
            linear_scores(0, 0, 0)
            for c in range(4):
                chunk(c, c % 2, c // 2)
            with pe.Fori(2, NC // 2 - 1) as i:
                for p in range(2):
                    chunk(i * 2 + p, p, i)
            for c in range(NC - 2, NC):
                chunk(c, c % 2, c // 2)
            for c in range(NC, NC + 3):
                for u in range(UNITS):
                    post(c, u, c % 2)

            pe.wait_ge(x1_ready, NC)
            pe.wait_ge(r_count, NC)
            pe.wait_ge(table_ready, 1)
            pe.wait_ge(e_in, 16 * 6)
            pe.wait_ge(b_in, 16 * 7)

            def rhs(ap):
                return ap.rearrange("p a f -> p (a f)")

            def step(j, k, turn, expert):
                static = isinstance(j, int)
                on = lambda d: not static or 0 <= j + d < NT
                if (on(0) or on(2)) and not (static and j == -2):
                    pe.wait_ge(zx_copied, j + 2)
                if on(0):
                    pe.wait_ge(z_ready, j + 1)
                    for s in range(2):
                        t = nc.tensor.transpose(ps[:, TZX, s * CH:(s + 1) * CH], z[:, k % 2, s * CH:(s + 1) * CH], ident[:])
                if on(2):
                    pe.wait_ge(xin_ready[(k + 2) % 4], 16 * (turn(2) + 1))
                    t = nc.tensor.transpose(ps[:, TZX, 2 * CH:3 * CH], xin[:, (k + 2) % 4, 0:D], ident[:])
                if on(0) or on(2):
                    t.then_inc(tzx_ready, 1)
                if on(1):
                    pe.wait_ge(zx_copied, computed(pe, j + 2))
                    if not static or j >= 0:
                        pe.wait_ge(x12_added, computed(pe, j + 1))
                    mm(ps[:, X12, :], zxT[:, (k + 1) % 2, 2, :], rhs(w12[:, bass.ds(expert(1), 1), :]), start=True, stop=True).then_inc(x12_ready, 1)
                if on(-2):
                    pe.wait_ge(oT_copied, computed(pe, j - 1))
                    if not static or j > 2:
                        pe.wait_ge(y_added, computed(pe, j - 2))
                    e = expert(-2)
                    for s in range(2):
                        t = mm(ps[:, Y, 0:D], oT[:, k % 2, s, :], rhs(w3[:, bass.ds(e, 1), s, :]), start=(s == 0), stop=(s == 1))
                    t.then_inc(y_ready, 1)
                if on(0):
                    pe.wait_ge(zx_copied, computed(pe, j + 3))
                    if not static or j > 0:
                        pe.wait_ge(gl_added, computed(pe, j))
                    e = expert(0)
                    for s in range(2):
                        t = mm(ps[:, GL, :], zxT[:, k % 2, s, :], rhs(wgl[:, bass.ds(e, 1), s, :]), start=(s == 0), stop=(s == 1))
                    t.then_inc(gl_ready, 1)
                if on(-1):
                    pe.wait_ge(o_ready, j)
                    if not static or j > 1:
                        pe.wait_ge(oT_copied, j - 1)
                    for s in range(2):
                        t = nc.tensor.transpose(ps[:, TO, s * CH:(s + 1) * CH], og[:, (k + 1) % 2, s * CH:(s + 1) * CH], ident[:])
                    t.then_inc(to_ready, 1)

            run_steps(pe, step, (-2, 0, 1))

        @block.scalar
        def _(act):
            a_ = nc.scalar.activation
            for dst, src in ((wfeat[:, 0, :], ins["WqfT"]), (wfeat[:, 1, :], ins["WkfT"]), (blockdiag[:], con["blockdiag"]), (wqT[:], ins["WqT"]),
                             (ident[:], con["ident"]), (norm_w[:], ins["norm_w"].rearrange("(d a) -> d a", a=1)), (wq[:], ins["Wq"]),
                             (wkv[:, 0, :], ins["Wk"]), (wkv[:, 1, :], ins["Wv"])):
                act.dma_start(dst, src).then_inc(w_in, 16)
            act.wait_ge(w_in, 16 * N_W)
            act.wait_ge(wstep, 2)
            nc.scalar.mul(wa[:], ps[:, A, 0:D], 0.5).then_inc(wstep_c, 1)

            def normed(g):
                act.wait_ge(hps_ready, g + 1)
                a_(hT[:, bass.ds(g * GT + WINDOW, GT)], ps[:, TR, :], ACT.Copy, scale=norm_w[:, 0:1]).then_inc(hT_ready, 1)

            def group(g, last):
                for t in range(3):
                    act.wait_ge(proj_ready, 3 * g + t + 1)
                    a_(part_of(g, t, 0), ps[:, SQ + t, :], ACT.Copy, scale=float(HD) ** -0.5 if t == 0 else 1.0).then_inc(part0, 1)
                for t in range(3):
                    act.wait_ge(rest1, 3 * g + t + 1)
                    nc.scalar.copy(part_of(g, t, 1), rest[:, t, :]).then_inc(part1, 1)
                if not last:
                    normed(g + 1)
                for cc in range(GC):
                    act.wait_ge(kv_proj, g * GC + cc + 1)
                    nc.scalar.copy(kv_tok[:, bass.ds(g * GC + cc, 1)].rearrange("p a w d -> p (a w d)"),
                                   ps[:, OUT0 + cc % 2, 0:3 * D]).then_inc(kv_copied, 1)

            normed(0)
            group(0, False)
            with act.Fori(1, NG - 1) as g:
                group(g, False)
            group(NG - 1, True)

            def post(c, u):
                static = isinstance(c, int)
                has = [not static or 0 <= c - k < NC for k in range(4)]
                if u == 0 and has[3]:
                    act.wait_ge(r_gap, c - 2)
                    a_(egap[:], gap[:], ACT.Exp).then_inc(r_egap, 1)
                if u == 1 and has[1]:
                    if not static or c > 1:
                        act.wait_ge(x1_ready, c - 1)
                    a_(xh[:], x_all[:, bass.ds(c - 1, 1), :].rearrange("p a d -> p (a d)"), ACT.Identity,
                       scale=xscale[:, bass.ds(c - 1, 1)], bias=xbias[:, bass.ds(c - 1, 1)]).then_inc(xh_ready, 1)
                if u == 2 and (has[1] or has[2]):
                    lo, hi = (0 if has[1] else 2), (3 if has[2] else 2)
                    act.wait_ge(t_cat, c)
                    nc.scalar.copy(catT[:, lo:hi].rearrange("p k t -> p (k t)"), ps[:, TR, lo * CH:hi * CH]).then_inc(cat_copied, 1)

            def squares(n, u):
                act.wait_ge(a_ready, n + 1)
                if not isinstance(n, int) or n > 1:
                    act.wait_ge(out_ready, n - 1)
                a_(amat[:, u % 2].rearrange("p g t -> p (g t)"), ps[:, A, :], ACT.Square).then_inc(square_done, 1)
                act.wait_ge(phi_ready, n + 1)
                a_(phiq[:, u % 2].rearrange("p k t -> p (k t)"), ps[0:PR, PHI, 0:2 * CH], ACT.Square).then_inc(phisq_done, 1)

            def chunk(c, p):
                for u in range(UNITS):
                    n = c * UNITS + u
                    early = isinstance(n, int)
                    j, hf = u // 2, u % 2
                    bank = OUT0 + u % 2
                    if not (early and c == 0):
                        post(c, u)
                    act.wait_ge(st_ready, n + 1)
                    a_(pmat[:, u % 2].rearrange("p g t -> p (g t)"), ps[:, ST, :], ACT.Exp).then_inc(exp_done, 1)
                    if not early or c < NC - 1 or u < 3:
                        squares(n + 1, (u + 1) % 4)
                    act.wait_ge(out_ready, n + 1)
                    if u == 0 and (not early or n > 4):
                        act.wait_ge(t_win, c - 1)
                    nc.scalar.copy(linT[:, p, u, :], ps[:, bank, 0:CH])
                    nc.scalar.copy(winT[:, p, 2 * hf:2 * hf + 2, j * WINDOW:(j + 1) * WINDOW],
                                   ps[:, bank, CH:2 * CH].rearrange("p (s t) -> p s t", s=2)).then_inc(evac_done, 1)

            act.wait_ge(xaffine, 1)
            squares(0, 0)
            weights = [(w12[:, :, 0:F], ins["W1"]), (w12[:, :, F:], ins["W2"])] + [
                (wgl[:, :, k, lo:lo + F], ins[n][:, k * 128:(k + 1) * 128, :]) for k in range(2) for lo, n in ((0, "Wg"), (F, "Wl"))]

            def weights_in(some):
                for dst, src in some:
                    act.dma_start(dst, src.rearrange("e d f -> d e f")).then_inc(e_in, 16)

            for c in range(4):
                chunk(c, c % 2)
                if c == 0:
                    for g in range(NG):
                        act.wait_ge(parts_out[g], 16 * WRITES)
                weights_in(weights[c:c + 1])
            with act.Fori(2, NC // 2 - 1) as i:
                for p in range(2):
                    chunk(i * 2 + p, p)
            for c in range(NC - 2, NC):
                chunk(c, c % 2)
                weights_in(weights[4 + c - (NC - 2):][:1])
            for c in range(NC, NC + 3):
                for u in range(UNITS):
                    post(c, u)

            pad_regions(act, range(E // 2, E))

            def step(j, k, turn, expert):
                static = isinstance(j, int)
                on = lambda d: not static or 0 <= j + d < NT
                if on(-2):
                    act.wait_ge(to_ready, j - 1)
                    if not static or j > 3:
                        act.wait_ge(y_ready, j - 3)
                    nc.scalar.copy(oT[:, k % 2].rearrange("p a t -> p (a t)"), ps[:, TO, 0:F]).then_inc(oT_copied, 1)
                if on(0) or on(2):
                    act.wait_ge(tzx_ready, j + 3)
                    if not static or j > -1:
                        act.wait_ge(x12_ready, j + 1)
                    if not static or j > 1:
                        act.wait_ge(gl_ready, j - 1)
                    lo, hi = (0 if on(0) else 2), (3 if on(2) else 2)
                    nc.scalar.copy(zxT[:, k % 2, lo:hi, :].rearrange("p k t -> p (k t)"), ps[:, TZX, lo * CH:hi * CH]).then_inc(zx_copied, 1)
                if on(-1):
                    act.wait_ge(gl_added, j)
                    if not static or j > 2:
                        act.wait_ge(o_ready, j - 2)
                    a_(sg[:, (k + 1) % 2, :], glb[:, (k + 1) % 2, 0:F], ACT.Silu).then_inc(silu_done, 1)
                if on(-2):
                    act.wait_ge(y_added, j - 1)
                    act.wait_ge(meta_copied, j - 1)
                    if not static or j >= 6:
                        act.wait_ge(y_out[(k + 2) % 4], 16 * turn(-2))
                    a_(yw[:, (k + 2) % 4, :], yb[:, k % 2, :], ACT.Copy, scale=mweight[:, (k + 2) % 4:(k + 2) % 4 + 1]).then_inc(y_weighted, 1)

            run_steps(act, step)

        @block.vector
        def _(dve):
            v = nc.vector
            v.memset(hT[:, 0:WINDOW], 0.0).then_inc(settled, 1)
            for c in range(NC):
                if c % GC == 0:
                    dve.wait_ge(x_in[c // GC], 16)
                v.bn_stats(stats[:, c, :], x_all[:, c, :]).then_inc(mv_ready, 1)
            for c in range(NC):
                if c % GC == 0:
                    dve.wait_ge(mv_ready, NC)
                v.bn_aggr(mv[:, c, :], stats[:, c, :]).then_inc(mv_ready, 1)
            dve.wait_ge(mv_ready, 2 * NC)
            var = mv[:, :, 1]
            v.tensor_scalar(vareps[:, 0, :], var, EPS_LN, None, ALU.add).then_inc(ve_ready, 1)
            dve.wait_ge(pow_ready, 1)
            v.tensor_tensor(rboth[:], rstd[:], rstd[:], ALU.mult).then_inc(rb_ready, 1)
            v.scalar_tensor_tensor(out=xbias[:], in0=mv[:, :, 0], scalar=-1.0, in1=rstd[:], op0=ALU.mult, op1=ALU.mult)
            v.tensor_scalar(xscale[:], rstd[:], 1.0, None, ALU.add).then_inc(xaffine, 1)
            dve.wait_ge(rb_ready, 1)
            v.tensor_tensor(rboth[:], rboth[:], var, ALU.mult).then_inc(rb_ready, 1)
            dve.wait_ge(rb_ready, 2)
            v.tensor_scalar(vareps[:, 1, :], rboth[:], EPS_RMS, None, ALU.add).then_inc(ve_ready, 1)
            dve.wait_ge(w_in, 16 * N_W)
            dve.wait_ge(wstep, 1)
            v.tensor_tensor(mblk[:], ps[:, TR, 0:D], blockdiag[:], ALU.mult).then_inc(wstep_c, 1)
            dve.wait_ge(pow_ready, 2)
            v.tensor_tensor(rboth[:], vareps[:, 1, :], rstd[:], ALU.mult).then_inc(rb_ready, 1)
            dve.wait_ge(rb_ready, 3)

            def key_features(c, p):
                static = isinstance(c, int)
                if not static or c > 1:
                    dve.wait_ge(out_ready, UNITS * (c - 1))
                    dve.wait_ge(phik_ready, c)
                if not static or c:
                    dve.wait_ge(cross_ready, c)
                if static and c < 2:
                    dve.wait_ge(kv_copied, NC if c else GC)
                v.tensor_copy(v1[:, p, 1, :, 0:HD], kv_tok[:, bass.ds(c, 1), 1, :].rearrange("p a (h d) -> p (a h) d", h=H))
                v.tensor_copy(v1[:, p, 0, :, 0:HD], kv_tok[:, bass.ds(c, 1), 2, :].rearrange("p a (h d) -> p (a h) d", h=H))
                v.tensor_copy(u_tok[:, :, 1:UD], kv_tok[:, bass.ds(c, 1), 0, :].rearrange("p a (h d) -> p (a h) d", h=H)).then_inc(us, 1)
                dve.wait_ge(us, c * 2 + 1)
                v.tensor_reduce(usum[:], u_tok[:], AX.X, ALU.add).then_inc(us, 1)
                dve.wait_ge(us, c * 2 + 2)
                v.scalar_tensor_tensor(out=ut[:], in0=u_tok[:], scalar=2.0, in1=usum[:].to_broadcast([CH, H, UD]),
                                       op0=ALU.mult, op1=ALU.subtract).then_inc(ut_done, 1)
                dve.wait_ge(ut_done, c + 1)
                v.tensor_tensor(phik[:, p, :, 0:UD], ut[:], u_tok[:], ALU.mult).then_inc(phik_ready, 1)

            def rows(g):
                if not isinstance(g, int) or g:
                    dve.wait_ge(hps_ready, g)
                for cc in range(GC):
                    at = bass.ds(g * GC + cc, 1)
                    t = v.tensor_scalar(h_tok[:, cc, :], x_all[:, at, :].rearrange("p a d -> p (a d)"),
                                        mv[:, at, 0:1].rearrange("p a d -> p (a d)"), rboth[:, at], ALU.subtract, ALU.mult)
                t.then_inc(h_ready, 1)

            def group(g, last):
                if not last:
                    rows(g + 1)
                for t in range(3):
                    dve.wait_ge(part0, 3 * g + t + 1)
                    if t == 0 and (not isinstance(g, int) or g):
                        dve.wait_ge(part2, 3 * g)
                    v.scalar_tensor_tensor(out=rest[:, t, :], in0=ps[:, SQ + t, :], scalar=float(HD) ** -0.5 if t == 0 else 1.0,
                                           in1=part_of(g, t, 0), op0=ALU.mult, op1=ALU.subtract).then_inc(rest1, 1)
                for t in range(3):
                    dve.wait_ge(part1, 3 * g + t + 1)
                    v.tensor_tensor(part_of(g, t, 2), rest[:, t, :], part_of(g, t, 1), ALU.subtract).then_inc(part2, 1)

            rows(0)
            dve.wait_ge(zeroed, 7)
            group(0, False)
            key_features(0, 0)
            with dve.Fori(1, NG - 1) as g:
                group(g, False)
            group(NG - 1, True)
            dve.wait_ge(c_in, 16 * N_C)

            def post(c, u, p, i):
                static = isinstance(c, int)
                has = [not static or 0 <= c - k < NC for k in range(4)]
                tr = ps[:, TR, :].rearrange("p (h f) -> p h f", f=32)
                z3 = zrec[:].rearrange("p (h a) -> p h a", a=1)
                if u == 0:
                    n = c - 2
                    if has[3]:
                        dve.wait_ge(r_egap, n)
                        v.tensor_scalar(wsum[:], egap[:], 1.0, None, ALU.add).then_inc(r_ws, 1)
                    if has[1]:
                        dve.wait_ge(t_lin, c)
                        v.tensor_scalar(z3, tr[:, :, HD:UD], EPS_LIN, None, ALU.add).then_inc(z1, 1)
                    if has[3]:
                        dve.wait_ge(r_ws, n)
                        v.reciprocal(w01[:, 0:1], wsum[:]).then_inc(r_w, 1)
                    if has[1]:
                        dve.wait_ge(z1, c)
                        v.reciprocal(zrec[:], zrec[:]).then_inc(z2, 1)
                    if has[3]:
                        dve.wait_ge(r_w, n)
                        v.tensor_tensor(w01[:, 1:2], w01[:, 0:1], egap[:], ALU.mult).then_inc(r_w2, 1)
                    if has[1]:
                        dve.wait_ge(z2, c * 2 - 1)
                        if not static or c > 1:
                            dve.wait_ge(t_cat, c - 1)
                        v.tensor_tensor(att[:, 0], tr[:, :, 0:HD], zrec[:].to_broadcast([CH, H, HD]), ALU.mult).then_inc(norm_lin, 1)
                    if has[3]:
                        row = routed_row[:, 1 - p, :]
                        v.tensor_scalar(tmp8[:, 0], onehot[:, 0], w01[:, 0:1], None, ALU.mult).then_inc(r_tmp, 1)
                        v.tensor_scalar(tmp8[:, 1], onehot[:, 1], float(N), None, ALU.mult).then_inc(r_tmp, 1)
                        dve.wait_ge(r_w2, n)
                        dve.wait_ge(r_tmp, 2 * n)
                        if not static or c > 4:
                            dve.wait_ge(scattered[1 - p], 32 * (i - 2 + p))
                        v.scalar_tensor_tensor(out=row[:, D:D + E], in0=onehot[:, 1], scalar=w01[:, 1:2], in1=tmp8[:, 0],
                                               op0=ALU.mult, op1=ALU.add)
                        v.scalar_tensor_tensor(out=row[:, D + E:], in0=member[:], scalar=tokid[:, bass.ds(c - 3, 1)], in1=tmp8[:, 1],
                                               op0=ALU.mult, op1=ALU.add).then_inc(r_row, 1)
                if u == 1 and has[1]:
                    dve.wait_ge(t_win, c)
                    dve.wait_ge(norm_lin, c)
                    v.reciprocal(z3, tr[:, :, HD:UD]).then_inc(z2, 1)
                    dve.wait_ge(z2, c * 2)
                    v.tensor_tensor(att[:, 1], tr[:, :, 0:HD], zrec[:].to_broadcast([CH, H, HD]), ALU.mult).then_inc(norm_win, 1)
                if u == 1 and has[2]:
                    dve.wait_ge(rstd2_ready, c - 1)
                    if not static or c > 3:
                        dve.wait_ge(staged, c - 3)
                    v.tensor_scalar(h2[:, p, :], x_all[:, bass.ds(c - 2, 1), :].rearrange("p a d -> p (a d)"), mv2[:, 0:1], rstd2[:, 0:1],
                                    ALU.subtract, ALU.mult).then_inc(h2_ready, 1)
                if u == 2 and has[3]:
                    n = c - 2
                    dve.wait_ge(pos_ready, n)
                    if has[1] or has[2]:
                        dve.wait_ge(cat_copied, c)
                    v.tensor_tensor(place[:], ps[:, TR, 384:384 + E], count[:], ALU.add).then_inc(r_place, 1)
                    dve.wait_ge(r_place, n)
                    v.tensor_tensor(count[:], ps[:, TR, 392:392 + E], count[:], ALU.add).then_inc(r_count, 1)
                    v.tensor_tensor(placed[:], onehot[:], place[:].rearrange("p (a e) -> p a e", a=1).to_broadcast([CH, 2, E]),
                                    ALU.mult).then_inc(r_placed, 1)
                    dve.wait_ge(r_placed, n)
                    v.tensor_reduce(slotf[:], placed[:], AX.X, ALU.add).then_inc(r_slotf, 1)
                    dve.wait_ge(r_slotf, n)
                    v.tensor_copy(slot[:, 1 - p, :], slotf[:]).then_inc(r_slot, 1)
                if u == 3 and (has[1] or has[2]):
                    n = c - 1
                    xc = x_all[:, bass.ds(c - 1, 1), :].rearrange("p a d -> p (a d)") if has[1] else None
                    dve.wait_ge(wout_ready, c)
                    if has[2]:
                        v.tensor_tensor(logit[:], ps[:, TR, 0:E], bgate[:], ALU.add).then_inc(r_logit, 1)
                    if has[1]:
                        dve.wait_ge(xh_ready, c)
                        v.tensor_tensor(xc, ps[:, TR, 384:384 + D], xh[:], ALU.add).then_inc(x1_ready, 1)
                    if has[2]:
                        dve.wait_ge(r_logit, computed(dve, n))
                        v.max(top[:], logit[:]).then_inc(r_top, 1)
                    if has[1]:
                        dve.wait_ge(x1_ready, computed(dve, c))
                        v.bn_stats(st2[:], xc).then_inc(st2_done, 1)
                    if has[2]:
                        dve.wait_ge(r_top, computed(dve, n))
                        v.max_index(topi[:], top[:], logit[:]).then_inc(r_idx, 1)
                    if has[1]:
                        dve.wait_ge(st2_done, computed(dve, c))
                        if not static or c > 1:
                            dve.wait_ge(h2_ready, computed(dve, c - 1))
                        v.bn_aggr(mv2[:], st2[:]).then_inc(mv2_ready, 1)
                    if has[2]:
                        if not static or c > 2:
                            dve.wait_ge(r_egap, n - 1)
                        v.tensor_tensor(gap[:], top[:, 1:2], top[:, 0:1], ALU.subtract).then_inc(r_gap, 1)
                        dve.wait_ge(r_idx, n)
                        v.tensor_copy(topf[:], topi[:, 0:2]).then_inc(r_idxf, 1)
                    if has[1]:
                        dve.wait_ge(mv2_ready, c)
                        v.tensor_scalar(ve2[:], mv2[:, 1:2], EPS_LN, None, ALU.add).then_inc(ve2_ready, 1)
                    if has[2]:
                        dve.wait_ge(r_idxf, n)
                        if not static or c > 2:
                            dve.wait_ge(r_placed, n - 1)
                            dve.wait_ge(r_row, n - 1)
                        for s in range(2):
                            v.tensor_scalar(onehot[:, s], iota8[:], topf[:, s:s + 1], None, ALU.is_equal).then_inc(r_oh, 1)
                        dve.wait_ge(r_oh, 2 * n)
                        if not static or c > 2:
                            dve.wait_ge(pos_ready, n - 1)
                        v.tensor_tensor(member[:], onehot[:, 0], onehot[:, 1], ALU.add).then_inc(r_member, 1)

            def maxima(n, b, between=None):
                dve.wait_ge(sq_ready, n + 1)
                if not isinstance(n, int) or n:
                    dve.wait_ge(mneg_ready, n)
                v.tensor_reduce(mrow[:], ps[:, SQ, :].rearrange("p (a k) -> p a k", k=CH), AX.X, ALU.max).then_inc(max_done, 1)
                if between:
                    between()
                dve.wait_ge(max_done, n + 1)
                if not isinstance(n, int) or n > 1:
                    dve.wait_ge(st_ready, n - 1)
                v.tensor_scalar(mneg[:, b, 0], mrow[:], -1.0, None, ALU.mult).then_inc(nh_done, 1)
                dve.wait_ge(nh_done, n + 1)
                v.scalar_tensor_tensor(out=mneg[:, b, 1], in0=mrow[:], scalar=-1.0, in1=mneg[:, b, 0],
                                       op0=ALU.mult, op1=ALU.subtract).then_inc(mneg_ready, 1)

            def chunk(c, p, i):
                first = isinstance(c, int) and c == 0
                for u in range(UNITS):
                    n = c * UNITS + u
                    last = isinstance(c, int) and c == NC - 1 and u == 3
                    if not first or u:
                        cu, cc = (u - 1) % 4, c if u else c - 1
                        dve.wait_ge(sadd_done, n)
                        dve.wait_ge(inter_done, n)
                        s = state[:, 4 * cu:4 * cu + 4, 0:UD]
                        v.scalar_tensor_tensor(out=s, in0=s, scalar=keep[0:PR, bass.ds(cc + 1, 1)], in1=sadd[:],
                                               op0=ALU.mult, op1=ALU.add).then_inc(state_done, 1)
                    def addition():
                        if not first or u:
                            dve.wait_ge(state_done, n)
                        dve.wait_ge(kv_ready, n + 1)
                        v.scalar_tensor_tensor(out=sadd[:], in0=ps[0:PR, KV, 0:4 * UD].rearrange("p (h f) -> p h f", f=UD),
                                               scalar=keep[0:PR, bass.ds(c + 1, 1)], in1=statemask[:].rearrange("p (h f) -> p h f", f=UD),
                                               op0=ALU.mult, op1=ALU.mult).then_inc(sadd_done, 1)

                    if not last:
                        maxima(n + 1, (u + 1) % 2, addition)
                    else:
                        addition()
                    if not first:
                        post(c, u, p, i)
                    if u == 1 and not (isinstance(c, int) and c == NC - 1):
                        key_features(c + 1, 1 - p)

            maxima(0, 0)
            for c in range(4):
                chunk(c, c % 2, c // 2)
            with dve.Fori(2, NC // 2 - 1) as i:
                for p in range(2):
                    chunk(i * 2 + p, p, i)
            for c in range(NC - 2, NC):
                chunk(c, c % 2, c // 2)
            for c in range(NC, NC + 3):
                for u in range(UNITS):
                    post(c, u, c % 2, c // 2)

            links = [0]

            def link(t):
                links[0] += 1
                t.then_inc(tab, 1)
                dve.wait_ge(tab, links[0])

            dve.wait_ge(r_count, NC)
            v.tensor_copy(tail_i[:], count[0:1, :]).then_inc(tail_ready, 1)
            link(v.tensor_tensor(ntile[:], count[0:1, :], region0[0:1, :], ALU.subtract))
            link(v.tensor_scalar(ntile[:], ntile[:], float(CH - 1), None, ALU.add))
            link(v.tensor_copy(counts_i[:], ntile[:]))
            link(v.tensor_scalar(ntile_i[:], counts_i[:], 7, None, ALU.arith_shift_right))
            link(v.tensor_copy(ntile[:], ntile_i[:]))
            link(v.tensor_tensor_scan(ends[:], ntile[:], ntile[:], 0.0, ALU.add, ALU.bypass))
            link(v.tensor_tensor(tmpt[:, 0], ends[:, E - 1:E].to_broadcast([1, NT]), tiles[:], ALU.min))
            t3 = lambda k: tmpt[:, k].rearrange("p (t a) -> p t a", a=1)
            e3 = lambda x: x.rearrange("p (a e) -> p a e", a=1).to_broadcast([1, NT, E])
            link(v.tensor_tensor(cmp8[:, 0], t3(0).to_broadcast([1, NT, E]), e3(ends[:]), ALU.is_ge))
            link(v.tensor_reduce(tmpt[:, 1], cmp8[:, 0], AX.X, ALU.add))
            link(v.tensor_tensor(cmp8[:, 1], cmp8[:, 0], e3(ntile[:]), ALU.mult))
            link(v.tensor_reduce(tmpt[:, 2], cmp8[:, 1], AX.X, ALU.add))
            link(v.tensor_tensor(tmpt[:, 0], tmpt[:, 0], tmpt[:, 2], ALU.subtract))
            link(v.tensor_scalar(tmpt[:, 0], tmpt[:, 0], float(CH), None, ALU.mult))
            link(v.scalar_tensor_tensor(out=tmpt[:, 3], in0=tmpt[:, 1], scalar=float(REGION), in1=tmpt[:, 0], op0=ALU.mult, op1=ALU.add))
            link(v.tensor_scalar(table[:, 0, :], tmpt[:, 1], float(E - 1), None, ALU.min))
            v.tensor_copy(table[:, 1, :], tmpt[:, 3]).then_inc(table_ready, 1)
            dve.wait_ge(table_ready, 1)
            dve.wait_ge(b_in, 16 * 7)

            def flat(ap):
                return ap.rearrange("p a f -> p (a f)")

            def step(j, k, turn, expert):
                static = isinstance(j, int)
                on = lambda d: not static or 0 <= j + d < NT
                if on(-1):
                    dve.wait_ge(gl_ready, computed(dve, j))
                    e = expert(-1)
                    q = (k + 1) % 2
                    if not static or j > 2:
                        dve.wait_ge(silu_done, j - 2)
                        dve.wait_ge(o_ready, j - 2)
                    v.tensor_tensor(glb[:, q, :], ps[:, GL, :], flat(bgl[:, bass.ds(e, 1), :]), ALU.add).then_inc(gl_added, 1)
                    dve.wait_ge(silu_done, j)
                    dve.wait_ge(gl_added, j)
                    if not static or j > 2:
                        dve.wait_ge(to_ready, j - 2)
                    v.tensor_tensor(og[:, q, :], sg[:, q, :], glb[:, q, F:], ALU.mult).then_inc(o_ready, 1)
                if on(1):
                    dve.wait_ge(x12_ready, computed(dve, j + 2))
                    q = (k + 1) % 2
                    e = expert(1)
                    if not static or j > 0:
                        dve.wait_ge(z_ready, j)
                    v.tensor_tensor(x12[:, q, :], ps[:, X12, :], flat(b12[:, bass.ds(e, 1), :]), ALU.add).then_inc(x12_added, 1)
                if on(-2):
                    dve.wait_ge(y_ready, computed(dve, j - 1))
                    if not static or j > 3:
                        dve.wait_ge(y_weighted, computed(dve, j - 3))
                    v.tensor_tensor(yb[:, k % 2, :], ps[:, Y, 0:D], flat(b3[:, bass.ds(expert(-2), 1), :]), ALU.add).then_inc(y_added, 1)
                if on(1):
                    dve.wait_ge(x12_added, j + 2)
                    if not static or j > 0:
                        dve.wait_ge(tzx_ready, j + 2)
                    v.tensor_tensor(z[:, q, :], x12[:, q, 0:F], x12[:, q, F:], ALU.mult).then_inc(z_ready, 1)
                    m = (k + 1) % 4
                    if not static or j >= 3:
                        dve.wait_ge(y_weighted, j - 2)
                        dve.wait_ge(y_out[m], 16 * turn(1))
                    v.tensor_copy(mweight[:, m:m + 1], xin[:, m, bass.ds(e + D, 1)])
                    v.tensor_copy(mrowid[:, m:m + 1], xin[:, m, bass.ds(e + (D + E), 1)]).then_inc(meta_copied, 1)

            run_steps(dve, step, (-2, -1, 1))
            for g in range(NG):
                at = slice(g * GC, (g + 1) * GC)
                dve.wait_ge(res_in[g], 32)
                v.tensor_tensor(res[0][:, at], res[0][:, at], res[1][:, at], ALU.add).then_inc(res_sum, 1)
                dve.wait_ge(res_sum, g + 1)
                v.tensor_tensor(x_all[:, at], x_all[:, at], res[0][:, at], ALU.add).then_inc(out_sum, 1)

        @block.gpsimd
        def _(pool):
            q = nc.gpsimd
            q.memset(minus_half[:], -0.5).then_inc(zeroed, 1)
            q.memset(v1[:], 0.0).then_inc(zeroed, 1)
            q.memset(kp[:, :, 0:WINDOW], 0.0).then_inc(zeroed, 1)
            q.memset(state[:], 0.0).then_inc(zeroed, 1)
            q.memset(phik[:], 0.0).then_inc(zeroed, 1)
            q.memset(u_tok[:, :, 0:1], 1.0).then_inc(zeroed, 1)
            pool.wait_ge(zeroed, 6)
            q.memset(v1[:, :, :, :, HD:HD + 1], 1.0).then_inc(zeroed, 1)
            for k in range(2):
                pool.wait_ge(ve_ready, k + 1)
                q.tensor_tensor(rstd[:] if k == 0 else vareps[:, 1, :], vareps[:, k, :], minus_half[:], ALU.pow).then_inc(pow_ready, 1)

            def cross_products(c, p, part):
                if part == 0:
                    pool.wait_ge(us, computed(pool, c * 2 + 1))
                at = UD
                for dl in range(1, UD):
                    w = UD - dl
                    if (dl > 3) == part:
                        t = q.tensor_tensor(phik[:, p, :, at:at + w], u_tok[:, :, 0:w], u_tok[:, :, dl:UD], ALU.mult)
                    at += w
                if part:
                    t.then_inc(cross_ready, 1)

            def scatter(b, k):
                q.indirect_dma_start(routed, bass.IndirectOffsetOnAxis(slot[:, b, k:k + 1], 0), routed_row[:, b, :], None).then_inc(scattered[b], 16)

            def post(c, u, p, i):
                static = isinstance(c, int)
                has = [not static or 0 <= c - k < NC for k in range(4)]
                if u == 1 and has[3]:
                    if not static or c > 4:
                        pool.wait_ge(scattered[1 - p], computed(pool, 32 * (i - 2 + p)))
                    pool.wait_ge(h2_ready, computed(pool, c - 2))
                    q.tensor_copy(routed_row[:, 1 - p, 0:D], h2[:, 1 - p, :]).then_inc(staged, 1)
                if u == 3 and has[1]:
                    pool.wait_ge(ve2_ready, computed(pool, c))
                    q.tensor_tensor(rstd2[:], ve2[:], minus_half[:, 0:1], ALU.pow).then_inc(rstd2_ready, 1)
                if u == 3 and has[3]:
                    pool.wait_ge(r_slot, computed(pool, c - 2))
                    pool.wait_ge(r_row, computed(pool, c - 2))
                    pool.wait_ge(staged, computed(pool, c - 2))
                    scatter(1 - p, 0)
                    if static and c == NC + 2:
                        scatter(1 - p, 1)
                if u == 0 and (not static or 0 <= c - 4 < NC - 1):
                    scatter(p, 1)

            def chunk(c, p, i):
                first = isinstance(c, int) and c == 0
                for u in range(UNITS):
                    n = c * UNITS + u
                    pool.wait_ge(square_done, computed(pool, n + 1))
                    q.affine_select(out=amat[:, u % 2], in_=amat[:, u % 2], compare_op=ALU.is_ge, fill=0.0, base=0,
                                    pattern=[[0, 4], [1, CH]], channel_multiplier=-1).then_inc(amask_ready, 1)
                    if u >= 2 and not (isinstance(c, int) and c == NC - 1):
                        cross_products(c + 1, 1 - p, u - 2)
                    if not first:
                        post(c, u, p, i)

            cross_products(0, 0, 0)
            cross_products(0, 0, 1)
            for c in range(4):
                chunk(c, c % 2, c // 2)
            with pool.Fori(2, NC // 2 - 1) as i:
                for p in range(2):
                    chunk(i * 2 + p, p, i)
            for c in range(NC - 2, NC):
                chunk(c, c % 2, c // 2)
            for c in range(NC, NC + 3):
                for u in range(UNITS):
                    post(c, u, c % 2, c // 2)

            def step(j, k, turn, expert):
                if not isinstance(j, int) or 0 <= j - 2 < NT:
                    m = (k + 2) % 4
                    pool.wait_ge(y_weighted, computed(pool, j - 1))
                    q.indirect_dma_start(results, bass.IndirectOffsetOnAxis(mrowid[:, m:m + 1], 0), yw[:, m, :], None,
                                         bounds_check=RESULTS - 1, oob_is_err=False).then_inc(y_out[m], 16)

            run_steps(pool, step)


_NAMES = {"x": "L0_attn_x", "norm_w": "L0_attn_norm_w", "Wq": "L0_attn_Wq", "Wk": "L0_attn_Wk", "Wv": "L0_attn_Wv", "Wout": "L0_attn_Wout",
          **{n: "L0_ffn_" + n for n in ("Wgate", "bgate", "W1", "b1", "W2", "b2", "Wg", "bg", "Wl", "bl", "W3", "b3")}}


def kernel(**inputs):
    import concourse.bacc as _bacc
    from concourse.bass_utils import run_bass_kernel_spmd as _run

    arrays = {k: np.ascontiguousarray(inputs[v]) for k, v in _NAMES.items()}
    arrays["WqT"] = np.ascontiguousarray(np.transpose(inputs["L0_attn_Wq"]))
    arrays["WqfT"] = np.ascontiguousarray(np.tile(np.transpose(inputs["L0_attn_Wqf"]), (1, H)))
    arrays["WkfT"] = np.ascontiguousarray(np.tile(np.transpose(inputs["L0_attn_Wkf"]), (1, H)))
    con = constants()
    nc = _bacc.Bacc("TRN2", target_bir_lowering=False, num_devices=1)
    feed, ins, cin = {}, {}, {}
    for group, aps, pre in ((arrays, ins, "in_"), (con, cin, "const_")):
        for k, a in group.items():
            feed[pre + k] = a
            aps[k] = nc.dram_tensor(pre + k, a.shape, mybir.dt.from_np(a.dtype), kind="ExternalInput").ap()
    out = nc.dram_tensor("out", (B, T, D), F32, kind="ExternalOutput").ap()
    build(nc, ins, cin, out)
    r = _run(nc, [feed], core_ids=[0])
    return r.results[0]["out"]
```
